# Optimizing a Trainium2 kernel written in Bass

```python
import numpy as np
import jax
import jax.numpy as jnp

def _softmax(x, axis=-1):
    return jax.nn.softmax(x, axis=axis)

def _gelu(x):
    return jax.nn.gelu(x, approximate=True)

def _silu(x):
    return jax.nn.silu(x)

def _sigmoid(x):
    return jax.nn.sigmoid(x)

def _layernorm(x, axis=-1, eps=1e-05):
    m = jnp.mean(x, axis=axis, keepdims=True)
    v = jnp.var(x, axis=axis, keepdims=True)
    return (x - m) / jnp.sqrt(v + eps)

def _scatter_add(tgt, idx, src, axis=0):
    return tgt.at[idx].add(src)

def _segment_sum(src, seg, n):
    return jax.ops.segment_sum(src, seg, n)
kernel_name = 'mk_xattn_ffn_d2_seqx_r4_0e161b'

def setup_inputs(seed: int=0):
    np.random.seed(seed)
    _w = jnp.asarray

    def _rec_inputs():
        import jax
        import jax.numpy as jnp
        _rk = jax.random.key(seed)
        x = 7.22e-05 + 1 * jax.random.normal(jax.random.fold_in(_rk, 1), (16, 128, 256), jnp.float32)
        _lenS = 128 - jax.random.randint(jax.random.fold_in(_rk, 7), (16,), 0, max(1, 128 // 4) + 1, jnp.int32)
        _lenS2 = 128 - jax.random.randint(jax.random.fold_in(_rk, 8), (16,), 0, max(1, 128 // 4) + 1, jnp.int32)
        _ctx_1024P = jax.random.normal(jax.random.fold_in(_rk, 11), (16, 16, 256), jnp.float32)
        _ctx_1024c = jax.random.dirichlet(jax.random.fold_in(_rk, 511), 0.3 * jnp.ones((16,), jnp.float32), (16, 128))
        _ctx_1024t = jnp.einsum('bsk,bkd->bsd', _ctx_1024c, _ctx_1024P)
        _ctx_1024t = _ctx_1024t * jax.lax.rsqrt(jnp.mean(jnp.square(_ctx_1024t)) + 1e-12) * 0.953939
        ctx_1024 = 4.13588e-05 + 0.999923 * (_ctx_1024t + 0.3 * jax.random.normal(jax.random.fold_in(_rk, 611), (16, 128, 256), jnp.float32))
        _validS = jnp.arange(128)[None, :] < _lenS[:, None]
        _validS2 = jnp.arange(128)[None, :] < _lenS2[:, None]
        _causal = jnp.tril(jnp.ones((128, 128), dtype=bool))
        mask_Bx1x1xS2_ik0 = jnp.where(jnp.broadcast_to(_validS2[:, None, None, :], (16, 1, 1, 128)), 0, 1).astype(jnp.int32)
        return (x, ctx_1024, mask_Bx1x1xS2_ik0)
    x, ctx_1024, mask_Bx1x1xS2_ik0 = _rec_inputs()

    def _L0_xattn_setup():
        import jax, jax.numpy as jnp
        import numpy as np
        D_MODEL = 256
        N_HEAD = 16
        D_HEAD = D_MODEL // N_HEAD
        SCALE = D_HEAD ** 0.5
        LN_EPS = 1e-06

        def _split_heads(x):
            b, s, _ = x.shape
            return x.reshape(b, s, N_HEAD, D_HEAD).transpose(0, 2, 1, 3)
        key = jax.random.key(seed)
        ks = jax.random.split(key, 8)
        B, S = (4, 512)
        w_std = (2.0 / (D_MODEL + D_MODEL)) ** 0.5 / 2 ** 0.5
        return {'query': jax.random.normal(ks[0], (B, S, D_MODEL), jnp.float32), 'key': jax.random.normal(ks[1], (B, S, D_MODEL), jnp.float32), 'value': jax.random.normal(ks[2], (B, S, D_MODEL), jnp.float32), 'attn_mask': jax.random.randint(ks[3], (B, 1, 1, S), 0, 2, jnp.int32), 'Wq': jax.random.normal(ks[4], (D_MODEL, D_MODEL), jnp.float32) * w_std, 'bq': jnp.zeros((D_MODEL,), jnp.float32), 'Wk': jax.random.normal(ks[5], (D_MODEL, D_MODEL), jnp.float32) * w_std, 'bk': jnp.zeros((D_MODEL,), jnp.float32), 'Wv': jax.random.normal(ks[6], (D_MODEL, D_MODEL), jnp.float32) * w_std, 'bv': jnp.zeros((D_MODEL,), jnp.float32), 'gamma': jnp.ones((D_MODEL,), jnp.float32), 'beta': jnp.zeros((D_MODEL,), jnp.float32)}
    _L0_xattn_all = _L0_xattn_setup()
    _L0_xattn_in = {k: v for k, v in _L0_xattn_all.items() if k in ('Wq', 'bq', 'Wk', 'bk', 'Wv', 'bv', 'gamma', 'beta')}
    del _L0_xattn_all

    def _L0_ffn_setup():
        import jax, jax.numpy as jnp
        import numpy as np
        D, H, N, K = (256, 512, 8, 2)
        B, S = (4, 512)
        key = jax.random.key(seed)
        ks = jax.random.split(key, 4)
        x = jax.random.normal(ks[0], (B, S, D), dtype=jnp.float32)
        Wr = jax.random.normal(ks[1], (N, D), dtype=jnp.float32) / np.sqrt(D)
        br = jnp.zeros((N,), jnp.float32)
        Wl1 = jax.random.normal(ks[2], (N, D, 2 * H), dtype=jnp.float32) / np.sqrt(D)
        bl1 = jnp.zeros((N, 2 * H), jnp.float32)
        Wl2 = jax.random.normal(ks[3], (N, H, D), dtype=jnp.float32) / np.sqrt(H)
        bl2 = jnp.zeros((N, D), jnp.float32)
        biases_N = jnp.zeros((N,), jnp.float32)
        return {'x': x, 'Wr': Wr, 'br': br, 'Wl1': Wl1, 'bl1': bl1, 'Wl2': Wl2, 'bl2': bl2, 'biases_N': biases_N}
    _L0_ffn_all = _L0_ffn_setup()
    _L0_ffn_in = {k: v for k, v in _L0_ffn_all.items() if k in ('Wr', 'br', 'Wl1', 'bl1', 'Wl2', 'bl2', 'biases_N')}
    del _L0_ffn_all

    def _L1_xattn_setup():
        import jax, jax.numpy as jnp
        import numpy as np
        H = 16
        D = 64
        SCALE = D ** (-0.5)
        TEXT = 77
        IMG = 16
        AUD = 32
        MAXREL = 16
        B, NQ, QD = (32, 256, 256)
        INNER = H * D

        def _heads(t):
            return t.reshape(t.shape[0], t.shape[1], H, D)
        key = jax.random.key(seed)
        ks = jax.random.split(key, 14)
        w = lambda k, s: jax.random.normal(k, s, jnp.float32) * 0.02
        return {'x': jax.random.normal(ks[0], (B, NQ, QD), jnp.float32), 'context': jax.random.normal(ks[1], (B, TEXT + IMG + AUD, QD), jnp.float32), 'Wq': w(ks[2], (QD, INNER)), 'Wk': w(ks[3], (QD, INNER)), 'Wv': w(ks[4], (QD, INNER)), 'Wk_ip': w(ks[5], (QD, INNER)), 'Wv_ip': w(ks[6], (QD, INNER)), 'Wk_ap': w(ks[7], (QD, INNER)), 'Wv_ap': w(ks[8], (QD, INNER)), 'Wo': w(ks[9], (INNER, QD)), 'bo': jnp.zeros((QD,), jnp.float32), 'rel_k': w(ks[10], (2 * MAXREL + 1, D)), 'rel_v': w(ks[11], (2 * MAXREL + 1, D)), 'alpha': jnp.zeros((), jnp.float32), 'beta': jnp.zeros((), jnp.float32)}
    _L1_xattn_all = _L1_xattn_setup()
    _L1_xattn_in = {k: v for k, v in _L1_xattn_all.items() if k in ('Wq', 'Wk', 'Wv', 'Wk_ip', 'Wv_ip', 'Wk_ap', 'Wv_ap', 'Wo', 'bo', 'rel_k', 'rel_v', 'alpha', 'beta')}
    del _L1_xattn_all

    def _L1_ffn_setup():
        import jax, jax.numpy as jnp
        import numpy as np
        B, S, D_MODEL, D_HIDDEN = (4, 512, 256, 1024)

        def act_quant(x):
            scale = 127.0 / jnp.clip(jnp.max(jnp.abs(x), axis=-1, keepdims=True), 1e-05)
            return jnp.clip(jnp.round(x * scale), -128, 127) / scale

        def weight_quant(w):
            scale = 1.0 / jnp.clip(jnp.mean(jnp.abs(w)), 1e-05)
            return jnp.clip(jnp.round(w * scale), -1, 1) / scale

        def bit_linear(x, w):
            xq = x + jax.lax.stop_gradient(act_quant(x) - x)
            wq = w + jax.lax.stop_gradient(weight_quant(w) - w)
            return jnp.einsum('bsd,hd->bsh', xq, wq)

        def depthwise_conv1d(x_bcl, w, b):
            y = jax.lax.conv_general_dilated(x_bcl, w, window_strides=(1,), padding=[(1, 1)], dimension_numbers=('NCH', 'OIH', 'NCH'), feature_group_count=x_bcl.shape[1])
            return y + b[None, :, None]
        key = jax.random.key(seed)
        ks = jax.random.split(key, 5)
        lim1 = 1.0 / np.sqrt(D_MODEL)
        lim2 = 1.0 / np.sqrt(D_HIDDEN)
        limc = 1.0 / np.sqrt(3.0)
        return {'x': jax.random.normal(ks[0], (B, S, D_MODEL), dtype=jnp.float32), 'w1': jax.random.uniform(ks[1], (D_HIDDEN, D_MODEL), jnp.float32, -lim1, lim1), 'conv_w': jax.random.uniform(ks[2], (D_HIDDEN, 1, 3), jnp.float32, -limc, limc), 'conv_b': jax.random.uniform(ks[3], (D_HIDDEN,), jnp.float32, -limc, limc), 'w2': jax.random.uniform(ks[4], (D_MODEL, D_HIDDEN), jnp.float32, -lim2, lim2)}
    _L1_ffn_all = _L1_ffn_setup()
    _L1_ffn_in = {k: v for k, v in _L1_ffn_all.items() if k in ('w1', 'conv_w', 'conv_b', 'w2')}
    del _L1_ffn_all
    return {'x': x, 'ctx_1024': ctx_1024, 'mask_Bx1x1xS2_ik0': mask_Bx1x1xS2_ik0, 'L0_xattn_Wq': _L0_xattn_in['Wq'], 'L0_xattn_bq': _L0_xattn_in['bq'], 'L0_xattn_Wk': _L0_xattn_in['Wk'], 'L0_xattn_bk': _L0_xattn_in['bk'], 'L0_xattn_Wv': _L0_xattn_in['Wv'], 'L0_xattn_bv': _L0_xattn_in['bv'], 'L0_xattn_gamma': _L0_xattn_in['gamma'], 'L0_xattn_beta': _L0_xattn_in['beta'], 'L0_ffn_Wr': _L0_ffn_in['Wr'], 'L0_ffn_br': _L0_ffn_in['br'], 'L0_ffn_Wl1': _L0_ffn_in['Wl1'], 'L0_ffn_bl1': _L0_ffn_in['bl1'], 'L0_ffn_Wl2': _L0_ffn_in['Wl2'], 'L0_ffn_bl2': _L0_ffn_in['bl2'], 'L0_ffn_biases_N': _L0_ffn_in['biases_N'], 'L1_xattn_Wq': _L1_xattn_in['Wq'], 'L1_xattn_Wk': _L1_xattn_in['Wk'], 'L1_xattn_Wv': _L1_xattn_in['Wv'], 'L1_xattn_Wk_ip': _L1_xattn_in['Wk_ip'], 'L1_xattn_Wv_ip': _L1_xattn_in['Wv_ip'], 'L1_xattn_Wk_ap': _L1_xattn_in['Wk_ap'], 'L1_xattn_Wv_ap': _L1_xattn_in['Wv_ap'], 'L1_xattn_Wo': _L1_xattn_in['Wo'], 'L1_xattn_bo': _L1_xattn_in['bo'], 'L1_xattn_rel_k': _L1_xattn_in['rel_k'], 'L1_xattn_rel_v': _L1_xattn_in['rel_v'], 'L1_xattn_alpha': _L1_xattn_in['alpha'], 'L1_xattn_beta': _L1_xattn_in['beta'], 'L1_ffn_w1': _L1_ffn_in['w1'], 'L1_ffn_conv_w': _L1_ffn_in['conv_w'], 'L1_ffn_conv_b': _L1_ffn_in['conv_b'], 'L1_ffn_w2': _L1_ffn_in['w2']}

def reference(x, ctx_1024, mask_Bx1x1xS2_ik0, L0_xattn_Wq, L0_xattn_bq, L0_xattn_Wk, L0_xattn_bk, L0_xattn_Wv, L0_xattn_bv, L0_xattn_gamma, L0_xattn_beta, L0_ffn_Wr, L0_ffn_br, L0_ffn_Wl1, L0_ffn_bl1, L0_ffn_Wl2, L0_ffn_bl2, L0_ffn_biases_N, L1_xattn_Wq, L1_xattn_Wk, L1_xattn_Wv, L1_xattn_Wk_ip, L1_xattn_Wv_ip, L1_xattn_Wk_ap, L1_xattn_Wv_ap, L1_xattn_Wo, L1_xattn_bo, L1_xattn_rel_k, L1_xattn_rel_v, L1_xattn_alpha, L1_xattn_beta, L1_ffn_w1, L1_ffn_conv_w, L1_ffn_conv_b, L1_ffn_w2):
    import jax
    import jax.numpy as jnp

    def _L0_xattn_ref(query, key, value, attn_mask, Wq, bq, Wk, bk, Wv, bv, gamma, beta):
        import jax, jax.numpy as jnp
        import numpy as np
        D_MODEL = 256
        N_HEAD = 16
        D_HEAD = D_MODEL // N_HEAD
        SCALE = D_HEAD ** 0.5
        LN_EPS = 1e-06

        def _split_heads(x):
            b, s, _ = x.shape
            return x.reshape(b, s, N_HEAD, D_HEAD).transpose(0, 2, 1, 3)
        q = _split_heads(query @ Wq.T + bq)
        k = _split_heads(key @ Wk.T + bk)
        v = _split_heads(value @ Wv.T + bv)
        scores = jnp.einsum('bhqd,bhkd->bhqk', q, k) / SCALE
        scores = jnp.where(attn_mask == 0, jnp.float32(-1000000000.0), scores)
        w = jax.nn.softmax(scores, axis=-1)
        att = jnp.einsum('bhqk,bhkd->bhqd', w, v)
        b, h, s, d = att.shape
        att = att.transpose(0, 2, 1, 3).reshape(b, s, D_MODEL)
        x = att + key
        mu = jnp.mean(x, axis=-1, keepdims=True)
        var = jnp.mean(jnp.square(x - mu), axis=-1, keepdims=True)
        return (x - mu) / jnp.sqrt(var + LN_EPS) * gamma + beta

    def _L0_ffn_ref(x, Wr, br, Wl1, bl1, Wl2, bl2, biases_N):
        import jax, jax.numpy as jnp
        import numpy as np
        D, H, N, K = (256, 512, 8, 2)
        B, S = (4, 512)
        Bb, Ss, Dd = x.shape
        scores_BSN = jnp.einsum('bsd,nd->bsn', x, Wr) + br
        w_BSN = jax.nn.softmax(scores_BSN, axis=-1)
        _, idx_BSK = jax.lax.top_k(scores_BSN + biases_N[None, None, :], K)
        val_BSK = jnp.take_along_axis(w_BSN, idx_BSK, axis=-1)
        val_BSK = val_BSK / jnp.sum(val_BSK, axis=-1, keepdims=True)
        M = Bb * Ss
        x_MD = x.reshape(M, Dd)
        idx_MK = idx_BSK.reshape(M, K)
        val_MK = val_BSK.reshape(M, K)
        h_NM2H = jnp.einsum('md,ndh->nmh', x_MD, Wl1) + bl1[:, None, :]
        a_NMH, b_NMH = (h_NM2H[..., :H], h_NM2H[..., H:])
        y_NMD = jnp.einsum('nmh,nhd->nmd', jax.nn.silu(a_NMH) * b_NMH, Wl2) + bl2[:, None, :]
        ew_MN = jnp.zeros((M, N), x.dtype)
        ew_MN = ew_MN.at[jnp.arange(M)[:, None], idx_MK].set(val_MK)
        y_MD = jnp.einsum('mn,nmd->md', ew_MN, y_NMD)
        return y_MD.reshape(Bb, Ss, Dd)

    def _L1_xattn_ref(x, context, Wq, Wk, Wv, Wk_ip, Wv_ip, Wk_ap, Wv_ap, Wo, bo, rel_k, rel_v, alpha, beta):
        import jax, jax.numpy as jnp
        import numpy as np
        H = 16
        D = 64
        SCALE = D ** (-0.5)
        TEXT = 77
        IMG = 16
        AUD = 32
        MAXREL = 16
        B, NQ, QD = (32, 256, 256)
        INNER = H * D

        def _heads(t):
            return t.reshape(t.shape[0], t.shape[1], H, D)
        b, nq, _ = x.shape
        q = _heads(x @ Wq)
        ctx_t = context[:, :TEXT]
        ctx_i = context[:, TEXT:TEXT + IMG]
        ctx_a = context[:, TEXT + IMG:]
        k = _heads(ctx_t @ Wk)
        v = _heads(ctx_t @ Wv)
        sim = jnp.einsum('bihd,bjhd->bhij', q, k) * SCALE
        dist = jnp.clip(jnp.arange(TEXT)[None, :] - jnp.arange(nq)[:, None], -MAXREL, MAXREL) + MAXREL
        k2 = rel_k[dist]
        sim = sim + jnp.einsum('bihd,ijd->bhij', q, k2) * SCALE
        attn = jax.nn.softmax(sim, axis=-1)
        out = jnp.einsum('bhij,bjhd->bihd', attn, v)
        out = out + jnp.einsum('bhij,ijd->bihd', attn, rel_v[dist])

        def stream(W_k, W_v, ctx):
            kh = _heads(ctx @ W_k)
            vh = _heads(ctx @ W_v)
            a = jax.nn.softmax(jnp.einsum('bihd,bjhd->bhij', q, kh) * SCALE, axis=-1)
            return jnp.einsum('bhij,bjhd->bihd', a, vh)
        out = out + stream(Wk_ip, Wv_ip, ctx_i) * (jnp.tanh(alpha) + 1.0)
        out = out + stream(Wk_ap, Wv_ap, ctx_a) * (jnp.tanh(beta) + 1.0)
        out = out.reshape(b, nq, INNER)
        return out @ Wo + bo

    def _L1_ffn_ref(x, w1, conv_w, conv_b, w2):
        import jax, jax.numpy as jnp
        import numpy as np
        B, S, D_MODEL, D_HIDDEN = (4, 512, 256, 1024)

        def act_quant(x):
            scale = 127.0 / jnp.clip(jnp.max(jnp.abs(x), axis=-1, keepdims=True), 1e-05)
            return jnp.clip(jnp.round(x * scale), -128, 127) / scale

        def weight_quant(w):
            scale = 1.0 / jnp.clip(jnp.mean(jnp.abs(w)), 1e-05)
            return jnp.clip(jnp.round(w * scale), -1, 1) / scale

        def bit_linear(x, w):
            xq = x + jax.lax.stop_gradient(act_quant(x) - x)
            wq = w + jax.lax.stop_gradient(weight_quant(w) - w)
            return jnp.einsum('bsd,hd->bsh', xq, wq)

        def depthwise_conv1d(x_bcl, w, b):
            y = jax.lax.conv_general_dilated(x_bcl, w, window_strides=(1,), padding=[(1, 1)], dimension_numbers=('NCH', 'OIH', 'NCH'), feature_group_count=x_bcl.shape[1])
            return y + b[None, :, None]
        h = bit_linear(x, w1)
        h = depthwise_conv1d(h.transpose(0, 2, 1), conv_w, conv_b)
        h = h.transpose(0, 2, 1)
        h = jax.nn.silu(h)
        return bit_linear(h, w2)
    x = x + _L0_xattn_ref(_layernorm(x, axis=-1), ctx_1024, ctx_1024, mask_Bx1x1xS2_ik0, L0_xattn_Wq, L0_xattn_bq, L0_xattn_Wk, L0_xattn_bk, L0_xattn_Wv, L0_xattn_bv, L0_xattn_gamma, L0_xattn_beta)
    x = x + _L0_ffn_ref(_layernorm(x, axis=-1), L0_ffn_Wr, L0_ffn_br, L0_ffn_Wl1, L0_ffn_bl1, L0_ffn_Wl2, L0_ffn_bl2, L0_ffn_biases_N)
    x = x + _L1_xattn_ref(_layernorm(x, axis=-1), ctx_1024, L1_xattn_Wq, L1_xattn_Wk, L1_xattn_Wv, L1_xattn_Wk_ip, L1_xattn_Wv_ip, L1_xattn_Wk_ap, L1_xattn_Wv_ap, L1_xattn_Wo, L1_xattn_bo, L1_xattn_rel_k, L1_xattn_rel_v, L1_xattn_alpha, L1_xattn_beta)
    x = x + _L1_ffn_ref(_layernorm(x, axis=-1), L1_ffn_w1, L1_ffn_conv_w, L1_ffn_conv_b, L1_ffn_w2)
    return x

_drawn_inputs = setup_inputs


def setup_inputs(seed=0):
    import zlib

    import numpy as np

    out = dict(_drawn_inputs(seed))
    spreads = {'L0_xattn_bq': (0.0, 0.33),
     'L0_xattn_bk': (0.0, 2.0),
     'L0_xattn_bv': (0.0, 0.1),
     'L0_xattn_gamma': (1.0, 0.2),
     'L0_xattn_beta': (0.0, 0.1),
     'L0_ffn_br': (0.0, 0.1),
     'L0_ffn_bl1': (0.0, 0.1),
     'L0_ffn_bl2': (0.0, 0.1),
     'L0_ffn_biases_N': (0.0, 0.1),
     'L1_xattn_bo': (0.0, 0.1)}
    factors = {'L1_xattn_Wq': 8.0,
     'L1_xattn_Wk': 8.0,
     'L1_xattn_Wk_ip': 8.0,
     'L1_xattn_Wk_ap': 8.0,
     'L1_xattn_rel_k': 44.678,
     'L1_xattn_rel_v': 7.962}
    for name, (base, spread) in spreads.items():
        noise = np.random.default_rng([zlib.crc32(name.encode()), seed]).standard_normal(out[name].shape)
        drawn = base * np.exp(spread * noise) if base else spread * noise
        out[name] = jnp.asarray(drawn.astype(out[name].dtype))
    for name, factor in factors.items():
        out[name] = (out[name] * factor).astype(out[name].dtype)
    return out
```

```python
from contextlib import ExitStack

import numpy as np

import concourse.bass as bass
from concourse import mybir

F32 = mybir.dt.float32
BF16 = mybir.dt.bfloat16
I32 = mybir.dt.int32
U32 = mybir.dt.uint32
ALU = mybir.AluOpType
ACT = mybir.ActivationFunctionType
X = mybir.AxisListType.X

P = 128
NB = 16
D = 256
KD = D // P
NH = 16

DH0 = D // NH
STRIP = 32
HPT = P // STRIP
MT0 = NH // HPT
SCALE0 = 1.0 / DH0 ** 0.5
MASKED = -1.0e9
EPS0 = 1e-6
EPS = 1e-5

TEXT, IMG = 77, 16
MAXREL = 16

NE = 8
TOPK = 2
HE = 512
KH = HE // P
ROWS_E = NB * P + P
N_TILES = (NB * P * TOPK + NE * (P - 1)) // P


class Link:

    def __init__(self, eng, sem, per):
        self.eng, self.sem, self.per, self.n, self.base = eng, sem, per, 0, 0

    def begin(self, b):
        self.base, self.n = b * self.per, 0

    def __call__(self, ins):
        ins.then_inc(self.sem, 1)
        self.n += 1
        assert self.n <= self.per, self.n
        apart(self.eng, self.sem, self.base + self.n)

    def end(self):
        assert self.n == self.per, (self.n, self.per)


def since(eng, sem, count):
    if isinstance(count, int) and count <= 0:
        return
    eng.wait_ge(sem, count)


def apart(eng, sem, count):
    if not isinstance(count, int):
        count = eng.to_reg(count)
        eng.wait_ge(sem, 1)
    since(eng, sem, count)


def constants():
    c = {}
    c["ident"] = np.eye(P, dtype=np.float32)
    c["before"] = np.triu(np.ones((P, P), np.float32), 1)
    c["ones"] = np.ones((P, P), np.float32)
    aug = np.zeros((P, 1), np.float32)
    aug[DH0::STRIP] = 1.0
    c["aug"] = aug
    e = np.arange(NE, dtype=np.float32)
    c["expert"] = np.tile(e, (P, 1))
    c["list"] = np.tile(e * ROWS_E, (P, 1))
    c["sizes"] = np.tile(np.arange(NB, dtype=np.float32) * P, (P, 1))
    c["upto"] = np.tile((e[None, :] <= e[:, None]).astype(np.float32).reshape(1, -1), (P, 1))
    c["tiles"] = np.tile(np.arange(N_TILES, dtype=np.float32), (P, 1))
    i, j = np.arange(P)[:, None], np.arange(TEXT)[None, :]
    c["before_band"] = (j - i <= -MAXREL).astype(np.float32)
    c["behind_band"] = (j - i >= MAXREL).astype(np.float32)
    return c


CONST = constants()
CONST_AT = {}
_at = 0
for _name, _a in CONST.items():
    CONST_AT[_name] = (_at, _at + _a.shape[1])
    _at += _a.shape[1]
CONST_W = _at


def layer0(nc, t, shared):
    with ExitStack() as ctx:
        def sb(name, shape, dt=F32):
            return ctx.enter_context(nc.sbuf_tensor(name, shape, dt))

        def ps(name, shape, dt=F32):
            return ctx.enter_context(nc.psum_tensor(name, shape, dt))

        def sem(name):
            shared["semaphores"].append(nc.alloc_semaphore(name=name))
            return shared["semaphores"][-1]

        const = shared["const"]

        def cst(name):
            a, z = CONST_AT[name]
            return const[:, a:z]

        ident, before, ones = cst("ident"), cst("before"), cst("ones")
        wq = sb("a_wq", [P, KD, MT0 * P])
        wk = sb("a_wk", [P, KD, MT0 * P])
        wv = sb("a_wv", [P, KD, D])
        wr = sb("a_wr", [P, KD, NE])
        bq = sb("a_bq", [P, MT0])
        bqs = sb("a_bqs", [P, MT0])
        bk = sb("a_bk", [P, MT0])
        bv = sb("a_bv", [P, D])
        gamma = sb("a_gamma", [P, D])
        beta = sb("a_beta", [P, D])
        br = sb("a_br", [P, NE])
        pick_bias = sb("a_pick_bias", [P, NE])
        zeros = sb("a_zeros", [P, D])

        x_in = [sb(f"a_x{p}", [P, D]) for p in range(2)]
        c_in = [sb(f"a_c{p}", [P, D]) for p in range(2)]
        mask_in = [sb(f"a_mask{p}", [P, P], I32) for p in range(2)]
        x_res = [sb(f"a_xr{p}", [P, D]) for p in range(2)]
        c_res = [sb(f"a_cr{p}", [P, D]) for p in range(2)]
        keep = [sb(f"a_keep{p}", [P, P]) for p in range(2)]
        stat = sb("a_stat", [P, 3, 6])
        agg = sb("a_agg", [P, 3, 2])
        rstd = sb("a_rstd", [P, 3, 2])
        xn = [sb(f"a_xn{p}", [P, D]) for p in range(2)]
        tT = [sb(f"a_tT{p}", [P, 4, P]) for p in range(2)]
        qT = [sb(f"a_qT{p}", [P, MT0, P]) for p in range(2)]
        kT = [sb(f"a_kT{p}", [P, MT0, P]) for p in range(2)]
        va = [sb(f"a_va{p}", [P, NH, DH0 + 1]) for p in range(2)]
        soft = [sb(f"a_soft{h}", [P, HPT // 2, MT0, P]) for h in range(2)]
        top = sb("a_top", [P, HPT, MT0])
        pT = [sb(f"a_pT{k}", [P, MT0, P]) for k in range(2)]
        den = sb("a_den", [P, NH])
        att = sb("a_att", [P, NH, DH0])
        attf = att[:, :, :].rearrange("p h d -> p (h d)")
        y = sb("a_y", [P, D])
        x1 = [sb(f"a_x1{p}", [P, D]) for p in range(2)]
        xn1 = [sb(f"a_xn1{p}", [P, D]) for p in range(2)]
        xn1T = sb("a_xn1T", [P, KD, P])
        score = sb("a_score", [P, NE])
        biased = sb("a_biased", [P, NE])
        best = sb("a_best", [P, 8])
        best_at = sb("a_best_at", [P, 8], U32)
        best_f = sb("a_best_f", [P, TOPK])
        chosen = sb("a_chosen", [P, NE])
        negmax = sb("a_negmax", [P, 1])
        escore = sb("a_escore", [P, NE])
        prod = sb("a_prod", [P, TOPK, NE])
        val = sb("a_val", [P, TOPK])
        tot = sb("a_tot", [P, 1])
        rtot = sb("a_rtot", [P, 1])
        at_row = sb("a_at_row", [P, NE])
        slot_i = [sb(f"a_slot{p}", [P, TOPK], I32) for p in range(2)]
        base = sb("a_base", [P, NE])
        count = sb("a_count", [P, NE])
        count_i = sb("a_count_i", [P, NE], I32)
        cmp16 = sb("a_cmp16", [P, NE, NB])
        ntile = sb("a_ntile", [P, NE])
        cmp8 = sb("a_cmp8", [P, NE, NE])
        tile_end = sb("a_tile_end", [P, NE])
        tile_start = sb("a_tile_start", [P, NE])
        shift = sb("a_shift", [P, NE])
        last = sb("a_last", [P, 1])
        tt = sb("a_tt", [P, N_TILES])
        cmpt = sb("a_cmpt", [P, N_TILES, NE])
        te = sb("a_te", [P, N_TILES])
        tr = sb("a_tr", [P, N_TILES])
        slot_c = sb("a_slot_c", [P, NB, TOPK])
        cmps = sb("a_cmps", [P, NB * TOPK, NE])

        S = [ps(f"a_S{j}", [P, MT0, P]) for j in range(HPT)]
        M = [ps(f"a_M{j}", [P, 512]) for j in range(2)]
        T = [ps(f"a_T{j}", [P, 512]) for j in range(2)]

        s_w = sem("a_weights")
        s_setup = sem("a_setup")
        s_bqs = sem("a_bqs")
        s_in = [sem(f"a_in{p}") for p in range(2)]
        s_res = [sem(f"a_res{p}") for p in range(2)]
        s_x1out = [sem(f"a_x1out{p}") for p in range(2)]
        names = ("keep var rstd xn t_mm t_sb q_mm q_sb k_mm k_sb v_mm v_sb s_mm s_sub s_exp p_mm p_sb pv_mm att var1 rstd1 "
                 "x1 var2 rstd2 xn1 t1_mm t1_sb r_mm score esc pos_mm chosen slot rows")
        g = {n: sem("a_" + n) for n in names.split()}
        s_sc = [sem(f"a_scatter{p}") for p in range(2)]
        s_pad = sem("a_pad")
        s_count = sem("a_count")
        l_ln, l_sm, l_a3, l_top, l_slot, l_fin, l_prefix = (
            sem("al_" + n) for n in "ln softmax out top slot final prefix".split())
        l_pool = [sem(f"al_pool{k}") for k in range(3)]

        W = [(wq[:, :, :], t["L0_wqT"].rearrange("(k p) n -> p k n", p=P)),
             (wk[:, :, :], t["L0_wkT"].rearrange("(k p) n -> p k n", p=P)),
             (wv[:, :, :], t["L0_wvT"].rearrange("(k p) n -> p k n", p=P)),
             (wr[:, :, :], t["L0_wrT"].rearrange("(k p) n -> p k n", p=P)),
             (bq[:, :], t["L0_bq"]), (bk[:, :], t["L0_bk"]),
             (bv[:, :], t["L0_bv"].partition_broadcast(P)),
             (gamma[:, :], t["L0_gamma"].partition_broadcast(P)),
             (beta[:, :], t["L0_beta"].partition_broadcast(P)),
             (br[:, :], t["L0_br"].partition_broadcast(P)),
             (pick_bias[:, :], t["L0_pick_bias"].partition_broadcast(P)),
             (const[:, :], t["const"])]
        W_READY = 16 * len(W)

        def by_batch(steps):
            def run(eng):
                for b in range(2):
                    steps(b, 0, b, b == 0, False)
                with eng.Fori(1, NB // 2 - 1) as i:
                    for p in range(2):
                        steps(i * 2 + p, i, p, False, False)
                for p in range(2):
                    steps(NB - 2 + p, NB // 2 - 1, p, False, p == 1)
            return run

        block = ctx.enter_context(nc.Block())

        @block.sync
        def _(sp):
            for dst, src in W[:3]:
                sp.dma_start(dst, src).then_inc(s_w, 16)

            def store(b, p):
                sp.wait_ge(g["x1"], b + 1)
                sp.dma_start(t["x1"][bass.ds(b, 1)].rearrange("o p d -> (o p) d"), x1[p][:, :]).then_inc(s_x1out[p], 16)

            def load(b, i, p, *_):
                since(sp, g["t_mm"], b - 1)
                since(sp, g["xn"], b - 1)
                since(sp, g["keep"], b - 1)
                sp.dma_start(x_in[p][:, :], t["x"][bass.ds(b, 1)].rearrange("o p d -> (o p) d")).then_inc(s_in[p], 16)
                sp.dma_start(c_in[p][:, :], t["ctx"][bass.ds(b, 1)].rearrange("o p d -> (o p) d")).then_inc(s_in[p], 16)
                sp.dma_start(mask_in[p][:, :], t["mask"][bass.ds(b, 1)].rearrange("o s -> (o s)").partition_broadcast(P))\
                    .then_inc(s_in[p], 16)
                if not (isinstance(b, int) and b < 2):
                    store(b - 2, p)
                sp.dma_start(x_res[p][:, :], t["x"][bass.ds(b, 1)].rearrange("o p d -> (o p) d")).then_inc(s_res[p], 16)
                sp.dma_start(c_res[p][:, :], t["ctx"][bass.ds(b, 1)].rearrange("o p d -> (o p) d")).then_inc(s_res[p], 16)

            by_batch(load)(sp)
            for p in range(2):
                store(NB - 2 + p, p)
            sp.wait_ge(s_count, 1)
            for e in range(NE):
                n = sp.value_load(count_i[0:1, e:e + 1], min_val=0, max_val=NB * P)
                sp.dma_start(t["lists"][bass.ds(n + e * ROWS_E, P)], zeros[:, :]).then_inc(s_pad, 16)
            sp.wait_ge(s_pad, 16 * NE)
            for p in range(2):
                sp.wait_ge(s_x1out[p], 16 * (NB // 2))

        @block.gpsimd
        def _(pool):
            nc.gpsimd.memset(zeros[:, :], 0.0).then_inc(s_setup, 1)
            nc.gpsimd.memset(shared["mhalf"][:, :], -0.5).then_inc(s_setup, 1)
            for p in range(2):
                nc.gpsimd.memset(va[p][:, :, :], 1.0).then_inc(s_setup, 1)
            pool.wait_ge(s_setup, 4)
            def inverse_std(link, eps, ready, done, b, k):
                apart(pool, ready, b + 1)
                link.begin(b)
                link(nc.gpsimd.tensor_scalar(rstd[:, k, 0:1], agg[:, k, 1:2], eps, None, ALU.add))
                nc.gpsimd.tensor_tensor(rstd[:, k, 1:2], rstd[:, k, 0:1], shared["mhalf"][:, :], ALU.pow).then_inc(done, 1)

            links = [Link(pool, l, 1) for l in l_pool]

            def std_in(b):
                inverse_std(links[0], EPS, g["var"], g["rstd"], b, 0)

            def std_out(b):
                inverse_std(links[1], EPS0, g["var1"], g["rstd1"], b, 1)
                inverse_std(links[2], EPS, g["var2"], g["rstd2"], b, 2)

            def scatter(b, i, p):
                apart(pool, g["slot"], b + 1)
                for k in range(TOPK):
                    nc.gpsimd.indirect_dma_start(t["lists"], bass.IndirectOffsetOnAxis(slot_i[p][:, k:k + 1], 0),
                                                 xn1[p][:, :], None).then_inc(s_sc[p], 16)

            std_in(0)
            std_in(1)

            def steps(b, i, p, first, last):
                if not first:
                    std_out(b - 1)
                if not (isinstance(b, int) and b + 2 >= NB):
                    std_in(b + 2)
                if not first:
                    scatter(b - 1, i - 1 + p, 1 - p)

            by_batch(steps)(pool)
            std_out(NB - 1)
            scatter(NB - 1, NB // 2 - 1, 1)
            for p in range(2):
                pool.wait_ge(s_sc[p], 32 * (NB // 2))

        @block.scalar
        def _(act):
            for dst, src in W[3:]:
                act.dma_start(dst, src).then_inc(s_w, 16)
            shared["load_experts"](act)
            act.wait_ge(s_w, W_READY)
            nc.scalar.activation(bqs[:, :], bq[:, :], ACT.Copy, scale=SCALE0).then_inc(s_bqs, 1)
            act.wait_ge(s_bqs, 1)
            act.wait_ge(s_setup, 4)

            def project(b, i, p):
                act.wait_ge(g["t_mm"], b + 1)
                since(act, g["v_mm"], b - 1)
                nc.scalar.activation(tT[p][:, :, :], T[0][:, :].rearrange("p (c n) -> p c n", c=4), ACT.Copy).then_inc(g["t_sb"], 1)

            def queries(b, i, p):
                act.wait_ge(g["q_mm"], b + 1)
                since(act, g["s_mm"], b - 1)
                for m in range(MT0):
                    ins = nc.scalar.activation(qT[p][:, m, :], M[0][:, m * P:(m + 1) * P], ACT.Identity,
                                               bias=bqs[:, m:m + 1], scale=SCALE0)
                ins.then_inc(g["q_sb"], 1)

            def values(b, i, p):
                act.wait_ge(g["v_mm"], b + 1)
                since(act, g["pv_mm"], 4 * (b - 1))
                nc.scalar.activation(va[p][:, :, 0:DH0], M[0][:, 0:D].rearrange("p (h d) -> p h d", h=NH), ACT.Copy)\
                    .then_inc(g["v_sb"], 1)

            def exps(b, h):
                act.wait_ge(g["s_sub"], 2 * b + h + 1)
                nc.scalar.activation(soft[h][:, :, :, :], soft[h][:, :, :, :], ACT.Exp).then_inc(g["s_exp"], 1)

            def probs(b, k):
                act.wait_ge(g["p_mm"], 4 * b + k + 1)
                since(act, g["pv_mm"], 4 * b + k - 1)
                nc.scalar.activation(pT[k % 2][:, :, :], T[k % 2][:, :].rearrange("p (h n) -> p h n", h=MT0), ACT.Copy)\
                    .then_inc(g["p_sb"], 1)

            def next_rows(b):
                act.wait_ge(g["t1_mm"], b + 1)
                since(act, g["r_mm"], b)
                nc.scalar.activation(xn1T[:, :, :], T[1][:, 0:D].rearrange("p (c n) -> p c n", c=KD), ACT.Copy).then_inc(g["t1_sb"], 1)

            def exp_scores(b):
                act.wait_ge(g["score"], b + 1)
                nc.scalar.activation(escore[:, :], score[:, :], ACT.Exp, bias=negmax[:, 0:1]).then_inc(g["esc"], 1)

            project(0, 0, 0)
            queries(0, 0, 0)
            values(0, 0, 0)

            def steps(b, i, p, first, last):
                if not first:
                    next_rows(b - 1)
                if not last:
                    project(b + 1, i + p, 1 - p)
                if not first:
                    exp_scores(b - 1)
                exps(b, 0)
                if not last:
                    queries(b + 1, i + p, 1 - p)
                exps(b, 1)
                if not last:
                    values(b + 1, i + p, 1 - p)
                for k in range(4):
                    probs(b, k)

            by_batch(steps)(act)
            next_rows(NB - 1)
            exp_scores(NB - 1)

        @block.tensor
        def _(pe):
            pe.wait_ge(s_w, W_READY)

            def transposes(b, i, p):
                pe.wait_ge(g["xn"], b + 1)
                pe.wait_ge(s_in[p], 48 * (i + 1))
                since(pe, g["p_sb"], 4 * b - 5)
                for c in range(KD):
                    nc.tensor.transpose(T[0][:, c * P:(c + 1) * P], xn[p][:, c * P:(c + 1) * P], ident)
                for c in range(KD):
                    ins = nc.tensor.transpose(T[0][:, (KD + c) * P:(KD + c + 1) * P], c_in[p][:, c * P:(c + 1) * P], ident)
                ins.then_inc(g["t_mm"], 1)

            def strips(out, w, src, done):
                for m in range(MT0):
                    for c in range(KD):
                        ins = nc.tensor.matmul(out[:, m * P:(m + 1) * P], w[:, c, m * P:(m + 1) * P], src[c],
                                               start=(c == 0), stop=(c == KD - 1))
                ins.then_inc(done, 1)

            def queries(b, i, p):
                pe.wait_ge(g["t_sb"], b + 1)
                since(pe, g["v_sb"], b)
                strips(M[0], wq, [tT[p][:, c, :] for c in range(KD)], g["q_mm"])

            def keys(b, i, p):
                since(pe, g["att"], b - 1)
                strips(M[1], wk, [tT[p][:, KD + c, :] for c in range(KD)], g["k_mm"])

            def values(b, i, p):
                pe.wait_ge(g["q_sb"], b + 1)
                for c in range(KD):
                    ins = nc.tensor.matmul(M[0][:, 0:D], tT[p][:, KD + c, :], wv[:, c, :], start=(c == 0), stop=(c == KD - 1))
                ins.then_inc(g["v_mm"], 1)

            def scores(b, i, p):
                pe.wait_ge(g["q_sb"], b + 1)
                pe.wait_ge(g["k_sb"], b + 1)
                since(pe, g["s_sub"], 2 * b)
                for m in range(MT0):
                    for j in range(HPT):
                        r = slice(j * STRIP, (j + 1) * STRIP)
                        ins = nc.tensor.matmul(S[j][:, m, :], qT[p][r, m, :], kT[p][r, m, :], start=True, stop=True)
                ins.then_inc(g["s_mm"], 1)

            def attend(b, i, p, k, last):
                pe.wait_ge(g["s_exp"], 2 * b + k // 2 + 1)
                since(pe, g["p_sb"], 4 * b + k - 1)
                if k == 0 and not last:
                    pe.wait_ge(g["t_sb"], b + 2)
                if k == 1:
                    since(pe, g["slot"], b)
                for m in range(MT0):
                    ins = nc.tensor.transpose(T[k % 2][:, m * P:(m + 1) * P], soft[k // 2][:, k % 2, m, :], ident)
                ins.then_inc(g["p_mm"], 1)
                pe.wait_ge(g["p_sb"], 4 * b + k + 1)
                if k == 0:
                    pe.wait_ge(g["v_sb"], b + 1)
                    if not last:
                        pe.wait_ge(g["k_sb"], b + 2)
                for m in range(MT0):
                    head = m * HPT + k
                    ins = nc.tensor.matmul(M[1][:, head * (DH0 + 1):(head + 1) * (DH0 + 1)], pT[k % 2][:, m, :],
                                           va[p][:, head, :], start=True, stop=True)
                ins.then_inc(g["pv_mm"], 1)

            def next_rows(b, i, p):
                pe.wait_ge(g["xn1"], b + 1)
                pe.wait_ge(g["p_sb"], 4 * b + 4)
                for c in range(KD):
                    ins = nc.tensor.transpose(T[1][:, c * P:(c + 1) * P], xn1[p][:, c * P:(c + 1) * P], ident)
                ins.then_inc(g["t1_mm"], 1)

            def router(b):
                pe.wait_ge(g["t1_sb"], b + 1)
                for c in range(KD):
                    ins = nc.tensor.matmul(T[1][:, D:D + NE], xn1T[:, c, :], wr[:, c, :], start=(c == 0), stop=(c == KD - 1))
                ins.then_inc(g["r_mm"], 1)

            def places(b):
                pe.wait_ge(g["chosen"], b + 1)
                nc.tensor.matmul(T[1][:, D + NE:D + 2 * NE], before, chosen[:, :], start=True, stop=True)
                nc.tensor.matmul(T[1][:, D + 2 * NE:D + 3 * NE], ones, chosen[:, :], start=True, stop=True)\
                    .then_inc(g["pos_mm"], 1)

            transposes(0, 0, 0)
            queries(0, 0, 0)
            keys(0, 0, 0)
            values(0, 0, 0)

            def steps(b, i, p, first, last):
                scores(b, i, p)
                if not first:
                    next_rows(b - 1, i - 1 + p, 1 - p)
                if not last:
                    transposes(b + 1, i + p, 1 - p)
                if not first:
                    router(b - 1)
                if not last:
                    queries(b + 1, i + p, 1 - p)
                    keys(b + 1, i + p, 1 - p)
                if not first:
                    places(b - 1)
                if not last:
                    values(b + 1, i + p, 1 - p)
                for k in range(4):
                    attend(b, i, p, k, last)

            by_batch(steps)(pe)
            next_rows(NB - 1, NB // 2 - 1, 1)
            router(NB - 1)
            places(NB - 1)

        @block.vector
        def _(dve):
            dve.wait_ge(s_w, W_READY)
            ln, sm, out, pick, place = (Link(dve, s, n) for s, n in
                                        ((l_ln, 1), (l_sm, 2), (l_a3, 8), (l_top, 7), (l_slot, 4)))
            fin = Link(dve, l_fin, 21)
            fin.begin(0)
            fin(nc.vector.tensor_copy(base[:, :], cst("list")))

            def norm_in(b, i, p):
                dve.wait_ge(s_in[p], 48 * (i + 1))
                nc.vector.tensor_scalar(keep[p][:, :], mask_in[p][:, :], 0.0, cst("aug"), ALU.not_equal, ALU.not_equal)\
                    .then_inc(g["keep"], 1)
                ln.begin(b)
                ln(nc.vector.bn_stats(stat[:, 0, :], x_in[p][:, :]))
                ln.end()
                nc.vector.bn_aggr(agg[:, 0, :], stat[:, 0, :]).then_inc(g["var"], 1)
                dve.wait_ge(g["rstd"], b + 1)
                since(dve, g["t_mm"], b - 1)
                nc.vector.tensor_scalar(xn[p][:, :], x_in[p][:, :], agg[:, 0, 0:1], rstd[:, 0, 1:2], ALU.subtract, ALU.mult)\
                    .then_inc(g["xn"], 1)

            def keys(b, i, p):
                dve.wait_ge(g["k_mm"], b + 1)
                since(dve, g["s_mm"], b - 1)
                dve.wait_ge(g["keep"], b + 1)
                for m in range(MT0):
                    ins = nc.vector.scalar_tensor_tensor(kT[p][:, m, :], M[1][:, m * P:(m + 1) * P], bk[:, m:m + 1],
                                                         keep[p][:, :], ALU.add, ALU.mult)
                ins.then_inc(g["k_sb"], 1)

            def less_max(b, h):
                dve.wait_ge(g["s_mm"], b + 1)
                for u in range(HPT // 2):
                    j = h * (HPT // 2) + u
                    ins = nc.vector.tensor_reduce(top[:, j, :], S[j][:, :, :], X, ALU.max)
                sm(ins)
                since(dve, g["p_mm"], 4 * (b - 1) + 2 * h + 2)
                for u in range(HPT // 2):
                    j = h * (HPT // 2) + u
                    ins = nc.vector.tensor_tensor(soft[h][:, u, :, :], S[j][:, :, :],
                                                  top[:, j, :].unsqueeze(2).to_broadcast([P, MT0, P]), ALU.subtract)
                ins.then_inc(g["s_sub"], 1)

            def attention_out(b, i, p):
                out.begin(b)
                dve.wait_ge(g["pv_mm"], 4 * b + 4)
                o = M[1][:, 0:NH * (DH0 + 1)].rearrange("p (h d) -> p h d", h=NH)
                out(nc.vector.reciprocal(den[:, :], o[:, :, DH0]))
                ins = nc.vector.tensor_tensor(att[:, :, :], o[:, :, 0:DH0], den[:, :].unsqueeze(2).to_broadcast([P, NH, DH0]),
                                              ALU.mult)
                ins.then_inc(g["att"], 1)
                dve.wait_ge(g["att"], b + 1)
                out(nc.vector.tensor_tensor(attf, attf, bv[:, :], ALU.add))
                dve.wait_ge(s_res[p], 32 * (i + 1))
                out(nc.vector.tensor_tensor(attf, attf, c_res[p][:, :], ALU.add))
                out(nc.vector.bn_stats(stat[:, 1, :], attf))
                nc.vector.bn_aggr(agg[:, 1, :], stat[:, 1, :]).then_inc(g["var1"], 1)
                dve.wait_ge(g["rstd1"], b + 1)
                out(nc.vector.tensor_scalar(y[:, :], attf, agg[:, 1, 0:1], rstd[:, 1, 1:2], ALU.subtract, ALU.mult))
                out(nc.vector.tensor_tensor(y[:, :], y[:, :], gamma[:, :], ALU.mult))
                out(nc.vector.tensor_tensor(y[:, :], y[:, :], beta[:, :], ALU.add))
                since(dve, s_x1out[p], 16 * i)
                nc.vector.tensor_tensor(x1[p][:, :], y[:, :], x_res[p][:, :], ALU.add).then_inc(g["x1"], 1)
                dve.wait_ge(g["x1"], b + 1)
                out(nc.vector.bn_stats(stat[:, 2, :], x1[p][:, :]))
                nc.vector.bn_aggr(agg[:, 2, :], stat[:, 2, :]).then_inc(g["var2"], 1)
                dve.wait_ge(g["rstd2"], b + 1)
                since(dve, s_sc[p], 32 * i)
                nc.vector.tensor_scalar(xn1[p][:, :], x1[p][:, :], agg[:, 2, 0:1], rstd[:, 2, 1:2], ALU.subtract, ALU.mult)\
                    .then_inc(g["xn1"], 1)
                out.end()

            onehot, slots, weights = shared["onehot"], shared["slots"], shared["weights"]

            def hot(b):
                return onehot[:, bass.ds(b, 1)].rearrange("p o k e -> p (o k) e")

            def choose(b):
                pick.begin(b)
                dve.wait_ge(g["r_mm"], b + 1)
                since(dve, g["esc"], b)
                pick(nc.vector.tensor_tensor(score[:, :], T[1][:, D:D + NE], br[:, :], ALU.add))
                nc.vector.tensor_reduce(negmax[:, :], score[:, :], X, ALU.max, negate=True).then_inc(g["score"], 1)
                pick(nc.vector.tensor_tensor(biased[:, :], score[:, :], pick_bias[:, :], ALU.add))
                pick(nc.vector.max(best[:, :], biased[:, :]))
                pick(nc.vector.max_index(best_at[:, :], best[:, :], biased[:, :]))
                pick(nc.vector.tensor_copy(best_f[:, :], best_at[:, 0:TOPK]))
                for k in range(TOPK):
                    ins = nc.vector.tensor_scalar(onehot[:, bass.ds(b, 1), k, :].rearrange("p o e -> p (o e)"), cst("expert"),
                                                  best_f[:, k:k + 1], None, ALU.is_equal)
                pick(ins)
                oh = hot(b)
                since(dve, g["pos_mm"], b)
                nc.vector.tensor_tensor(chosen[:, :], oh[:, 0, :], oh[:, 1, :], ALU.add).then_inc(g["chosen"], 1)
                dve.wait_ge(g["esc"], b + 1)
                pick(nc.vector.tensor_tensor(prod[:, :, :], oh, escore[:, :].unsqueeze(1).to_broadcast([P, TOPK, NE]), ALU.mult))
                pick.end()

            def list_rows(b, i, p):
                place.begin(b)
                place(nc.vector.tensor_reduce(val[:, :], prod[:, :, :], X, ALU.add))
                place(nc.vector.tensor_tensor(tot[:, :], val[:, 0:1], val[:, 1:2], ALU.add))
                place(nc.vector.reciprocal(rtot[:, :], tot[:, :]))
                nc.vector.tensor_scalar(weights[:, bass.ds(b, 1), :].rearrange("p o k -> p (o k)"), val[:, :], rtot[:, 0:1], None, ALU.mult)
                dve.wait_ge(g["pos_mm"], b + 1)
                place(nc.vector.tensor_tensor(at_row[:, :], T[1][:, D + NE:D + 2 * NE], base[:, :], ALU.add))
                place.end()
                nc.vector.tensor_tensor(base[:, :], T[1][:, D + 2 * NE:D + 3 * NE], base[:, :], ALU.add).then_inc(l_prefix, 1)
                nc.vector.tensor_tensor(prod[:, :, :], hot(b), at_row[:, :].unsqueeze(1).to_broadcast([P, TOPK, NE]), ALU.mult)\
                    .then_inc(l_prefix, 1)
                dve.wait_ge(l_prefix, 3 * b + 2)
                row = slots[:, bass.ds(b, 1), :].rearrange("p o k -> p (o k)")
                nc.vector.tensor_reduce(row, prod[:, :, :], X, ALU.add).then_inc(l_prefix, 1)
                apart(dve, l_prefix, 3 * b + 3)
                since(dve, s_sc[p], 32 * i)
                nc.vector.tensor_copy(slot_i[p][:, :], row).then_inc(g["slot"], 1)

            norm_in(0, 0, 0)
            keys(0, 0, 0)
            norm_in(1, 0, 1)

            def steps(b, i, p, first, last):
                sm.begin(b)
                if not first:
                    attention_out(b - 1, i - 1 + p, 1 - p)
                less_max(b, 0)
                if not first:
                    choose(b - 1)
                less_max(b, 1)
                sm.end()
                if not last:
                    keys(b + 1, i + p, 1 - p)
                if not first:
                    list_rows(b - 1, i - 1 + p, 1 - p)

            def steps_and_norm(b, i, p, first, last):
                steps(b, i, p, first, last)
                if not (isinstance(b, int) and b + 2 >= NB):
                    norm_in(b + 2, i + 1, p)

            by_batch(steps_and_norm)(dve)
            attention_out(NB - 1, NB // 2 - 1, 1)
            choose(NB - 1)
            list_rows(NB - 1, NB // 2 - 1, 1)

            dve.wait_ge(g["slot"], NB)
            dve.wait_ge(l_prefix, 3 * NB)
            fin(nc.vector.tensor_tensor(count[:, :], base[:, :], cst("list"), ALU.subtract))
            nc.vector.tensor_copy(count_i[:, :], count[:, :]).then_inc(s_count, 1)
            fin(nc.vector.tensor_tensor(cmp16[:, :, :], count[:, :].unsqueeze(2).to_broadcast([P, NE, NB]),
                                        cst("sizes").unsqueeze(1).to_broadcast([P, NE, NB]), ALU.is_gt))
            fin(nc.vector.tensor_reduce(ntile[:, :], cmp16[:, :, :], X, ALU.add))
            fin(nc.vector.tensor_tensor(cmp8[:, :, :], cst("upto").rearrange("p (a b) -> p a b", a=NE),
                                        ntile[:, :].unsqueeze(1).to_broadcast([P, NE, NE]), ALU.mult))
            fin(nc.vector.tensor_reduce(tile_end[:, :], cmp8[:, :, :], X, ALU.add))
            fin(nc.vector.tensor_tensor(tile_start[:, :], tile_end[:, :], ntile[:, :], ALU.subtract))
            fin(nc.vector.scalar_tensor_tensor(shift[:, :], tile_start[:, :], -float(P), cst("list"), ALU.mult, ALU.add))
            fin(nc.vector.tensor_scalar(last[:, :], tile_end[:, NE - 1:NE], -1.0, None, ALU.add))
            fin(nc.vector.tensor_scalar(tt[:, :], cst("tiles"), last[:, 0:1], None, ALU.min))
            fin(nc.vector.tensor_tensor(cmpt[:, :, :], tile_end[:, :].unsqueeze(1).to_broadcast([P, N_TILES, NE]),
                                        tt[:, :].unsqueeze(2).to_broadcast([P, N_TILES, NE]), ALU.is_le))
            fin(nc.vector.tensor_reduce(te[:, :], cmpt[:, :, :], X, ALU.add))
            nc.vector.tensor_copy(shared["tile_expert"][:, :], te[:, :])
            fin(nc.vector.tensor_tensor(cmpt[:, :, :], cst("expert").unsqueeze(1).to_broadcast([P, N_TILES, NE]),
                                        te[:, :].unsqueeze(2).to_broadcast([P, N_TILES, NE]), ALU.is_equal))
            fin(nc.vector.tensor_tensor(cmpt[:, :, :], cmpt[:, :, :], shift[:, :].unsqueeze(1).to_broadcast([P, N_TILES, NE]), ALU.mult))
            fin(nc.vector.tensor_reduce(tr[:, :], cmpt[:, :, :], X, ALU.add))
            fin(nc.vector.scalar_tensor_tensor(tr[:, :], tt[:, :], float(P), tr[:, :], ALU.mult, ALU.add))
            fin(nc.vector.tensor_copy(shared["tile_row"][:, :], tr[:, :]))
            flat = onehot[:, :, :, :].rearrange("p b k e -> p (b k) e")
            fin(nc.vector.tensor_tensor(cmps[:, :, :], flat, shift[:, :].unsqueeze(1).to_broadcast([P, NB * TOPK, NE]), ALU.mult))
            fin(nc.vector.tensor_reduce(slot_c[:, :, :].rearrange("p b k -> p (b k)"), cmps[:, :, :], X, ALU.add))
            fin(nc.vector.tensor_tensor(slot_c[:, :, :], slots[:, :, :], slot_c[:, :, :], ALU.subtract))
            fin(nc.vector.tensor_copy(shared["tile_rows"][:, :, :], slot_c[:, :, :]))
            fin.end()


def experts(nc, t, shared):
    with ExitStack() as ctx:
        def sb(name, shape, dt=F32):
            return ctx.enter_context(nc.sbuf_tensor(name, shape, dt))

        def ps(name, shape, dt=F32):
            return ctx.enter_context(nc.psum_tensor(name, shape, dt))

        def sem(name):
            shared["semaphores"].append(nc.alloc_semaphore(name=name))
            return shared["semaphores"][-1]

        a, z = CONST_AT["ident"]
        ident = shared["const"][:, a:z]
        w1, w2, b1, b2 = (shared[n] for n in ("w1", "w2", "b1", "b2"))
        tile_expert, tile_row = shared["tile_expert"], shared["tile_row"]
        rows = [sb(f"b_rows{p}", [P, D]) for p in range(2)]
        rowsT = [sb(f"b_rowsT{p}", [P, KD, P]) for p in range(2)]
        gate = [sb(f"b_gate{p}", [P, HE]) for p in range(2)]
        up = [sb(f"b_up{p}", [P, HE]) for p in range(2)]
        hidT = [sb(f"b_hidT{p}", [P, KH, P]) for p in range(2)]
        out = [sb(f"b_out{p}", [P, D]) for p in range(2)]
        G = [ps(f"b_G{p}", [P, HE]) for p in range(2)]
        U = [ps(f"b_U{p}", [P, HE]) for p in range(2)]
        RT = ps("b_RT", [P, KD, P])
        HT = ps("b_HT", [P, KH, P])
        Y = ps("b_Y", [P, D])

        s_in = [sem(f"b_in{p}") for p in range(2)]
        s_out = [sem(f"b_out_{p}") for p in range(2)]
        names = "rt_mm rt_sb g_mm u_mm gate silu up hid ht_mm ht_sb y_mm y_sb"
        g = {n: sem("b_" + n) for n in names.split()}

        def by_tile(steps):
            def run(eng):
                for n in range(2):
                    steps(n, 0, n, n == 0, False)
                with eng.Fori(1, (N_TILES - 3) // 2 + 1) as i:
                    for p in range(2):
                        steps(i * 2 + p, i, p, False, False)
                n = 2 * ((N_TILES - 3) // 2 + 1)
                while n < N_TILES:
                    steps(n, n // 2, n % 2, False, n == N_TILES - 1)
                    n += 1
            return run

        block = ctx.enter_context(nc.Block())

        @block.sync
        def _(sp):
            def steps(n, i, p, *_):
                if isinstance(n, int):
                    at = tile_row[0:1, n:n + 1]
                else:
                    at = tile_row[0:1, bass.ds(n, 1)]
                row = sp.value_load(at, min_val=0, max_val=NE * ROWS_E - P)
                since(sp, g["rt_mm"], n - 1)
                sp.dma_start(rows[p][:, :], t["lists"][bass.ds(row, P)]).then_inc(s_in[p], 16)

            by_tile(steps)(sp)

        @block.gpsimd
        def _(pool):
            def steps(n, i, p, *_):
                pool.wait_ge(g["silu"], n + 1)
                pool.wait_ge(g["up"], n + 1)
                nc.gpsimd.tensor_tensor(up[p][:, :], up[p][:, :], gate[p][:, :], ALU.mult).then_inc(g["hid"], 1)

            by_tile(steps)(pool)

        @block.scalar
        def _(act):
            def rows_sb(n, i, p):
                act.wait_ge(g["rt_mm"], n + 1)
                since(act, g["u_mm"], n - 1)
                nc.scalar.activation(rowsT[p][:, :, :], RT[:, :, :], ACT.Copy).then_inc(g["rt_sb"], 1)

            rows_sb(0, 0, 0)

            def steps(n, i, p, first, last):
                if not last:
                    rows_sb(n + 1, i + p, 1 - p)
                act.wait_ge(g["gate"], n + 1)
                nc.scalar.activation(gate[p][:, :], gate[p][:, :], ACT.Silu).then_inc(g["silu"], 1)
                act.wait_ge(g["ht_mm"], n + 1)
                since(act, g["y_mm"], n - 1)
                nc.scalar.activation(hidT[p][:, :, :], HT[:, :, :], ACT.Copy).then_inc(g["ht_sb"], 1)
                act.wait_ge(g["y_sb"], n + 1)
                act.dma_start(t["expert_out"][bass.ds(n * P, P)], out[p][:, :]).then_inc(s_out[p], 16)

            by_tile(steps)(act)
            act.wait_ge(s_out[0], 16 * ((N_TILES + 1) // 2))
            act.wait_ge(s_out[1], 16 * (N_TILES // 2))

        def expert_of(eng, n):
            at = tile_expert[0:1, n:n + 1] if isinstance(n, int) else tile_expert[0:1, bass.ds(n, 1)]
            return eng.value_load(at, min_val=0, max_val=NE - 1)

        @block.tensor
        def _(pe):
            pe.wait_ge(shared["s_experts"], 16 * 4)

            def transposes(n, i, p):
                pe.wait_ge(s_in[p], 16 * (i + 1))
                since(pe, g["rt_sb"], n)
                for c in range(KD):
                    ins = nc.tensor.transpose(RT[:, c, :], rows[p][:, c * P:(c + 1) * P], ident)
                ins.then_inc(g["rt_mm"], 1)

            def first_products(n, i, p):
                e = expert_of(pe, n)
                pe.wait_ge(g["rt_sb"], n + 1)
                since(pe, g["gate"], n - 1)
                since(pe, g["up"], n - 1)
                for at, dst, done in ((0, G[p], g["g_mm"]), (HE, U[p], g["u_mm"])):
                    for c in range(KD):
                        w = w1[:, bass.ds(e, 1), c, at:at + HE].rearrange("p o n -> p (o n)")
                        ins = nc.tensor.matmul(dst[:, :], rowsT[p][:, c, :], w, start=(c == 0), stop=(c == KD - 1))
                    ins.then_inc(done, 1)

            transposes(0, 0, 0)
            first_products(0, 0, 0)

            def steps(n, i, p, first, last):
                if not last:
                    transposes(n + 1, i + p, 1 - p)
                    first_products(n + 1, i + p, 1 - p)
                pe.wait_ge(g["hid"], n + 1)
                since(pe, g["ht_sb"], n)
                for k in range(KH):
                    ins = nc.tensor.transpose(HT[:, k, :], up[p][:, k * P:(k + 1) * P], ident)
                ins.then_inc(g["ht_mm"], 1)
                e = expert_of(pe, n)
                pe.wait_ge(g["ht_sb"], n + 1)
                since(pe, g["y_sb"], n)
                for k in range(KH):
                    w = w2[:, bass.ds(e, 1), k, :].rearrange("p o n -> p (o n)")
                    ins = nc.tensor.matmul(Y[:, :], hidT[p][:, k, :], w, start=(k == 0), stop=(k == KH - 1))
                ins.then_inc(g["y_mm"], 1)

            by_tile(steps)(pe)

        @block.vector
        def _(dve):
            dve.wait_ge(shared["s_experts"], 16 * 4)

            def hidden(n, i, p):
                e = expert_of(dve, n)
                dve.wait_ge(g["g_mm"], n + 1)
                since(dve, g["hid"], n - 1)
                bias = b1[:, bass.ds(e, 1), :].rearrange("p o n -> p (o n)")
                nc.vector.tensor_tensor(gate[p][:, :], G[p][:, :], bias[:, 0:HE], ALU.add).then_inc(g["gate"], 1)
                dve.wait_ge(g["u_mm"], n + 1)
                since(dve, g["ht_mm"], n - 1)
                nc.vector.tensor_tensor(up[p][:, :], U[p][:, :], bias[:, HE:2 * HE], ALU.add).then_inc(g["up"], 1)

            hidden(0, 0, 0)

            def steps(n, i, p, first, last):
                if not last:
                    hidden(n + 1, i + p, 1 - p)
                e = expert_of(dve, n)
                dve.wait_ge(g["y_mm"], n + 1)
                since(dve, s_out[p], 16 * i)
                nc.vector.tensor_tensor(out[p][:, :], Y[:, :], b2[:, bass.ds(e, 1), :].rearrange("p o n -> p (o n)"), ALU.add)\
                    .then_inc(g["y_sb"], 1)

            by_tile(steps)(dve)


DH1 = 64
INNER = NH * DH1
MT1 = INNER // P
NREL = 2 * MAXREL + 1
STREAMS = [(0, TEXT), (TEXT, TEXT + IMG), (TEXT + IMG, P)]
NS = len(STREAMS)
SCALE1 = 1.0 / DH1 ** 0.5
RELW = P - 1 + TEXT
REL_LO = P - 1 - MAXREL
BANDW = P + 2 * MAXREL
HS = NH // 2


def attention1(nc, t, shared):
    with ExitStack() as ctx:
        def sb(name, shape, dt=F32):
            return ctx.enter_context(nc.sbuf_tensor(name, shape, dt))

        def ps(name, shape, dt=F32):
            return ctx.enter_context(nc.psum_tensor(name, shape, dt))

        def sem(name):
            shared["semaphores"].append(nc.alloc_semaphore(name=name))
            return shared["semaphores"][-1]

        const = shared["const"]

        def cst(name):
            a, z = CONST_AT[name]
            return const[:, a:z]

        ident = cst("ident")
        wq = sb("c_wq", [P, KD, INNER])
        wk = [sb(f"c_wk{s}", [P, KD, INNER]) for s in range(NS)]
        wv = [sb(f"c_wv{s}", [P, KD, INNER]) for s in range(NS)]
        wo = sb("c_wo", [P, MT1, D])
        relk = sb("c_relk", [P, 2 * NREL])
        relv = sb("c_relv", [2 * NREL, 2 * DH1])
        bo = sb("c_bo", [P, D])
        alphas = sb("c_alphas", [P, 2])
        tanhs = sb("c_tanhs", [P, 2])
        coef = sb("c_coef", [P, NS, NH])
        zeros = sb("c_zeros", [P, BANDW])

        two = range(2)
        x_in = [sb(f"c_x{p}", [P, D]) for p in two]
        c_in = [sb(f"c_c{p}", [P, D]) for p in two]
        pick = [sb(f"c_pick{p}", [P, TOPK], I32) for p in two]
        picked = [[sb(f"c_y{p}{k}", [P, D]) for k in range(TOPK)] for p in two]
        x2 = [sb(f"c_x2{p}", [P, D]) for p in two]
        x2b = [sb(f"c_x2b{p}", [P, D]) for p in two]
        x3 = [sb(f"c_x3{p}", [P, D]) for p in two]
        stat = sb("c_stat", [P, 6])
        agg = sb("c_agg", [P, 2])
        rstd = sb("c_rstd", [P, 2])
        xn = [sb(f"c_xn{p}", [P, D]) for p in two]
        tT = [sb(f"c_tT{p}", [P, 4, P]) for p in two]
        qT = [sb(f"c_qT{p}", [P, MT1, P]) for p in two]
        kT = [sb(f"c_kT{p}", [P, MT1, P]) for p in two]
        vT = sb("c_vT", [P, MT1, P])
        v = [sb(f"c_v{p}", [P, INNER]) for p in two]
        rel = sb("c_rel", [P, NH, NREL])
        relw = [sb(f"c_relw{p}", [P, NH, RELW]) for p in two]
        bias = [sb(f"c_bias{p}", [P, NH, TEXT]) for p in two]
        soft = [sb(f"c_soft{p}", [P, NH, P]) for p in two]
        top = sb("c_top", [P, NS, NH])
        total = sb("c_total", [P, NS, NH])
        share = sb("c_share", [P, NS, NH])
        pT = [sb(f"c_pT{k}", [P, 4, P]) for k in two]
        near = sb("c_near", [P, NH, TEXT])
        far = sb("c_far", [P, NH, TEXT])
        band = [sb(f"c_band{p}", [P, NH, NREL]) for p in two]
        bandT = sb("c_bandT", [2 * NREL, NH // 2, P])
        att = sb("c_att", [P, INNER])
        attT = sb("c_attT", [P, MT1, P])

        S = ps("c_S", [P, NH, P])
        T = [ps(f"c_T{k}", [P, 512]) for k in two]
        O = ps("c_O", [P, INNER])

        rel_d = [nc.dram_tensor(f"rel_windows{p}", (P, NH, RELW), F32, kind="Internal").ap() for p in two]
        prob_d = [nc.dram_tensor(f"prob_rows{p}", (P, NH, BANDW), F32, kind="Internal").ap() for p in two]

        s_w = sem("c_weights")
        s_zero = sem("c_zero")
        s_setup = sem("c_setup")
        s_alpha = sem("c_alpha")
        s_clear = sem("c_clear")
        s_in = [sem(f"c_in{p}") for p in two]
        s_pick = [sem(f"c_picked{p}") for p in two]
        s_relout = [sem(f"c_relout{p}") for p in two]
        s_relin = [sem(f"c_relin{p}") for p in two]
        s_pout = [sem(f"c_pout{p}") for p in two]
        s_pin = [sem(f"c_pin{p}") for p in two]
        s_x3 = [sem(f"c_x3out{p}") for p in two]
        names = ("pick x2 var rstd xn x2b t_mm t_sb q_mm q_sb r_mm r_sb k_mm k_sb vt_mm vt_sb v_mm v_sb relw s_mm s_sub s_exp "
                 "share soft tails bandv w_mm w_sb o_mm o_sb ot_mm ot_sb y_mm x3 p_mm p_sb pv_mm")
        g = {n: sem("c_" + n) for n in names.split()}
        l_front, l_sum, l_pool = (sem("cl_" + n) for n in "front sum pool".split())
        l_softs = [sem(f"cl_soft{h}") for h in range(2)]

        W = [(wq[:, :, :], t["L1_Wq"].rearrange("(k p) n -> p k n", p=P))]
        W += [(relk[:, :], t["L1_relk"]), (relv[:, :], t["L1_relv"]), (bo[:, :], t["L1_bo"].partition_broadcast(P)),
              (alphas[:, :], t["L1_alphas"].partition_broadcast(P))]
        for s in range(NS):
            W.append((wk[s][:, :, :], t[f"L1_Wk{s}"].rearrange("(k p) n -> p k n", p=P)))
        for s in range(NS):
            W.append((wv[s][:, :, :], t[f"L1_Wv{s}"].rearrange("(k p) n -> p k n", p=P)))
        W.append((wo[:, :, :], t["L1_Wo"].rearrange("(k p) n -> p k n", p=P)))
        W_READY = 16 * len(W)

        def sheared(d, at, step, parts, width):
            part, head, _ = d.ap
            return bass.AP(d.tensor, d.offset + at, [[part[0] + step, parts], [head[0], NH], [1, width]])

        def by_batch(steps):
            def run(eng):
                for b in range(2):
                    steps(b, 0, b, b == 0, False)
                with eng.Fori(1, NB // 2 - 1) as i:
                    for p in range(2):
                        steps(i * 2 + p, i, p, False, False)
                for p in range(2):
                    steps(NB - 2 + p, NB // 2 - 1, p, False, p == 1)
            return run

        def beyond(b):
            return isinstance(b, int) and b >= NB

        def rows_of(d, b):
            return d[bass.ds(b, 1)].rearrange("o p d -> (o p) d")

        block = ctx.enter_context(nc.Block())

        @block.sync
        def _(sp):
            def load(b, i, p):
                since(sp, g["xn"], b - 1)
                since(sp, g["t_mm"], b - 1)
                sp.dma_start(x_in[p][:, :], rows_of(t["x1"], b)).then_inc(s_in[p], 16)
                sp.dma_start(c_in[p][:, :], rows_of(t["ctx"], b)).then_inc(s_in[p], 16)

            def rel_out(b, i, p):
                sp.wait_ge(g["relw"], b + 1)
                since(sp, s_relin[p], 16 * i)
                sp.dma_start(rel_d[p], relw[p][:, :, :]).then_inc(s_relout[p], 16)

            def rel_in(b, i, p):
                sp.wait_ge(s_relout[p], 16 * (i + 1))
                since(sp, g["s_sub"], 2 * (b - 1))
                sp.dma_start(bias[p][:, :, :], sheared(rel_d[p], P - 1, -1, P, TEXT)).then_inc(s_relin[p], 16)

            def prob_out(b, i, p):
                apart(sp, g["soft"], 2 * b + 2)
                since(sp, s_pin[p], 16 * i)
                sp.dma_start(prob_d[p][:, :, MAXREL:MAXREL + TEXT], soft[p][:, :, 0:TEXT]).then_inc(s_pout[p], 16)

            def band_in(b, i, p):
                sp.wait_ge(s_pout[p], 16 * (i + 1))
                since(sp, g["w_mm"], b - 1)
                sp.dma_start(band[p][:, :, 1:NREL - 1], sheared(prob_d[p], 1, 1, P, NREL - 2)).then_inc(s_pin[p], 16)

            def store(b, p):
                sp.wait_ge(g["x3"], b + 1)
                sp.dma_start(rows_of(t["x3"], b), x3[p][:, :]).then_inc(s_x3[p], 16)

            load(0, 0, 0)
            load(1, 0, 1)
            for dst, src in W[:5]:
                sp.dma_start(dst, src).then_inc(s_w, 16)
            for p in two:
                sp.wait_ge(s_zero, 1)
                for h in range(NH):
                    sp.dma_start(prob_d[p][:, h, :], zeros[:, :]).then_inc(s_clear, 16)
            sp.wait_ge(s_clear, 16 * 2 * NH)
            rel_out(0, 0, 0)
            rel_in(0, 0, 0)

            def steps(b, i, p, first, last):
                if not first:
                    store(b - 1, 1 - p)
                if not beyond(b + 2):
                    load(b + 2, i + 1, p)
                prob_out(b, i, p)
                if not last:
                    rel_out(b + 1, i + p, 1 - p)
                band_in(b, i, p)
                if not last:
                    rel_in(b + 1, i + p, 1 - p)

            by_batch(steps)(sp)
            store(NB - 1, 1)
            for p in two:
                sp.wait_ge(s_x3[p], 16 * (NB // 2))

        @block.gpsimd
        def _(pool):
            nc.gpsimd.memset(zeros[:, :], 0.0).then_inc(s_zero, 1)
            pool.wait_ge(s_w, W_READY)
            pool.wait_ge(s_alpha, NS)
            lk = Link(pool, l_pool, 1)

            def gather(b, i, p):
                since(pool, g["x2"], b - 1)
                apart(pool, g["pick"], b + 1)
                for k in range(TOPK):
                    nc.gpsimd.indirect_dma_start(picked[p][k][:, :], None, t["expert_out"],
                                                 bass.IndirectOffsetOnAxis(pick[p][:, k:k + 1], 0)).then_inc(s_pick[p], 16)

            def inverse_std(b):
                apart(pool, g["var"], b + 1)
                lk.begin(b)
                lk(nc.gpsimd.tensor_scalar(rstd[:, 0:1], agg[:, 1:2], EPS, None, ALU.add))
                nc.gpsimd.tensor_tensor(rstd[:, 1:2], rstd[:, 0:1], shared["mhalf"][:, :], ALU.pow).then_inc(g["rstd"], 1)

            def residual(b, i, p):
                pool.wait_ge(g["x2"], b + 1)
                since(pool, g["x3"], b - 1)
                nc.gpsimd.tensor_tensor(x2b[p][:, :], x2[p][:, :], bo[:, :], ALU.add).then_inc(g["x2b"], 1)

            def normalise(b, i, p, h):
                hs = slice(h * HS, (h + 1) * HS)
                pool.wait_ge(g["share"], 2 * b + h + 1)
                for s, (a, z) in enumerate(STREAMS):
                    ins = nc.gpsimd.tensor_tensor(soft[p][:, hs, a:z], soft[p][:, hs, a:z],
                                                  share[:, s, hs].unsqueeze(2).to_broadcast([P, HS, z - a]), ALU.mult)
                ins.then_inc(g["soft"], 1)

            def tails(b, i, p):
                pool.wait_ge(g["soft"], 2 * b + 2)
                since(pool, g["bandv"], b)
                for dst, m in ((near, "before_band"), (far, "behind_band")):
                    ins = nc.gpsimd.tensor_tensor(dst[:, :, :], soft[p][:, :, 0:TEXT],
                                                  cst(m).unsqueeze(1).to_broadcast([P, NH, TEXT]), ALU.mult)
                ins.then_inc(g["tails"], 1)

            def windows(b, i, p):
                apart(pool, s_relout[p], 16 * i)
                apart(pool, g["r_sb"], b + 1)
                hi = REL_LO + NREL
                nc.gpsimd.tensor_copy(relw[p][:, :, 0:REL_LO], rel[:, :, 0:1].to_broadcast([P, NH, REL_LO]))
                nc.gpsimd.tensor_copy(relw[p][:, :, REL_LO:hi], rel[:, :, :])
                ins = nc.gpsimd.tensor_copy(relw[p][:, :, hi:RELW], rel[:, :, NREL - 1:NREL].to_broadcast([P, NH, RELW - hi]))
                ins.then_inc(g["relw"], 1)

            gather(0, 0, 0)
            gather(1, 0, 1)
            inverse_std(0)
            inverse_std(1)
            residual(0, 0, 0)
            windows(0, 0, 0)

            def steps(b, i, p, first, last):
                if not beyond(b + 2):
                    gather(b + 2, i + 1, p)
                for h in range(2):
                    normalise(b, i, p, h)
                if not last:
                    windows(b + 1, i + p, 1 - p)
                if not beyond(b + 2):
                    inverse_std(b + 2)
                if not last:
                    residual(b + 1, i + p, 1 - p)
                tails(b, i, p)

            by_batch(steps)(pool)

        @block.scalar
        def _(act):
            for dst, src in W[5:]:
                act.dma_start(dst, src).then_inc(s_w, 16)
            act.wait_ge(s_w, W_READY)
            nc.scalar.activation(tanhs[:, :], alphas[:, :], ACT.Tanh).then_inc(s_setup, 1)

            def rows_sb(b, i, p):
                act.wait_ge(g["t_mm"], b + 1)
                since(act, g["vt_mm"], b - 1)
                nc.scalar.activation(tT[p][:, :, :], T[0][:, :].rearrange("p (c n) -> p c n", c=4), ACT.Copy).then_inc(g["t_sb"], 1)

            def queries(b, i, p):
                act.wait_ge(g["q_mm"], b + 1)
                since(act, g["s_mm"], 2 * (b - 1))
                nc.scalar.activation(qT[p][:, :, :], S[:, 0:HS, :], ACT.Copy, scale=SCALE1).then_inc(g["q_sb"], 1)

            def distances(b, i, p):
                act.wait_ge(g["r_mm"], b + 1)
                since(act, g["relw"], b)
                for k in range(2):
                    half = MT1 // 2
                    dst = rel[:, :, :].rearrange("p (a m) r -> p m a r", a=2)[:, k * half:(k + 1) * half]
                    ins = nc.scalar.activation(dst, T[k][:, 0:half * 2 * NREL].rearrange("p (m a r) -> p m a r", m=half, a=2), ACT.Copy)
                ins.then_inc(g["r_sb"], 1)

            def keys(b, i, p):
                act.wait_ge(g["k_mm"], b + 1)
                since(act, g["s_mm"], 2 * (b - 1))
                nc.scalar.activation(kT[p][:, :, :], S[:, HS:NH, :], ACT.Copy).then_inc(g["k_sb"], 1)

            def values(b, i, p):
                act.wait_ge(g["vt_mm"], b + 1)
                since(act, g["v_mm"], b)
                nc.scalar.activation(vT[:, :, :], S[:, 0:HS, :], ACT.Copy).then_inc(g["vt_sb"], 1)

            def exps(b, p, h):
                act.wait_ge(g["s_sub"], 2 * b + h + 1)
                hs = slice(h * HS, (h + 1) * HS)
                nc.scalar.activation(soft[p][:, hs, :], soft[p][:, hs, :], ACT.Exp).then_inc(g["s_exp"], 1)

            def probs(b, k):
                act.wait_ge(g["p_mm"], 4 * b + k + 1)
                since(act, g["pv_mm"], 4 * b + k - 1)
                nc.scalar.activation(pT[k % 2][:, :, :], T[k % 2][:, :].rearrange("p (h n) -> p h n", h=4), ACT.Copy)\
                    .then_inc(g["p_sb"], 1)

            def bands(b):
                for k in range(2):
                    act.wait_ge(g["w_mm"], b + 1)
                    since(act, g["o_mm"], b)
                    ins = nc.scalar.activation(bandT[:, 4 * k:4 * k + 4, :], T[k][0:2 * NREL, :].rearrange("p (h n) -> p h n", h=4), ACT.Copy)
                ins.then_inc(g["w_sb"], 1)

            def attended(b):
                act.wait_ge(g["o_mm"], b + 1)
                since(act, g["ot_mm"], 2 * b)
                nc.scalar.activation(att[:, :], O[:, :], ACT.Copy).then_inc(g["o_sb"], 1)
                for k in range(2):
                    act.wait_ge(g["ot_mm"], 2 * b + k + 1)
                    since(act, g["y_mm"], b)
                    nc.scalar.activation(attT[:, 4 * k:4 * k + 4, :], T[k][:, :].rearrange("p (h n) -> p h n", h=4), ACT.Copy)\
                        .then_inc(g["ot_sb"], 1)

            rows_sb(0, 0, 0)
            queries(0, 0, 0)
            distances(0, 0, 0)
            keys(0, 0, 0)
            values(0, 0, 0)

            def steps(b, i, p, first, last):
                if not first:
                    bands(b - 1)
                    attended(b - 1)
                for h in range(2):
                    exps(b, p, h)
                if not last:
                    rows_sb(b + 1, i + p, 1 - p)
                    queries(b + 1, i + p, 1 - p)
                    distances(b + 1, i + p, 1 - p)
                    keys(b + 1, i + p, 1 - p)
                    values(b + 1, i + p, 1 - p)
                for k in range(4):
                    probs(b, k)

            by_batch(steps)(act)
            bands(NB - 1)
            attended(NB - 1)

        @block.tensor
        def _(pe):
            pe.wait_ge(s_w, W_READY)

            def transposes(b, i, p):
                pe.wait_ge(g["xn"], b + 1)
                pe.wait_ge(s_in[p], 32 * (i + 1))
                since(pe, g["ot_sb"], 2 * (b - 1))
                for c in range(KD):
                    nc.tensor.transpose(T[0][:, c * P:(c + 1) * P], xn[p][:, c * P:(c + 1) * P], ident)
                for c in range(KD):
                    ins = nc.tensor.transpose(T[0][:, (KD + c) * P:(KD + c + 1) * P], c_in[p][:, c * P:(c + 1) * P], ident)
                ins.then_inc(g["t_mm"], 1)

            def queries(b, i, p):
                pe.wait_ge(g["t_sb"], b + 1)
                since(pe, g["s_sub"], 2 * (b - 1) + 1)
                for m in range(MT1):
                    for c in range(KD):
                        ins = nc.tensor.matmul(S[:, m, :], wq[:, c, m * P:(m + 1) * P], tT[p][:, c, :], start=(c == 0), stop=(c == KD - 1))
                ins.then_inc(g["q_mm"], 1)

            def distances(b, i, p):
                pe.wait_ge(g["q_sb"], b + 1)
                since(pe, g["ot_sb"], 2 * (b - 1))
                for m in range(MT1):
                    k, mm = m // (MT1 // 2), m % (MT1 // 2)
                    ins = nc.tensor.matmul(T[k][:, mm * 2 * NREL:(mm + 1) * 2 * NREL], qT[p][:, m, :], relk[:, :], start=True, stop=True)
                ins.then_inc(g["r_mm"], 1)

            def by_stream(w, at, p):
                for m in range(MT1):
                    for s, (a, z) in enumerate(STREAMS):
                        for c in range(KD):
                            ins = nc.tensor.matmul(S[:, at + m, a:z], w[s][:, c, m * P:(m + 1) * P], tT[p][:, KD + c, a:z],
                                                   start=(c == 0), stop=(c == KD - 1))
                return ins

            def keys(b, i, p):
                since(pe, g["s_sub"], 2 * b)
                by_stream(wk, HS, p).then_inc(g["k_mm"], 1)

            def values(b, i, p):
                pe.wait_ge(g["q_sb"], b + 1)
                by_stream(wv, 0, p).then_inc(g["vt_mm"], 1)
                pe.wait_ge(g["vt_sb"], b + 1)
                pe.wait_ge(g["k_sb"], b + 1)
                for m in range(MT1):
                    ins = nc.tensor.transpose(S[:, HS + m, :], vT[:, m, :], ident)
                ins.then_inc(g["v_mm"], 1)

            def scores(b, i, p):
                pe.wait_ge(g["q_sb"], b + 1)
                pe.wait_ge(g["k_sb"], b + 1)
                pe.wait_ge(g["vt_sb"], b + 1)
                pe.wait_ge(g["v_sb"], b + 1)
                for half in range(2):
                    r = slice(half * DH1, (half + 1) * DH1)
                    for m in range(MT1):
                        ins = nc.tensor.matmul(S[:, half * HS + m, :], qT[p][r, m, :], kT[p][r, m, :], start=True, stop=True)
                    ins.then_inc(g["s_mm"], 1)

            def attend(b, i, p, k, last):
                half, bank = k // 2, k % 2
                pe.wait_ge(g["soft"], 2 * b + half + 1)
                if k < 2:
                    since(pe, g["ot_sb"], 2 * b)
                    if not last:
                        pe.wait_ge(g["r_sb"], b + 2)
                else:
                    pe.wait_ge(g["p_sb"], 4 * b + k - 1)
                for j in range(4):
                    ins = nc.tensor.transpose(T[k % 2][:, j * P:(j + 1) * P], soft[p][:, 4 * k + j, :], ident)
                ins.then_inc(g["p_mm"], 1)
                pe.wait_ge(g["p_sb"], 4 * b + k + 1)
                if k == 0:
                    pe.wait_ge(g["v_sb"], b + 1)
                    since(pe, g["x3"], b)
                for j in range(4):
                    head = 2 * (4 * bank + j) + half
                    ins = nc.tensor.matmul(O[:, head * DH1:(head + 1) * DH1], pT[k % 2][:, j, :], v[p][:, head * DH1:(head + 1) * DH1],
                                           start=(half == 0 and j == 0), stop=False, skip_group_check=True)
                ins.then_inc(g["pv_mm"], 1)

            def finish(b, i, p):
                pe.wait_ge(g["bandv"], b + 1)
                pe.wait_ge(s_pin[p], 16 * (i + 1))
                pe.wait_ge(g["p_sb"], 4 * b + 4)
                for k in range(NH // 2):
                    ins = nc.tensor.transpose(T[k // 4][0:2 * NREL, (k % 4) * P:(k % 4 + 1) * P],
                                              band[p][:, 2 * k:2 * k + 2, :].rearrange("p h r -> p (h r)"), ident)
                ins.then_inc(g["w_mm"], 1)
                pe.wait_ge(g["w_sb"], b + 1)
                o = O[:, :].rearrange("p (m u a d) -> p m u a d", m=4, u=2, a=2)
                for k in range(NH // 2):
                    half, m = k // 4, k % 4
                    ins = nc.tensor.matmul(o[:, m, :, half, :], bandT[:, k, :], relv[:, :],
                                           start=False, stop=(half == 1 and m % 2 == 1), skip_group_check=True)
                ins.then_inc(g["o_mm"], 1)
                pe.wait_ge(g["o_sb"], b + 1)
                for k in range(2):
                    for j in range(4):
                        m = 4 * k + j
                        ins = nc.tensor.transpose(T[k][:, j * P:(j + 1) * P], att[:, m * P:(m + 1) * P], ident)
                    ins.then_inc(g["ot_mm"], 1)
                pe.wait_ge(g["ot_sb"], 2 * b + 2)
                for m in range(MT1):
                    ins = nc.tensor.matmul(O[:, 0:D], attT[:, m, :], wo[:, m, :], start=(m == 0), stop=(m == MT1 - 1))
                ins.then_inc(g["y_mm"], 1)

            def project(b, i, p):
                transposes(b, i, p)
                queries(b, i, p)
                distances(b, i, p)
                keys(b, i, p)
                values(b, i, p)

            project(0, 0, 0)

            def steps(b, i, p, first, last):
                scores(b, i, p)
                if not first:
                    finish(b - 1, i - 1 + p, 1 - p)
                if not last:
                    project(b + 1, i + p, 1 - p)
                for k in range(4):
                    attend(b, i, p, k, last)

            by_batch(steps)(pe)
            finish(NB - 1, NB // 2 - 1, 1)

        @block.vector
        def _(dve):
            dve.wait_ge(s_setup, 1)
            nc.vector.memset(coef[:, 0, :], 1.0).then_inc(s_alpha, 1)
            for s in range(1, NS):
                nc.vector.tensor_scalar(coef[:, s, :], tanhs[:, s - 1:s].to_broadcast([P, NH]), 1.0, None, ALU.add).then_inc(s_alpha, 1)
            dve.wait_ge(s_alpha, NS)
            front = Link(dve, l_front, 2)
            soft_l = [Link(dve, l, 2) for l in l_softs]
            sum_l = Link(dve, l_sum, 2)

            def pick_rows(b, i, p):
                since(dve, s_pick[p], 32 * i)
                nc.vector.tensor_copy(pick[p][:, :], shared["tile_rows"][:, bass.ds(b, 1), :].rearrange("p o k -> p (o k)"))\
                    .then_inc(g["pick"], 1)

            def rows(b, i, p):
                front.begin(b)
                dve.wait_ge(s_in[p], 32 * (i + 1))
                dve.wait_ge(s_pick[p], 32 * (i + 1))
                w = [shared["weights"][:, bass.ds(b, 1), k:k + 1].rearrange("p o k -> p (o k)") for k in range(TOPK)]
                front(nc.vector.scalar_tensor_tensor(x_in[p][:, :], picked[p][0][:, :], w[0], x_in[p][:, :], ALU.mult, ALU.add))
                since(dve, g["x2b"], b - 1)
                nc.vector.scalar_tensor_tensor(x2[p][:, :], picked[p][1][:, :], w[1], x_in[p][:, :], ALU.mult, ALU.add)\
                    .then_inc(g["x2"], 1)
                dve.wait_ge(g["x2"], b + 1)
                front(nc.vector.bn_stats(stat[:, :], x2[p][:, :]))
                front.end()
                since(dve, g["xn"], b)
                nc.vector.bn_aggr(agg[:, :], stat[:, :]).then_inc(g["var"], 1)

            def rows_normal(b, i, p):
                dve.wait_ge(g["rstd"], b + 1)
                since(dve, g["t_mm"], b - 1)
                nc.vector.tensor_scalar(xn[p][:, :], x2[p][:, :], agg[:, 0:1], rstd[:, 1:2], ALU.subtract, ALU.mult)\
                    .then_inc(g["xn"], 1)

            def less_max(b, i, p, h):
                lk = soft_l[h]
                lk.begin(b)
                hs = slice(h * HS, (h + 1) * HS)
                dve.wait_ge(g["s_mm"], 2 * b + h + 1)
                dve.wait_ge(s_relin[p], 16 * (i + 1))
                since(dve, g["p_mm"], 4 * (b - 1))
                since(dve, s_pout[p], 16 * i)
                since(dve, g["tails"], b - 1)
                a, z = STREAMS[0]
                lk(nc.vector.tensor_tensor(soft[p][:, hs, a:z], S[:, hs, a:z], bias[p][:, hs, :], ALU.add))
                nc.vector.tensor_reduce(top[:, 0, hs], soft[p][:, hs, a:z], X, ALU.max)
                for s, (a, z) in list(enumerate(STREAMS))[1:]:
                    ins = nc.vector.tensor_reduce(top[:, s, hs], S[:, hs, a:z], X, ALU.max)
                lk(ins)
                for s, (a, z) in enumerate(STREAMS):
                    src = S if s else soft[p]
                    ins = nc.vector.tensor_tensor(soft[p][:, hs, a:z], src[:, hs, a:z],
                                                  top[:, s, hs].unsqueeze(2).to_broadcast([P, HS, z - a]), ALU.subtract)
                lk.end()
                ins.then_inc(g["s_sub"], 1)

            def shares(b, i, p, h):
                hs = slice(h * HS, (h + 1) * HS)
                if h == 0:
                    sum_l.begin(2 * b)
                else:
                    sum_l.begin(2 * b + 1)
                dve.wait_ge(g["s_exp"], 2 * b + h + 1)
                for s, (a, z) in enumerate(STREAMS):
                    ins = nc.vector.tensor_reduce(total[:, s, hs], soft[p][:, hs, a:z], X, ALU.add)
                sum_l(ins)
                since(dve, g["soft"], 2 * b + h - 1)
                sum_l(nc.vector.reciprocal(share[:, :, hs], total[:, :, hs]))
                nc.vector.tensor_tensor(share[:, :, hs], share[:, :, hs], coef[:, :, hs], ALU.mult).then_inc(g["share"], 1)
                sum_l.end()

            def ends(b, i, p):
                dve.wait_ge(g["tails"], b + 1)
                since(dve, g["w_mm"], b - 1)
                nc.vector.tensor_reduce(band[p][:, :, 0], near[:, :, :], X, ALU.add)
                nc.vector.tensor_reduce(band[p][:, :, NREL - 1], far[:, :, :], X, ALU.add).then_inc(g["bandv"], 1)

            def output(b, i, p):
                dve.wait_ge(g["y_mm"], b + 1)
                dve.wait_ge(g["x2b"], b + 1)
                since(dve, s_x3[p], 16 * i)
                nc.vector.tensor_tensor(x3[p][:, :], O[:, 0:D], x2b[p][:, :], ALU.add).then_inc(g["x3"], 1)

            pick_rows(0, 0, 0)
            pick_rows(1, 0, 1)
            for b in range(2):
                rows(b, 0, b)
                rows_normal(b, 0, b)

            def values(b, i, p):
                dve.wait_ge(g["v_mm"], b + 1)
                since(dve, g["pv_mm"], 4 * (b - 1))
                nc.vector.tensor_copy(v[p][:, :], S[:, HS:NH, :].rearrange("p m n -> p (m n)")).then_inc(g["v_sb"], 1)

            values(0, 0, 0)

            def steps(b, i, p, first, last):
                if not beyond(b + 2):
                    pick_rows(b + 2, i + 1, p)
                for h in range(2):
                    less_max(b, i, p, h)
                for h in range(2):
                    shares(b, i, p, h)
                if not first:
                    output(b - 1, i - 1 + p, 1 - p)
                if not last:
                    values(b + 1, i + p, 1 - p)
                if not beyond(b + 2):
                    rows(b + 2, i + 1, p)
                    rows_normal(b + 2, i + 1, p)
                ends(b, i, p)

            by_batch(steps)(dve)
            output(NB - 1, NB // 2 - 1, 1)


HID = 1024
MH = HID // P
W_N = D * HID
LEVELS = 127.0
FLOOR = 1e-5
ROUND = 1.5 * 2.0 ** 23


def feed_forward(nc, t, shared, out):
    with ExitStack() as ctx:
        def sb(name, shape, dt=F32):
            return ctx.enter_context(nc.sbuf_tensor(name, shape, dt))

        def ps(name, shape, dt=F32):
            return ctx.enter_context(nc.psum_tensor(name, shape, dt))

        def sem(name):
            shared["semaphores"].append(nc.alloc_semaphore(name=name))
            return shared["semaphores"][-1]

        const = shared["const"]

        def cst(name):
            a, z = CONST_AT[name]
            return const[:, a:z]

        ident, ones = cst("ident"), cst("ones")
        two = range(2)
        wf = [sb(f"d_wf{k}", [P, W_N // P]) for k in two]
        wi = [sb(f"d_wi{k}", [P, W_N // P], BF16) for k in two]
        w1, w2 = wi[0][:, :].rearrange("p (k n) -> p k n", k=KD), wi[1][:, :].rearrange("p (k n) -> p k n", k=MH)
        ident_b = sb("d_ident", [P, P], BF16)
        taps = sb("d_taps", [P, MH, 3])
        cbias = sb("d_cbias", [P, MH])
        wsum = sb("d_wsum", [P, 2])
        wunit = sb("d_wunit", [P, 2])
        wscale = sb("d_wscale", [P, 2])
        x_in = [sb(f"d_x{p}", [P, D]) for p in two]
        stat = sb("d_stat", [P, 6])
        agg = sb("d_agg", [P, 2])
        rstd = sb("d_rstd", [P, 2])
        xn = sb("d_xn", [P, D])
        peak = sb("d_peak", [P, 4])
        unit = sb("d_unit", [P, 2])
        rnd = sb("d_rnd", [P, D])
        xi = [sb(f"d_xi{p}", [P, D], BF16) for p in two]
        diag = [sb(f"d_diag{k}", [P, P]) for k in two]
        xiT = sb("d_xiT", [P, KD, P], BF16)
        row = [sb(f"d_row{k}", [P, P]) for k in two]
        hp = [sb(f"d_hp{p}", [P, MH, P + 2]) for p in two]
        conv = [sb(f"d_conv{p}", [P, MH, P]) for p in two]
        gi = sb("d_gi", [P, MH, P], BF16)
        step = sb("d_step", [P, 1])
        res = [sb(f"d_res{p}", [P, D]) for p in two]
        XT = ps("d_XT", [P, KD, P], BF16)
        H = ps("d_H", [P, MH, P])
        B = ps("d_B", [P, 2 * P])
        GT = ps("d_GT", [P, HID])
        Y = ps("d_Y", [P, D])

        s_w = sem("d_weights")
        s_pad = sem("d_pad")
        s_id = sem("d_id")
        s_tot = sem("d_tot")
        s_wi = sem("d_wi")
        l_w, l_front, l_conv, l_q = (sem("dl_" + n) for n in "weights front conv quant".split())
        l_pool = sem("dl_pool")
        s_in = [sem(f"d_in{p}") for p in two]
        s_out = [sem(f"d_out{p}") for p in two]
        names = "var rstd xn xi xt_mm xt_sb row_mm row_sb h_mm h tap conv silu gt_mm peak2 diag2 row2_mm row2_sb gi y_mm y"
        g = {n: sem("d_" + n) for n in names.split()}

        W = [(wf[0][:, :].rearrange("p (k n) -> p k n", k=KD), t["L1_w1T"].rearrange("(k p) n -> p k n", p=P)),
             (wf[1][:, :].rearrange("p (k n) -> p k n", k=MH), t["L1_w2T"].rearrange("(k p) n -> p k n", p=P)),
             (taps[:, :, :], t["L1_conv_w"].rearrange("(m p) k -> p m k", p=P)),
             (cbias[:, :], t["L1_conv_b"])]
        W_READY = 16 * len(W)

        def by_batch(steps):
            def run(eng):
                for b in range(2):
                    steps(b, 0, b, b == 0, False)
                with eng.Fori(1, NB // 2 - 1) as i:
                    for p in range(2):
                        steps(i * 2 + p, i, p, False, False)
                for p in range(2):
                    steps(NB - 2 + p, NB // 2 - 1, p, False, p == 1)
            return run

        def rows_of(d, b):
            return d[bass.ds(b, 1)].rearrange("o p d -> (o p) d")

        block = ctx.enter_context(nc.Block())

        @block.sync
        def _(sp):
            def load(b, i, p):
                since(sp, g["y"], b - 1)
                sp.dma_start(x_in[p][:, :], rows_of(t["x3"], b)).then_inc(s_in[p], 16)

            def store(b, p):
                sp.wait_ge(g["y"], b + 1)
                sp.dma_start(rows_of(out, b), res[p][:, :]).then_inc(s_out[p], 16)

            load(0, 0, 0)
            load(1, 0, 1)

            def steps(b, i, p, first, last):
                store(b, p)
                if not (isinstance(b, int) and b + 2 >= NB):
                    load(b + 2, i + 1, p)

            by_batch(steps)(sp)
            for p in two:
                sp.wait_ge(s_out[p], 16 * (NB // 2))

        @block.gpsimd
        def _(pool):
            for p in two:
                nc.gpsimd.memset(hp[p][:, :, 0:1], 0.0).then_inc(s_pad, 1)
                nc.gpsimd.memset(hp[p][:, :, P + 1:P + 2], 0.0).then_inc(s_pad, 1)
            nc.gpsimd.tensor_copy(ident_b[:, :], ident).then_inc(s_id, 1)
            lk = Link(pool, l_pool, 1)

            def inverse_std(b):
                apart(pool, g["var"], b + 1)
                lk.begin(b)
                lk(nc.gpsimd.tensor_scalar(rstd[:, 0:1], agg[:, 1:2], EPS, None, ALU.add))
                nc.gpsimd.tensor_tensor(rstd[:, 1:2], rstd[:, 0:1], shared["mhalf"][:, :], ALU.pow).then_inc(g["rstd"], 1)

            by_batch(lambda b, *_: inverse_std(b))(pool)

        @block.scalar
        def _(act):
            for dst, src in W:
                act.dma_start(dst, src).then_inc(s_w, 16)
            act.wait_ge(s_w, W_READY)

            def front(b):
                act.wait_ge(g["xt_mm"], b + 1)
                since(act, g["h_mm"], b)
                nc.scalar.activation(xiT[:, :, :], XT[:, :, :], ACT.Copy).then_inc(g["xt_sb"], 1)
                act.wait_ge(g["row_mm"], b + 1)
                since(act, g["h"], b)
                nc.scalar.activation(row[0][:, :], B[:, 0:P], ACT.Copy).then_inc(g["row_sb"], 1)

            def middle_tap(b, p):
                act.wait_ge(g["h"], b + 1)
                since(act, g["gt_mm"], b - 1)
                since(act, g["gi"], b - 1)
                for m in range(MH):
                    ins = nc.scalar.activation(conv[p][:, m, :], hp[p][:, m, 1:P + 1], ACT.Identity,
                                               bias=cbias[:, m:m + 1], scale=taps[:, m, 1:2])
                ins.then_inc(g["tap"], 1)

            def activate(b, p):
                act.wait_ge(g["conv"], b + 1)
                nc.scalar.activation(conv[p][:, :, :], conv[p][:, :, :], ACT.Silu).then_inc(g["silu"], 1)

            def second(b):
                act.wait_ge(g["row2_mm"], b + 1)
                since(act, g["gi"], b)
                nc.scalar.activation(row[1][:, :], B[:, P:2 * P], ACT.Copy).then_inc(g["row2_sb"], 1)

            front(0)
            middle_tap(0, 0)

            def steps(b, i, p, first, last):
                activate(b, p)
                if not last:
                    front(b + 1)
                second(b)
                if not last:
                    middle_tap(b + 1, 1 - p)

            by_batch(steps)(act)

        @block.tensor
        def _(pe):
            pe.wait_ge(s_id, 1)
            pe.wait_ge(l_w, 2)
            nc.tensor.matmul(Y[:, 0:2], ones, wsum[:, :], start=True, stop=True).then_inc(s_tot, 1)
            pe.wait_ge(s_wi, 2)

            def front(b, i, p):
                pe.wait_ge(g["xi"], b + 1)
                since(pe, g["xt_sb"], b)
                for c in range(KD):
                    ins = nc.tensor.transpose(XT[:, c, :], xi[p][:, c * P:(c + 1) * P], ident_b[:, :])
                ins.then_inc(g["xt_mm"], 1)
                since(pe, g["row2_sb"], b - 1)
                nc.tensor.matmul(B[:, 0:P], ones, diag[0][:, :], start=True, stop=True).then_inc(g["row_mm"], 1)
                pe.wait_ge(g["xt_sb"], b + 1)
                since(pe, g["h"], b)
                for m in range(MH):
                    for c in range(KD):
                        ins = nc.tensor.matmul(H[:, m, :], w1[:, c, m * P:(m + 1) * P], xiT[:, c, :], start=(c == 0), stop=(c == KD - 1))
                ins.then_inc(g["h_mm"], 1)

            front(0, 0, 0)

            def steps(b, i, p, first, last):
                pe.wait_ge(g["silu"], b + 1)
                since(pe, g["peak2"], b)
                for m in range(MH):
                    ins = nc.tensor.transpose(GT[:, m * P:(m + 1) * P], conv[p][:, m, :], ident)
                ins.then_inc(g["gt_mm"], 1)
                if not last:
                    front(b + 1, i + p, 1 - p)
                pe.wait_ge(g["diag2"], b + 1)
                if not last:
                    pe.wait_ge(g["row_sb"], b + 2)
                nc.tensor.matmul(B[:, P:2 * P], ones, diag[1][:, :], start=True, stop=True).then_inc(g["row2_mm"], 1)
                pe.wait_ge(g["gi"], b + 1)
                since(pe, g["y"], b)
                for m in range(MH):
                    ins = nc.tensor.matmul(Y[:, :], gi[:, m, :], w2[:, m, :], start=(m == 0), stop=(m == MH - 1))
                ins.then_inc(g["y_mm"], 1)

            by_batch(steps)(pe)

        @block.vector
        def _(dve):
            dve.wait_ge(s_w, W_READY)
            wl = Link(dve, l_w, 8)
            for k in two:
                wl(nc.vector.tensor_reduce(wsum[:, k:k + 1], wf[k][:, :], X, ALU.add, apply_absolute_value=True))
            dve.wait_ge(s_tot, 1)
            wl(nc.vector.tensor_scalar(wunit[:, :], Y[:, 0:2], 1.0 / W_N, FLOOR, ALU.mult, ALU.max))
            wl(nc.vector.reciprocal(wscale[:, :], wunit[:, :]))
            for k in two:
                wl(nc.vector.tensor_scalar(wf[k][:, :], wf[k][:, :], wscale[:, k:k + 1], ROUND, ALU.mult, ALU.add))
                wl(nc.vector.tensor_scalar(wf[k][:, :], wf[k][:, :], -ROUND, -1.0, ALU.add, ALU.max))
                nc.vector.tensor_scalar(wi[k][:, :], wf[k][:, :], 1.0, None, ALU.min).then_inc(s_wi, 1)
            dve.wait_ge(s_wi, 2)
            front_l, conv_l, quant_l = Link(dve, l_front, 7), Link(dve, l_conv, 1), Link(dve, l_q, 5)

            def front(b, i, p):
                front_l.begin(b)
                dve.wait_ge(s_in[p], 16 * (i + 1))
                front_l(nc.vector.bn_stats(stat[:, :], x_in[p][:, :]))
                nc.vector.bn_aggr(agg[:, :], stat[:, :]).then_inc(g["var"], 1)
                dve.wait_ge(g["rstd"], b + 1)
                front_l(nc.vector.tensor_scalar(xn[:, :], x_in[p][:, :], agg[:, 0:1], rstd[:, 1:2], ALU.subtract, ALU.mult))
                front_l(nc.vector.tensor_reduce(peak[:, 0:1], xn[:, :], X, ALU.max, apply_absolute_value=True))
                front_l(nc.vector.tensor_scalar(unit[:, 0:1], peak[:, 0:1], FLOOR, 1.0 / LEVELS, ALU.max, ALU.mult))
                front_l(nc.vector.reciprocal(peak[:, 1:2], unit[:, 0:1]))
                front_l(nc.vector.tensor_scalar(rnd[:, :], xn[:, :], peak[:, 1:2], LEVELS, ALU.mult, ALU.min))
                front_l(nc.vector.tensor_scalar(rnd[:, :], rnd[:, :], -LEVELS - 1.0, ROUND, ALU.max, ALU.add))
                front_l.end()
                since(dve, g["xt_mm"], b - 1)
                nc.vector.tensor_scalar(xi[p][:, :], rnd[:, :], -ROUND, None, ALU.add)
                since(dve, g["row_mm"], b)
                nc.vector.tensor_scalar(diag[0][:, :], ident, unit[:, 0:1], wunit[:, 0:1], ALU.mult, ALU.mult).then_inc(g["xi"], 1)

            def hidden(b, i, p):
                dve.wait_ge(g["h_mm"], b + 1)
                dve.wait_ge(g["row_sb"], b + 1)
                if isinstance(b, int) and b < 2:
                    dve.wait_ge(s_pad, 4)
                nc.vector.tensor_tensor(hp[p][:, :, 1:P + 1], H[:, :, :], row[0][:, :].unsqueeze(1).to_broadcast([P, MH, P]), ALU.mult)\
                    .then_inc(g["h"], 1)

            def convolve(b, i, p):
                conv_l.begin(b)
                dve.wait_ge(g["tap"], b + 1)
                dve.wait_ge(g["h"], b + 1)
                for k in (0, 2):
                    for m in range(MH):
                        ins = nc.vector.scalar_tensor_tensor(conv[p][:, m, :], hp[p][:, m, k:k + P], taps[:, m, k:k + 1],
                                                             conv[p][:, m, :], ALU.mult, ALU.add)
                    if k == 0:
                        conv_l(ins)
                ins.then_inc(g["conv"], 1)

            def quantise(b, i, p):
                quant_l.begin(b)
                dve.wait_ge(g["gt_mm"], b + 1)
                nc.vector.tensor_reduce(peak[:, 2:3], GT[:, :], X, ALU.max, apply_absolute_value=True).then_inc(g["peak2"], 1)
                dve.wait_ge(g["peak2"], b + 1)
                quant_l(nc.vector.tensor_scalar(unit[:, 1:2], peak[:, 2:3], FLOOR, 1.0 / LEVELS, ALU.max, ALU.mult))
                quant_l(nc.vector.reciprocal(peak[:, 3:4], unit[:, 1:2]))
                since(dve, g["row2_mm"], b)
                nc.vector.tensor_scalar(diag[1][:, :], ident, peak[:, 3:4], None, ALU.mult).then_inc(g["diag2"], 1)
                quant_l(nc.vector.tensor_scalar(step[:, :], unit[:, 1:2], wunit[:, 1:2], None, ALU.mult))
                dve.wait_ge(g["row2_sb"], b + 1)
                quant_l(nc.vector.tensor_tensor(conv[p][:, :, :], conv[p][:, :, :], row[1][:, :].unsqueeze(1).to_broadcast([P, MH, P]), ALU.mult))
                quant_l(nc.vector.tensor_scalar(conv[p][:, :, :], conv[p][:, :, :], LEVELS, -LEVELS - 1.0, ALU.min, ALU.max))
                quant_l.end()
                since(dve, g["y_mm"], b)
                nc.vector.tensor_scalar(gi[:, :, :], conv[p][:, :, :], ROUND, -ROUND, ALU.add, ALU.add).then_inc(g["gi"], 1)

            def output(b, i, p):
                dve.wait_ge(g["y_mm"], b + 1)
                since(dve, s_out[p], 16 * i)
                nc.vector.scalar_tensor_tensor(res[p][:, :], Y[:, :], step[:, 0:1], x_in[p][:, :], ALU.mult, ALU.add)\
                    .then_inc(g["y"], 1)

            front(0, 0, 0)
            hidden(0, 0, 0)
            convolve(0, 0, 0)
            front(1, 0, 1)

            def steps(b, i, p, first, last):
                quantise(b, i, p)
                if not last:
                    hidden(b + 1, i + p, 1 - p)
                    convolve(b + 1, i + p, 1 - p)
                output(b, i, p)
                if not (isinstance(b, int) and b + 2 >= NB):
                    front(b + 2, i + 1, p)

            by_batch(steps)(dve)


def layer1(nc, t, shared, out):
    attention1(nc, t, shared)
    feed_forward(nc, t, shared, out)


def release_semaphores(nc, shared):
    nc.clear_and_free_semaphores(shared["semaphores"])
    nc.all_engine_barrier()
    shared["semaphores"] = []


def build(nc, t, out, phases="ABC"):
    with ExitStack() as ctx:
        def sb(name, shape, dt=F32):
            return ctx.enter_context(nc.sbuf_tensor(name, shape, dt))

        shared = {
            "const": sb("const", [P, CONST_W]),
            "mhalf": sb("mhalf", [P, 1]),
            "onehot": sb("onehot", [P, NB, TOPK, NE]),
            "slots": sb("slots", [P, NB, TOPK]),
            "weights": sb("weights", [P, NB, TOPK]),
            "tile_rows": sb("tile_rows", [P, NB, TOPK], I32),
            "tile_expert": sb("tile_expert", [P, N_TILES], I32),
            "tile_row": sb("tile_row", [P, N_TILES], I32),
            "semaphores": [],
            "s_experts": ctx.enter_context(nc.semaphore("s_experts")),
        }
        t["lists"] = nc.dram_tensor("expert_lists", (NE * ROWS_E, D), F32, kind="Internal").ap()
        t["expert_out"] = nc.dram_tensor("expert_out", (N_TILES * P, D), F32, kind="Internal").ap()
        t["x1"] = nc.dram_tensor("rows_after_attention", (NB, P, D), F32, kind="Internal").ap()
        t["x3"] = nc.dram_tensor("rows_after_attention_1", (NB, P, D), F32, kind="Internal").ap()
        with ExitStack() as moe:
            for name, shape in (("w1", [P, NE, KD, 2 * HE]), ("w2", [P, NE, KH, D]), ("b1", [P, NE, 2 * HE]), ("b2", [P, NE, D])):
                shared[name] = moe.enter_context(nc.sbuf_tensor("moe_" + name, shape, F32))

            def load_experts(eng):
                s = shared["s_experts"]
                eng.dma_start(shared["b1"][:, :, :], t["L0_bl1"].partition_broadcast(P)).then_inc(s, 16)
                eng.dma_start(shared["b2"][:, :, :], t["L0_bl2"].partition_broadcast(P)).then_inc(s, 16)
                eng.dma_start(shared["w1"][:, :, :, :], t["L0_Wl1"].rearrange("e (k p) n -> p e k n", p=P)).then_inc(s, 16)
                eng.dma_start(shared["w2"][:, :, :, :], t["L0_Wl2"].rearrange("e (k p) n -> p e k n", p=P)).then_inc(s, 16)

            shared["load_experts"] = load_experts
            layer0(nc, t, shared)
            release_semaphores(nc, shared)
            experts(nc, t, shared)
        layer1(nc, t, shared, out)


def strip_columns(w):
    a = np.zeros((w.shape[1], NH, STRIP), w.dtype)
    a[:, :, :DH0] = w.T.reshape(w.shape[1], NH, DH0)
    return a.reshape(w.shape[1], NH * STRIP)


def strip_bias(b, mask_row):
    a = np.zeros((NH, STRIP), b.dtype)
    a[:, :DH0] = b.reshape(NH, DH0)
    a[:, DH0] = mask_row
    return np.ascontiguousarray(a.reshape(MT0, P).T)


def pair_blocks(a):
    r, c = a.shape
    z = np.zeros((2 * r, 2 * c), a.dtype)
    z[:r, :c] = a
    z[r:, c:] = a
    return z


def layout1(L1_xattn_Wq, L1_xattn_Wk, L1_xattn_Wv, L1_xattn_Wk_ip, L1_xattn_Wv_ip, L1_xattn_Wk_ap, L1_xattn_Wv_ap, L1_xattn_Wo,
            L1_xattn_bo, L1_xattn_rel_k, L1_xattn_rel_v, L1_xattn_alpha, L1_xattn_beta, L1_ffn_w1, L1_ffn_conv_w, L1_ffn_conv_b,
            L1_ffn_w2):
    return {
        "L1_Wq": L1_xattn_Wq, "L1_Wk0": L1_xattn_Wk, "L1_Wk1": L1_xattn_Wk_ip, "L1_Wk2": L1_xattn_Wk_ap,
        "L1_Wv0": L1_xattn_Wv, "L1_Wv1": L1_xattn_Wv_ip, "L1_Wv2": L1_xattn_Wv_ap, "L1_Wo": L1_xattn_Wo, "L1_bo": L1_xattn_bo,
        "L1_relk": pair_blocks(L1_xattn_rel_k.T), "L1_relv": pair_blocks(L1_xattn_rel_v),
        "L1_alphas": np.stack([L1_xattn_alpha, L1_xattn_beta]),
        "L1_w1T": L1_ffn_w1.T, "L1_w2T": L1_ffn_w2.T, "L1_conv_w": L1_ffn_conv_w.reshape(HID, 3),
        "L1_conv_b": L1_ffn_conv_b.reshape(MH, P).T,
    }


def layout(x, ctx_1024, mask_Bx1x1xS2_ik0, L0_xattn_Wq, L0_xattn_bq, L0_xattn_Wk, L0_xattn_bk, L0_xattn_Wv, L0_xattn_bv,
           L0_xattn_gamma, L0_xattn_beta, L0_ffn_Wr, L0_ffn_br, L0_ffn_Wl1, L0_ffn_bl1, L0_ffn_Wl2, L0_ffn_bl2,
           L0_ffn_biases_N, **layer1_inputs):
    c = np.ascontiguousarray
    arrays = {
        "x": x, "ctx": ctx_1024, "mask": mask_Bx1x1xS2_ik0.reshape(NB, P),
        "L0_wqT": strip_columns(L0_xattn_Wq), "L0_wkT": strip_columns(L0_xattn_Wk), "L0_wvT": c(L0_xattn_Wv.T),
        "L0_wrT": c(L0_ffn_Wr.T),
        "L0_bq": strip_bias(L0_xattn_bq, 1.0 / SCALE0), "L0_bk": strip_bias(L0_xattn_bk, MASKED), "L0_bv": L0_xattn_bv,
        "L0_gamma": L0_xattn_gamma, "L0_beta": L0_xattn_beta, "L0_br": L0_ffn_br, "L0_pick_bias": L0_ffn_biases_N,
        "L0_Wl1": L0_ffn_Wl1, "L0_bl1": L0_ffn_bl1, "L0_Wl2": L0_ffn_Wl2, "L0_bl2": L0_ffn_bl2,
        "const": np.concatenate(list(CONST.values()), axis=1),
    }
    arrays.update(layout1(**layer1_inputs))
    return {n: c(a) for n, a in arrays.items()}


def kernel(**inputs):
    import concourse.bacc as bacc
    from concourse.bass_utils import run_bass_kernel_spmd

    nc = bacc.Bacc("TRN2", target_bir_lowering=False, num_devices=1)
    arrays = layout(**{n: np.asarray(a) for n, a in inputs.items()})
    t = {n: nc.dram_tensor("in_" + n, a.shape, mybir.dt.from_np(a.dtype), kind="ExternalInput").ap() for n, a in arrays.items()}
    out = nc.dram_tensor("out", (NB, P, D), F32, kind="ExternalOutput").ap()
    build(nc, t, out)
    result = run_bass_kernel_spmd(nc, [{"in_" + n: a for n, a in arrays.items()}], core_ids=[0])
    return result.results[0]["out"]
```

```python
from contextlib import ExitStack

import numpy as np

import concourse.bass as bass
from concourse import mybir

F32 = mybir.dt.float32
BF16 = mybir.dt.bfloat16
I32 = mybir.dt.int32
U32 = mybir.dt.uint32
ALU = mybir.AluOpType
ACT = mybir.ActivationFunctionType
X = mybir.AxisListType.X

P = 128
NB = 16
D = 256
KD = D // P
NH = 16

DH0 = D // NH
STRIP = 32
HPT = P // STRIP
MT0 = NH // HPT
SCALE0 = 1.0 / DH0 ** 0.5
MASKED = -1.0e9
EPS0 = 1e-6
EPS = 1e-5

TEXT, IMG = 77, 16
MAXREL = 16

NE = 8
TOPK = 2
HE = 512
KH = HE // P
ROWS_E = NB * P + P
N_TILES = (NB * P * TOPK + NE * (P - 1)) // P


class Link:

    def __init__(self, eng, sem, per):
        self.eng, self.sem, self.per, self.n, self.base = eng, sem, per, 0, 0

    def begin(self, b):
        self.base, self.n = b * self.per, 0

    def __call__(self, ins):
        ins.then_inc(self.sem, 1)
        self.n += 1
        assert self.n <= self.per, self.n
        apart(self.eng, self.sem, self.base + self.n)

    def end(self):
        assert self.n == self.per, (self.n, self.per)


def since(eng, sem, count):
    if isinstance(count, int) and count <= 0:
        return
    eng.wait_ge(sem, count)


def apart(eng, sem, count):
    if not isinstance(count, int):
        count = eng.to_reg(count)
        eng.wait_ge(sem, 1)
    since(eng, sem, count)


def constants():
    c = {}
    c["ident"] = np.eye(P, dtype=np.float32)
    c["before"] = np.triu(np.ones((P, P), np.float32), 1)
    c["ones"] = np.ones((P, P), np.float32)
    aug = np.zeros((P, 1), np.float32)
    aug[DH0::STRIP] = 1.0
    c["aug"] = aug
    e = np.arange(NE, dtype=np.float32)
    c["expert"] = np.tile(e, (P, 1))
    c["list"] = np.tile(e * ROWS_E, (P, 1))
    c["sizes"] = np.tile(np.arange(NB, dtype=np.float32) * P, (P, 1))
    c["upto"] = np.tile((e[None, :] <= e[:, None]).astype(np.float32).reshape(1, -1), (P, 1))
    c["tiles"] = np.tile(np.arange(N_TILES, dtype=np.float32), (P, 1))
    i, j = np.arange(P)[:, None], np.arange(TEXT)[None, :]
    c["before_band"] = (j - i <= -MAXREL).astype(np.float32)
    c["behind_band"] = (j - i >= MAXREL).astype(np.float32)
    return c


CONST = constants()
CONST_AT = {}
_at = 0
for _name, _a in CONST.items():
    CONST_AT[_name] = (_at, _at + _a.shape[1])
    _at += _a.shape[1]
CONST_W = _at


def layer0(nc, t, shared):
    with ExitStack() as ctx:
        early, used = shared["early"], [0]

        def sb(name, shape, dt=F32):
            n = int(np.prod(shape[1:]))
            if dt != F32 or used[0] + n > early.shape[1]:
                return ctx.enter_context(nc.sbuf_tensor(name, shape, dt))
            a = early[:, used[0]:used[0] + n]
            used[0] += n
            if len(shape) == 3:
                a = a.rearrange("p (a b) -> p a b", a=shape[1])
            if len(shape) == 4:
                a = a.rearrange("p (a b c) -> p a b c", a=shape[1], b=shape[2])
            return a

        def ps(name, shape, dt=F32):
            return ctx.enter_context(nc.psum_tensor(name, shape, dt))

        def sem(name):
            shared["semaphores"].append(nc.alloc_semaphore(name=name))
            return shared["semaphores"][-1]

        const = shared["const"]

        def cst(name):
            a, z = CONST_AT[name]
            return const[:, a:z]

        ident, before, ones = cst("ident"), cst("before"), cst("ones")
        wq = sb("a_wq", [P, KD, MT0 * P])
        wk = sb("a_wk", [P, KD, MT0 * P])
        wv = sb("a_wv", [P, KD, D])
        wr = sb("a_wr", [P, KD, NE])
        bq = sb("a_bq", [P, MT0])
        bqs = sb("a_bqs", [P, MT0])
        bk = sb("a_bk", [P, MT0])
        bv = sb("a_bv", [P, D])
        gamma = sb("a_gamma", [P, D])
        beta = sb("a_beta", [P, D])
        br = sb("a_br", [P, NE])
        pick_bias = sb("a_pick_bias", [P, NE])
        zeros = sb("a_zeros", [P, D])

        x_in = [sb(f"a_x{p}", [P, D]) for p in range(2)]
        c_in = [sb(f"a_c{p}", [P, D]) for p in range(2)]
        mask_in = [sb(f"a_mask{p}", [P, P], I32) for p in range(2)]
        x_res = [sb(f"a_xr{p}", [P, D]) for p in range(2)]
        c_res = [sb(f"a_cr{p}", [P, D]) for p in range(2)]
        keep = [sb(f"a_keep{p}", [P, P]) for p in range(2)]
        stat = sb("a_stat", [P, 3, 6])
        agg = sb("a_agg", [P, 3, 2])
        rstd = sb("a_rstd", [P, 3, 2])
        xn = [sb(f"a_xn{p}", [P, D]) for p in range(2)]
        tT = [sb(f"a_tT{p}", [P, 4, P]) for p in range(2)]
        qT = [sb(f"a_qT{p}", [P, MT0, P]) for p in range(2)]
        kT = [sb(f"a_kT{p}", [P, MT0, P]) for p in range(2)]
        va = [sb(f"a_va{p}", [P, NH, DH0 + 1]) for p in range(2)]
        soft = [sb(f"a_soft{h}", [P, HPT // 2, MT0, P]) for h in range(2)]
        top = sb("a_top", [P, HPT, MT0])
        pT = [sb(f"a_pT{k}", [P, MT0, P]) for k in range(2)]
        den = sb("a_den", [P, NH])
        att = sb("a_att", [P, NH, DH0])
        attf = att[:, :, :].rearrange("p h d -> p (h d)")
        y = sb("a_y", [P, D])
        x1 = [sb(f"a_x1{p}", [P, D]) for p in range(2)]
        xn1 = [sb(f"a_xn1{p}", [P, D]) for p in range(2)]
        xn1T = sb("a_xn1T", [P, KD, P])
        score = sb("a_score", [P, NE])
        biased = sb("a_biased", [P, NE])
        best = sb("a_best", [P, 8])
        best_at = sb("a_best_at", [P, 8], U32)
        best_f = sb("a_best_f", [P, TOPK])
        chosen = sb("a_chosen", [P, NE])
        negmax = sb("a_negmax", [P, 1])
        escore = sb("a_escore", [P, NE])
        prod = sb("a_prod", [P, TOPK, NE])
        val = sb("a_val", [P, TOPK])
        tot = sb("a_tot", [P, 1])
        rtot = sb("a_rtot", [P, 1])
        at_row = sb("a_at_row", [P, NE])
        slot_i = [sb(f"a_slot{p}", [P, TOPK], I32) for p in range(2)]
        base = sb("a_base", [P, NE])
        count = sb("a_count", [P, NE])
        count_i = sb("a_count_i", [P, NE], I32)
        cmp16 = sb("a_cmp16", [P, NE, NB])
        ntile = sb("a_ntile", [P, NE])
        cmp8 = sb("a_cmp8", [P, NE, NE])
        tile_end = sb("a_tile_end", [P, NE])
        tile_start = sb("a_tile_start", [P, NE])
        shift = sb("a_shift", [P, NE])
        last = sb("a_last", [P, 1])
        tt = sb("a_tt", [P, N_TILES])
        cmpt = sb("a_cmpt", [P, N_TILES, NE])
        te = sb("a_te", [P, N_TILES])
        tr = sb("a_tr", [P, N_TILES])
        slot_c = sb("a_slot_c", [P, NB, TOPK])
        cmps = sb("a_cmps", [P, NB * TOPK, NE])

        S = [ps(f"a_S{j}", [P, MT0, P]) for j in range(HPT)]
        M = [ps(f"a_M{j}", [P, 512]) for j in range(2)]
        T = [ps(f"a_T{j}", [P, 512]) for j in range(2)]

        s_w = sem("a_weights")
        s_setup = sem("a_setup")
        s_bqs = sem("a_bqs")
        s_in = [sem(f"a_in{p}") for p in range(2)]
        s_res = [sem(f"a_res{p}") for p in range(2)]
        s_x1out = [sem(f"a_x1out{p}") for p in range(2)]
        names = ("keep var rstd xn t_mm t_sb q_mm q_sb k_mm k_sb v_mm v_sb s_mm s_sub s_exp p_mm p_sb pv_mm att var1 rstd1 "
                 "x1 var2 rstd2 xn1 t1_mm t1_sb r_mm score esc pos_mm chosen slot rows")
        g = {n: sem("a_" + n) for n in names.split()}
        s_sc = [sem(f"a_scatter{p}") for p in range(2)]
        s_pad = sem("a_pad")
        s_count = sem("a_count")
        l_ln, l_sm, l_a3, l_top, l_slot, l_fin, l_prefix = (
            sem("al_" + n) for n in "ln softmax out top slot final prefix".split())
        l_pool = [sem(f"al_pool{k}") for k in range(3)]

        W = [(wq[:, :, :], t["L0_wqT"].rearrange("(k p) n -> p k n", p=P)),
             (wk[:, :, :], t["L0_wkT"].rearrange("(k p) n -> p k n", p=P)),
             (wv[:, :, :], t["L0_wvT"].rearrange("(k p) n -> p k n", p=P)),
             (wr[:, :, :], t["L0_wrT"].rearrange("(k p) n -> p k n", p=P)),
             (bq[:, :], t["L0_bq"]), (bk[:, :], t["L0_bk"]),
             (bv[:, :], t["L0_bv"].partition_broadcast(P)),
             (gamma[:, :], t["L0_gamma"].partition_broadcast(P)),
             (beta[:, :], t["L0_beta"].partition_broadcast(P)),
             (br[:, :], t["L0_br"].partition_broadcast(P)),
             (pick_bias[:, :], t["L0_pick_bias"].partition_broadcast(P)),
             (const[:, :], t["const"])]
        W_READY = 16 * len(W)

        def by_batch(steps):
            def run(eng):
                for b in range(2):
                    steps(b, 0, b, b == 0, False)
                with eng.Fori(1, NB // 2 - 1) as i:
                    for p in range(2):
                        steps(i * 2 + p, i, p, False, False)
                for p in range(2):
                    steps(NB - 2 + p, NB // 2 - 1, p, False, p == 1)
            return run

        block = ctx.enter_context(nc.Block())

        @block.sync
        def _(sp):
            for dst, src in W[:3]:
                sp.dma_start(dst, src).then_inc(s_w, 16)

            def store(b, p):
                sp.wait_ge(g["x1"], b + 1)
                sp.dma_start(t["x1"][bass.ds(b, 1)].rearrange("o p d -> (o p) d"), x1[p][:, :]).then_inc(s_x1out[p], 16)

            def load(b, i, p, *_):
                since(sp, g["t_mm"], b - 1)
                since(sp, g["xn"], b - 1)
                since(sp, g["keep"], b - 1)
                sp.dma_start(x_in[p][:, :], t["x"][bass.ds(b, 1)].rearrange("o p d -> (o p) d")).then_inc(s_in[p], 16)
                sp.dma_start(c_in[p][:, :], t["ctx"][bass.ds(b, 1)].rearrange("o p d -> (o p) d")).then_inc(s_in[p], 16)
                sp.dma_start(mask_in[p][:, :], t["mask"][bass.ds(b, 1)].rearrange("o s -> (o s)").partition_broadcast(P))\
                    .then_inc(s_in[p], 16)
                if not (isinstance(b, int) and b < 2):
                    store(b - 2, p)
                sp.dma_start(x_res[p][:, :], t["x"][bass.ds(b, 1)].rearrange("o p d -> (o p) d")).then_inc(s_res[p], 16)
                sp.dma_start(c_res[p][:, :], t["ctx"][bass.ds(b, 1)].rearrange("o p d -> (o p) d")).then_inc(s_res[p], 16)

            by_batch(load)(sp)
            for p in range(2):
                store(NB - 2 + p, p)
            sp.wait_ge(s_count, 1)
            for e in range(NE):
                n = sp.value_load(count_i[0:1, e:e + 1], min_val=0, max_val=NB * P)
                sp.dma_start(t["lists"][bass.ds(n + e * ROWS_E, P)], zeros[:, :]).then_inc(s_pad, 16)
            sp.wait_ge(s_pad, 16 * NE)
            for p in range(2):
                sp.wait_ge(s_x1out[p], 16 * (NB // 2))

        @block.gpsimd
        def _(pool):
            nc.gpsimd.memset(zeros[:, :], 0.0).then_inc(s_setup, 1)
            nc.gpsimd.memset(shared["mhalf"][:, :], -0.5).then_inc(s_setup, 1)
            for p in range(2):
                nc.gpsimd.memset(va[p][:, :, :], 1.0).then_inc(s_setup, 1)
            pool.wait_ge(s_setup, 4)
            def inverse_std(link, eps, ready, done, b, k):
                apart(pool, ready, b + 1)
                link.begin(b)
                link(nc.gpsimd.tensor_scalar(rstd[:, k, 0:1], agg[:, k, 1:2], eps, None, ALU.add))
                nc.gpsimd.tensor_tensor(rstd[:, k, 1:2], rstd[:, k, 0:1], shared["mhalf"][:, :], ALU.pow).then_inc(done, 1)

            links = [Link(pool, l, 1) for l in l_pool]

            def std_in(b):
                inverse_std(links[0], EPS, g["var"], g["rstd"], b, 0)

            def std_out(b):
                inverse_std(links[1], EPS0, g["var1"], g["rstd1"], b, 1)
                inverse_std(links[2], EPS, g["var2"], g["rstd2"], b, 2)

            def scatter(b, i, p):
                apart(pool, g["slot"], b + 1)
                for k in range(TOPK):
                    nc.gpsimd.indirect_dma_start(t["lists"], bass.IndirectOffsetOnAxis(slot_i[p][:, k:k + 1], 0),
                                                 xn1[p][:, :], None).then_inc(s_sc[p], 16)

            std_in(0)
            std_in(1)

            def steps(b, i, p, first, last):
                if not first:
                    std_out(b - 1)
                if not (isinstance(b, int) and b + 2 >= NB):
                    std_in(b + 2)
                if not first:
                    scatter(b - 1, i - 1 + p, 1 - p)

            by_batch(steps)(pool)
            std_out(NB - 1)
            scatter(NB - 1, NB // 2 - 1, 1)
            for p in range(2):
                pool.wait_ge(s_sc[p], 32 * (NB // 2))

        @block.scalar
        def _(act):
            for dst, src in W[3:]:
                act.dma_start(dst, src).then_inc(s_w, 16)
            shared["load_experts"](act)
            act.wait_ge(s_w, W_READY)
            nc.scalar.activation(bqs[:, :], bq[:, :], ACT.Copy, scale=SCALE0).then_inc(s_bqs, 1)
            act.wait_ge(s_bqs, 1)
            act.wait_ge(s_setup, 4)

            def project(b, i, p):
                act.wait_ge(g["t_mm"], b + 1)
                since(act, g["v_mm"], b - 1)
                nc.scalar.activation(tT[p][:, :, :], T[0][:, :].rearrange("p (c n) -> p c n", c=4), ACT.Copy).then_inc(g["t_sb"], 1)

            def queries(b, i, p):
                act.wait_ge(g["q_mm"], b + 1)
                since(act, g["s_mm"], b - 1)
                for m in range(MT0):
                    ins = nc.scalar.activation(qT[p][:, m, :], M[0][:, m * P:(m + 1) * P], ACT.Identity,
                                               bias=bqs[:, m:m + 1], scale=SCALE0)
                ins.then_inc(g["q_sb"], 1)

            def values(b, i, p):
                act.wait_ge(g["v_mm"], b + 1)
                since(act, g["pv_mm"], 4 * (b - 1))
                nc.scalar.activation(va[p][:, :, 0:DH0], M[0][:, 0:D].rearrange("p (h d) -> p h d", h=NH), ACT.Copy)\
                    .then_inc(g["v_sb"], 1)

            def exps(b, h):
                act.wait_ge(g["s_sub"], 2 * b + h + 1)
                nc.scalar.activation(soft[h][:, :, :, :], soft[h][:, :, :, :], ACT.Exp).then_inc(g["s_exp"], 1)

            def probs(b, k):
                act.wait_ge(g["p_mm"], 4 * b + k + 1)
                since(act, g["pv_mm"], 4 * b + k - 1)
                nc.scalar.activation(pT[k % 2][:, :, :], T[k % 2][:, :].rearrange("p (h n) -> p h n", h=MT0), ACT.Copy)\
                    .then_inc(g["p_sb"], 1)

            def next_rows(b):
                act.wait_ge(g["t1_mm"], b + 1)
                since(act, g["r_mm"], b)
                nc.scalar.activation(xn1T[:, :, :], T[1][:, 0:D].rearrange("p (c n) -> p c n", c=KD), ACT.Copy).then_inc(g["t1_sb"], 1)

            def exp_scores(b):
                act.wait_ge(g["score"], b + 1)
                nc.scalar.activation(escore[:, :], score[:, :], ACT.Exp, bias=negmax[:, 0:1]).then_inc(g["esc"], 1)

            project(0, 0, 0)
            queries(0, 0, 0)
            values(0, 0, 0)

            def steps(b, i, p, first, last):
                if not first:
                    next_rows(b - 1)
                if not last:
                    project(b + 1, i + p, 1 - p)
                if not first:
                    exp_scores(b - 1)
                exps(b, 0)
                if not last:
                    queries(b + 1, i + p, 1 - p)
                exps(b, 1)
                if not last:
                    values(b + 1, i + p, 1 - p)
                for k in range(4):
                    probs(b, k)

            by_batch(steps)(act)
            next_rows(NB - 1)
            exp_scores(NB - 1)

        @block.tensor
        def _(pe):
            pe.wait_ge(s_w, W_READY)

            def transposes(b, i, p):
                pe.wait_ge(g["xn"], b + 1)
                pe.wait_ge(s_in[p], 48 * (i + 1))
                since(pe, g["p_sb"], 4 * b - 5)
                for c in range(KD):
                    nc.tensor.transpose(T[0][:, c * P:(c + 1) * P], xn[p][:, c * P:(c + 1) * P], ident)
                for c in range(KD):
                    ins = nc.tensor.transpose(T[0][:, (KD + c) * P:(KD + c + 1) * P], c_in[p][:, c * P:(c + 1) * P], ident)
                ins.then_inc(g["t_mm"], 1)

            def strips(out, w, src, done):
                for m in range(MT0):
                    for c in range(KD):
                        ins = nc.tensor.matmul(out[:, m * P:(m + 1) * P], w[:, c, m * P:(m + 1) * P], src[c],
                                               start=(c == 0), stop=(c == KD - 1))
                ins.then_inc(done, 1)

            def queries(b, i, p):
                pe.wait_ge(g["t_sb"], b + 1)
                since(pe, g["v_sb"], b)
                strips(M[0], wq, [tT[p][:, c, :] for c in range(KD)], g["q_mm"])

            def keys(b, i, p):
                since(pe, g["att"], b - 1)
                strips(M[1], wk, [tT[p][:, KD + c, :] for c in range(KD)], g["k_mm"])

            def values(b, i, p):
                pe.wait_ge(g["q_sb"], b + 1)
                for c in range(KD):
                    ins = nc.tensor.matmul(M[0][:, 0:D], tT[p][:, KD + c, :], wv[:, c, :], start=(c == 0), stop=(c == KD - 1))
                ins.then_inc(g["v_mm"], 1)

            def scores(b, i, p):
                pe.wait_ge(g["q_sb"], b + 1)
                pe.wait_ge(g["k_sb"], b + 1)
                since(pe, g["s_sub"], 2 * b)
                for m in range(MT0):
                    for j in range(HPT):
                        r = slice(j * STRIP, (j + 1) * STRIP)
                        ins = nc.tensor.matmul(S[j][:, m, :], qT[p][r, m, :], kT[p][r, m, :], start=True, stop=True)
                ins.then_inc(g["s_mm"], 1)

            def attend(b, i, p, k, last):
                pe.wait_ge(g["s_exp"], 2 * b + k // 2 + 1)
                since(pe, g["p_sb"], 4 * b + k - 1)
                if k == 0 and not last:
                    pe.wait_ge(g["t_sb"], b + 2)
                if k == 1:
                    since(pe, g["slot"], b)
                for m in range(MT0):
                    ins = nc.tensor.transpose(T[k % 2][:, m * P:(m + 1) * P], soft[k // 2][:, k % 2, m, :], ident)
                ins.then_inc(g["p_mm"], 1)
                pe.wait_ge(g["p_sb"], 4 * b + k + 1)
                if k == 0:
                    pe.wait_ge(g["v_sb"], b + 1)
                    if not last:
                        pe.wait_ge(g["k_sb"], b + 2)
                for m in range(MT0):
                    head = m * HPT + k
                    ins = nc.tensor.matmul(M[1][:, head * (DH0 + 1):(head + 1) * (DH0 + 1)], pT[k % 2][:, m, :],
                                           va[p][:, head, :], start=True, stop=True)
                ins.then_inc(g["pv_mm"], 1)

            def next_rows(b, i, p):
                pe.wait_ge(g["xn1"], b + 1)
                pe.wait_ge(g["p_sb"], 4 * b + 4)
                for c in range(KD):
                    ins = nc.tensor.transpose(T[1][:, c * P:(c + 1) * P], xn1[p][:, c * P:(c + 1) * P], ident)
                ins.then_inc(g["t1_mm"], 1)

            def router(b):
                pe.wait_ge(g["t1_sb"], b + 1)
                for c in range(KD):
                    ins = nc.tensor.matmul(T[1][:, D:D + NE], xn1T[:, c, :], wr[:, c, :], start=(c == 0), stop=(c == KD - 1))
                ins.then_inc(g["r_mm"], 1)

            def places(b):
                pe.wait_ge(g["chosen"], b + 1)
                nc.tensor.matmul(T[1][:, D + NE:D + 2 * NE], before, chosen[:, :], start=True, stop=True)
                nc.tensor.matmul(T[1][:, D + 2 * NE:D + 3 * NE], ones, chosen[:, :], start=True, stop=True)\
                    .then_inc(g["pos_mm"], 1)

            transposes(0, 0, 0)
            queries(0, 0, 0)
            keys(0, 0, 0)
            values(0, 0, 0)

            def steps(b, i, p, first, last):
                scores(b, i, p)
                if not first:
                    next_rows(b - 1, i - 1 + p, 1 - p)
                if not last:
                    transposes(b + 1, i + p, 1 - p)
                if not first:
                    router(b - 1)
                if not last:
                    queries(b + 1, i + p, 1 - p)
                    keys(b + 1, i + p, 1 - p)
                if not first:
                    places(b - 1)
                if not last:
                    values(b + 1, i + p, 1 - p)
                for k in range(4):
                    attend(b, i, p, k, last)

            by_batch(steps)(pe)
            next_rows(NB - 1, NB // 2 - 1, 1)
            router(NB - 1)
            places(NB - 1)

        @block.vector
        def _(dve):
            dve.wait_ge(s_w, W_READY)
            ln, sm, out, pick, place = (Link(dve, s, n) for s, n in
                                        ((l_ln, 1), (l_sm, 2), (l_a3, 8), (l_top, 7), (l_slot, 4)))
            fin = Link(dve, l_fin, 21)
            fin.begin(0)
            fin(nc.vector.tensor_copy(base[:, :], cst("list")))

            def norm_in(b, i, p):
                dve.wait_ge(s_in[p], 48 * (i + 1))
                nc.vector.tensor_scalar(keep[p][:, :], mask_in[p][:, :], 0.0, cst("aug"), ALU.not_equal, ALU.not_equal)\
                    .then_inc(g["keep"], 1)
                ln.begin(b)
                ln(nc.vector.bn_stats(stat[:, 0, :], x_in[p][:, :]))
                ln.end()
                nc.vector.bn_aggr(agg[:, 0, :], stat[:, 0, :]).then_inc(g["var"], 1)
                dve.wait_ge(g["rstd"], b + 1)
                since(dve, g["t_mm"], b - 1)
                nc.vector.tensor_scalar(xn[p][:, :], x_in[p][:, :], agg[:, 0, 0:1], rstd[:, 0, 1:2], ALU.subtract, ALU.mult)\
                    .then_inc(g["xn"], 1)

            def keys(b, i, p):
                dve.wait_ge(g["k_mm"], b + 1)
                since(dve, g["s_mm"], b - 1)
                dve.wait_ge(g["keep"], b + 1)
                for m in range(MT0):
                    ins = nc.vector.scalar_tensor_tensor(kT[p][:, m, :], M[1][:, m * P:(m + 1) * P], bk[:, m:m + 1],
                                                         keep[p][:, :], ALU.add, ALU.mult)
                ins.then_inc(g["k_sb"], 1)

            def less_max(b, h):
                dve.wait_ge(g["s_mm"], b + 1)
                for u in range(HPT // 2):
                    j = h * (HPT // 2) + u
                    ins = nc.vector.tensor_reduce(top[:, j, :], S[j][:, :, :], X, ALU.max)
                sm(ins)
                since(dve, g["p_mm"], 4 * (b - 1) + 2 * h + 2)
                for u in range(HPT // 2):
                    j = h * (HPT // 2) + u
                    ins = nc.vector.tensor_tensor(soft[h][:, u, :, :], S[j][:, :, :],
                                                  top[:, j, :].unsqueeze(2).to_broadcast([P, MT0, P]), ALU.subtract)
                ins.then_inc(g["s_sub"], 1)

            def attention_out(b, i, p):
                out.begin(b)
                dve.wait_ge(g["pv_mm"], 4 * b + 4)
                o = M[1][:, 0:NH * (DH0 + 1)].rearrange("p (h d) -> p h d", h=NH)
                out(nc.vector.reciprocal(den[:, :], o[:, :, DH0]))
                ins = nc.vector.tensor_tensor(att[:, :, :], o[:, :, 0:DH0], den[:, :].unsqueeze(2).to_broadcast([P, NH, DH0]),
                                              ALU.mult)
                ins.then_inc(g["att"], 1)
                dve.wait_ge(g["att"], b + 1)
                out(nc.vector.tensor_tensor(attf, attf, bv[:, :], ALU.add))
                dve.wait_ge(s_res[p], 32 * (i + 1))
                out(nc.vector.tensor_tensor(attf, attf, c_res[p][:, :], ALU.add))
                out(nc.vector.bn_stats(stat[:, 1, :], attf))
                nc.vector.bn_aggr(agg[:, 1, :], stat[:, 1, :]).then_inc(g["var1"], 1)
                dve.wait_ge(g["rstd1"], b + 1)
                out(nc.vector.tensor_scalar(y[:, :], attf, agg[:, 1, 0:1], rstd[:, 1, 1:2], ALU.subtract, ALU.mult))
                out(nc.vector.tensor_tensor(y[:, :], y[:, :], gamma[:, :], ALU.mult))
                out(nc.vector.tensor_tensor(y[:, :], y[:, :], beta[:, :], ALU.add))
                since(dve, s_x1out[p], 16 * i)
                nc.vector.tensor_tensor(x1[p][:, :], y[:, :], x_res[p][:, :], ALU.add).then_inc(g["x1"], 1)
                dve.wait_ge(g["x1"], b + 1)
                out(nc.vector.bn_stats(stat[:, 2, :], x1[p][:, :]))
                nc.vector.bn_aggr(agg[:, 2, :], stat[:, 2, :]).then_inc(g["var2"], 1)
                dve.wait_ge(g["rstd2"], b + 1)
                since(dve, s_sc[p], 32 * i)
                nc.vector.tensor_scalar(xn1[p][:, :], x1[p][:, :], agg[:, 2, 0:1], rstd[:, 2, 1:2], ALU.subtract, ALU.mult)\
                    .then_inc(g["xn1"], 1)
                out.end()

            onehot, slots, weights = shared["onehot"], shared["slots"], shared["weights"]

            def hot(b):
                return onehot[:, bass.ds(b, 1)].rearrange("p o k e -> p (o k) e")

            def choose(b):
                pick.begin(b)
                dve.wait_ge(g["r_mm"], b + 1)
                since(dve, g["esc"], b)
                pick(nc.vector.tensor_tensor(score[:, :], T[1][:, D:D + NE], br[:, :], ALU.add))
                nc.vector.tensor_reduce(negmax[:, :], score[:, :], X, ALU.max, negate=True).then_inc(g["score"], 1)
                pick(nc.vector.tensor_tensor(biased[:, :], score[:, :], pick_bias[:, :], ALU.add))
                pick(nc.vector.max(best[:, :], biased[:, :]))
                pick(nc.vector.max_index(best_at[:, :], best[:, :], biased[:, :]))
                pick(nc.vector.tensor_copy(best_f[:, :], best_at[:, 0:TOPK]))
                for k in range(TOPK):
                    ins = nc.vector.tensor_scalar(onehot[:, bass.ds(b, 1), k, :].rearrange("p o e -> p (o e)"), cst("expert"),
                                                  best_f[:, k:k + 1], None, ALU.is_equal)
                pick(ins)
                oh = hot(b)
                since(dve, g["pos_mm"], b)
                nc.vector.tensor_tensor(chosen[:, :], oh[:, 0, :], oh[:, 1, :], ALU.add).then_inc(g["chosen"], 1)
                dve.wait_ge(g["esc"], b + 1)
                pick(nc.vector.tensor_tensor(prod[:, :, :], oh, escore[:, :].unsqueeze(1).to_broadcast([P, TOPK, NE]), ALU.mult))
                pick.end()

            def list_rows(b, i, p):
                place.begin(b)
                place(nc.vector.tensor_reduce(val[:, :], prod[:, :, :], X, ALU.add))
                place(nc.vector.tensor_tensor(tot[:, :], val[:, 0:1], val[:, 1:2], ALU.add))
                place(nc.vector.reciprocal(rtot[:, :], tot[:, :]))
                nc.vector.tensor_scalar(weights[:, bass.ds(b, 1), :].rearrange("p o k -> p (o k)"), val[:, :], rtot[:, 0:1], None, ALU.mult)
                dve.wait_ge(g["pos_mm"], b + 1)
                place(nc.vector.tensor_tensor(at_row[:, :], T[1][:, D + NE:D + 2 * NE], base[:, :], ALU.add))
                place.end()
                nc.vector.tensor_tensor(base[:, :], T[1][:, D + 2 * NE:D + 3 * NE], base[:, :], ALU.add).then_inc(l_prefix, 1)
                nc.vector.tensor_tensor(prod[:, :, :], hot(b), at_row[:, :].unsqueeze(1).to_broadcast([P, TOPK, NE]), ALU.mult)\
                    .then_inc(l_prefix, 1)
                dve.wait_ge(l_prefix, 3 * b + 2)
                row = slots[:, bass.ds(b, 1), :].rearrange("p o k -> p (o k)")
                nc.vector.tensor_reduce(row, prod[:, :, :], X, ALU.add).then_inc(l_prefix, 1)
                apart(dve, l_prefix, 3 * b + 3)
                since(dve, s_sc[p], 32 * i)
                nc.vector.tensor_copy(slot_i[p][:, :], row).then_inc(g["slot"], 1)

            norm_in(0, 0, 0)
            keys(0, 0, 0)
            norm_in(1, 0, 1)

            def steps(b, i, p, first, last):
                sm.begin(b)
                if not first:
                    attention_out(b - 1, i - 1 + p, 1 - p)
                less_max(b, 0)
                if not first:
                    choose(b - 1)
                less_max(b, 1)
                sm.end()
                if not last:
                    keys(b + 1, i + p, 1 - p)
                if not first:
                    list_rows(b - 1, i - 1 + p, 1 - p)

            def steps_and_norm(b, i, p, first, last):
                steps(b, i, p, first, last)
                if not (isinstance(b, int) and b + 2 >= NB):
                    norm_in(b + 2, i + 1, p)

            by_batch(steps_and_norm)(dve)
            attention_out(NB - 1, NB // 2 - 1, 1)
            choose(NB - 1)
            list_rows(NB - 1, NB // 2 - 1, 1)

            dve.wait_ge(g["slot"], NB)
            dve.wait_ge(l_prefix, 3 * NB)
            fin(nc.vector.tensor_tensor(count[:, :], base[:, :], cst("list"), ALU.subtract))
            nc.vector.tensor_copy(count_i[:, :], count[:, :]).then_inc(s_count, 1)
            fin(nc.vector.tensor_tensor(cmp16[:, :, :], count[:, :].unsqueeze(2).to_broadcast([P, NE, NB]),
                                        cst("sizes").unsqueeze(1).to_broadcast([P, NE, NB]), ALU.is_gt))
            fin(nc.vector.tensor_reduce(ntile[:, :], cmp16[:, :, :], X, ALU.add))
            fin(nc.vector.tensor_tensor(cmp8[:, :, :], cst("upto").rearrange("p (a b) -> p a b", a=NE),
                                        ntile[:, :].unsqueeze(1).to_broadcast([P, NE, NE]), ALU.mult))
            fin(nc.vector.tensor_reduce(tile_end[:, :], cmp8[:, :, :], X, ALU.add))
            fin(nc.vector.tensor_tensor(tile_start[:, :], tile_end[:, :], ntile[:, :], ALU.subtract))
            fin(nc.vector.scalar_tensor_tensor(shift[:, :], tile_start[:, :], -float(P), cst("list"), ALU.mult, ALU.add))
            fin(nc.vector.tensor_scalar(last[:, :], tile_end[:, NE - 1:NE], -1.0, None, ALU.add))
            fin(nc.vector.tensor_scalar(tt[:, :], cst("tiles"), last[:, 0:1], None, ALU.min))
            fin(nc.vector.tensor_tensor(cmpt[:, :, :], tile_end[:, :].unsqueeze(1).to_broadcast([P, N_TILES, NE]),
                                        tt[:, :].unsqueeze(2).to_broadcast([P, N_TILES, NE]), ALU.is_le))
            fin(nc.vector.tensor_reduce(te[:, :], cmpt[:, :, :], X, ALU.add))
            nc.vector.tensor_copy(shared["tile_expert"][:, :], te[:, :])
            fin(nc.vector.tensor_tensor(cmpt[:, :, :], cst("expert").unsqueeze(1).to_broadcast([P, N_TILES, NE]),
                                        te[:, :].unsqueeze(2).to_broadcast([P, N_TILES, NE]), ALU.is_equal))
            fin(nc.vector.tensor_tensor(cmpt[:, :, :], cmpt[:, :, :], shift[:, :].unsqueeze(1).to_broadcast([P, N_TILES, NE]), ALU.mult))
            fin(nc.vector.tensor_reduce(tr[:, :], cmpt[:, :, :], X, ALU.add))
            fin(nc.vector.scalar_tensor_tensor(tr[:, :], tt[:, :], float(P), tr[:, :], ALU.mult, ALU.add))
            fin(nc.vector.tensor_copy(shared["tile_row"][:, :], tr[:, :]))
            flat = onehot[:, :, :, :].rearrange("p b k e -> p (b k) e")
            fin(nc.vector.tensor_tensor(cmps[:, :, :], flat, shift[:, :].unsqueeze(1).to_broadcast([P, NB * TOPK, NE]), ALU.mult))
            fin(nc.vector.tensor_reduce(slot_c[:, :, :].rearrange("p b k -> p (b k)"), cmps[:, :, :], X, ALU.add))
            fin(nc.vector.tensor_tensor(slot_c[:, :, :], slots[:, :, :], slot_c[:, :, :], ALU.subtract))
            fin(nc.vector.tensor_copy(shared["tile_rows"][:, :, :], slot_c[:, :, :]))
            fin.end()


def experts(nc, t, shared):
    with ExitStack() as ctx:
        def sb(name, shape, dt=F32):
            return ctx.enter_context(nc.sbuf_tensor(name, shape, dt))

        def ps(name, shape, dt=F32):
            return ctx.enter_context(nc.psum_tensor(name, shape, dt))

        def sem(name):
            shared["semaphores"].append(nc.alloc_semaphore(name=name))
            return shared["semaphores"][-1]

        a, z = CONST_AT["ident"]
        ident = shared["const"][:, a:z]
        w1, w2, b1, b2 = (shared[n] for n in ("w1", "w2", "b1", "b2"))
        tile_expert, tile_row = shared["tile_expert"], shared["tile_row"]
        rows = [sb(f"b_rows{p}", [P, D]) for p in range(2)]
        rowsT = [sb(f"b_rowsT{p}", [P, KD, P]) for p in range(2)]
        gate = [sb(f"b_gate{p}", [P, HE]) for p in range(2)]
        up = [sb(f"b_up{p}", [P, HE]) for p in range(2)]
        hidT = [sb(f"b_hidT{p}", [P, KH, P]) for p in range(2)]
        out = [sb(f"b_out{p}", [P, D]) for p in range(2)]
        G = [ps(f"b_G{p}", [P, HE]) for p in range(2)]
        U = [ps(f"b_U{p}", [P, HE]) for p in range(2)]
        RT = ps("b_RT", [P, KD, P])
        HT = ps("b_HT", [P, KH, P])
        Y = ps("b_Y", [P, D])

        s_in = [sem(f"b_in{p}") for p in range(2)]
        s_out = [sem(f"b_out_{p}") for p in range(2)]
        names = "rt_mm rt_sb g_mm u_mm gate silu up hid ht_mm ht_sb y_mm y_sb"
        g = {n: sem("b_" + n) for n in names.split()}

        def by_tile(steps):
            def run(eng):
                for n in range(2):
                    steps(n, 0, n, n == 0, False)
                with eng.Fori(1, (N_TILES - 3) // 2 + 1) as i:
                    for p in range(2):
                        steps(i * 2 + p, i, p, False, False)
                n = 2 * ((N_TILES - 3) // 2 + 1)
                while n < N_TILES:
                    steps(n, n // 2, n % 2, False, n == N_TILES - 1)
                    n += 1
            return run

        block = ctx.enter_context(nc.Block())

        @block.sync
        def _(sp):
            def steps(n, i, p, *_):
                if isinstance(n, int):
                    at = tile_row[0:1, n:n + 1]
                else:
                    at = tile_row[0:1, bass.ds(n, 1)]
                row = sp.value_load(at, min_val=0, max_val=NE * ROWS_E - P)
                since(sp, g["rt_mm"], n - 1)
                sp.dma_start(rows[p][:, :], t["lists"][bass.ds(row, P)]).then_inc(s_in[p], 16)
                if not (isinstance(n, int) and n < 2):
                    store(n - 2, p)

            def store(n, p):
                sp.wait_ge(g["y_sb"], n + 1)
                sp.dma_start(t["expert_out"][bass.ds(n * P, P)], out[p][:, :]).then_inc(s_out[p], 16)

            by_tile(steps)(sp)
            for n in range(N_TILES - 2, N_TILES):
                store(n, n % 2)
            sp.wait_ge(s_out[0], 16 * ((N_TILES + 1) // 2))
            sp.wait_ge(s_out[1], 16 * (N_TILES // 2))

        @block.gpsimd
        def _(pool):
            def steps(n, i, p, *_):
                pool.wait_ge(g["silu"], n + 1)
                pool.wait_ge(g["up"], n + 1)
                nc.gpsimd.tensor_tensor(up[p][:, :], up[p][:, :], gate[p][:, :], ALU.mult).then_inc(g["hid"], 1)

            by_tile(steps)(pool)

        @block.scalar
        def _(act):
            def rows_sb(n, i, p):
                act.wait_ge(g["rt_mm"], n + 1)
                since(act, g["u_mm"], n - 1)
                nc.scalar.activation(rowsT[p][:, :, :], RT[:, :, :], ACT.Copy).then_inc(g["rt_sb"], 1)

            shared["load_layer1"](act)
            rows_sb(0, 0, 0)

            def steps(n, i, p, first, last):
                if not last:
                    rows_sb(n + 1, i + p, 1 - p)
                act.wait_ge(g["gate"], n + 1)
                nc.scalar.activation(gate[p][:, :], gate[p][:, :], ACT.Silu).then_inc(g["silu"], 1)
                act.wait_ge(g["ht_mm"], n + 1)
                since(act, g["y_mm"], n - 1)
                nc.scalar.activation(hidT[p][:, :, :], HT[:, :, :], ACT.Copy).then_inc(g["ht_sb"], 1)

            by_tile(steps)(act)

        def expert_of(eng, n):
            at = tile_expert[0:1, n:n + 1] if isinstance(n, int) else tile_expert[0:1, bass.ds(n, 1)]
            return eng.value_load(at, min_val=0, max_val=NE - 1)

        @block.tensor
        def _(pe):
            pe.wait_ge(shared["s_experts"], 16 * 4)

            def transposes(n, i, p):
                pe.wait_ge(s_in[p], 16 * (i + 1))
                since(pe, g["rt_sb"], n)
                for c in range(KD):
                    ins = nc.tensor.transpose(RT[:, c, :], rows[p][:, c * P:(c + 1) * P], ident)
                ins.then_inc(g["rt_mm"], 1)

            def first_products(n, i, p):
                e = expert_of(pe, n)
                pe.wait_ge(g["rt_sb"], n + 1)
                since(pe, g["gate"], n - 1)
                since(pe, g["up"], n - 1)
                for at, dst, done in ((0, G[p], g["g_mm"]), (HE, U[p], g["u_mm"])):
                    for c in range(KD):
                        w = w1[:, bass.ds(e, 1), c, at:at + HE].rearrange("p o n -> p (o n)")
                        ins = nc.tensor.matmul(dst[:, :], rowsT[p][:, c, :], w, start=(c == 0), stop=(c == KD - 1))
                    ins.then_inc(done, 1)

            transposes(0, 0, 0)
            first_products(0, 0, 0)

            def steps(n, i, p, first, last):
                if not last:
                    transposes(n + 1, i + p, 1 - p)
                    first_products(n + 1, i + p, 1 - p)
                pe.wait_ge(g["hid"], n + 1)
                since(pe, g["ht_sb"], n)
                for k in range(KH):
                    ins = nc.tensor.transpose(HT[:, k, :], up[p][:, k * P:(k + 1) * P], ident)
                ins.then_inc(g["ht_mm"], 1)
                e = expert_of(pe, n)
                pe.wait_ge(g["ht_sb"], n + 1)
                since(pe, g["y_sb"], n)
                for k in range(KH):
                    w = w2[:, bass.ds(e, 1), k, :].rearrange("p o n -> p (o n)")
                    ins = nc.tensor.matmul(Y[:, :], hidT[p][:, k, :], w, start=(k == 0), stop=(k == KH - 1))
                ins.then_inc(g["y_mm"], 1)

            by_tile(steps)(pe)

        @block.vector
        def _(dve):
            dve.wait_ge(shared["s_experts"], 16 * 4)

            def hidden(n, i, p):
                e = expert_of(dve, n)
                dve.wait_ge(g["g_mm"], n + 1)
                since(dve, g["hid"], n - 1)
                bias = b1[:, bass.ds(e, 1), :].rearrange("p o n -> p (o n)")
                nc.vector.tensor_tensor(gate[p][:, :], G[p][:, :], bias[:, 0:HE], ALU.add).then_inc(g["gate"], 1)
                dve.wait_ge(g["u_mm"], n + 1)
                since(dve, g["ht_mm"], n - 1)
                nc.vector.tensor_tensor(up[p][:, :], U[p][:, :], bias[:, HE:2 * HE], ALU.add).then_inc(g["up"], 1)

            hidden(0, 0, 0)

            def steps(n, i, p, first, last):
                if not last:
                    hidden(n + 1, i + p, 1 - p)
                e = expert_of(dve, n)
                dve.wait_ge(g["y_mm"], n + 1)
                since(dve, s_out[p], 16 * i)
                nc.vector.tensor_tensor(out[p][:, :], Y[:, :], b2[:, bass.ds(e, 1), :].rearrange("p o n -> p (o n)"), ALU.add)\
                    .then_inc(g["y_sb"], 1)

            by_tile(steps)(dve)


DH1 = 64
INNER = NH * DH1
MT1 = INNER // P
NREL = 2 * MAXREL + 1
STREAMS = [(0, TEXT), (TEXT, TEXT + IMG), (TEXT + IMG, P)]
NS = len(STREAMS)
SCALE1 = 1.0 / DH1 ** 0.5
RELW = P - 1 + TEXT
REL_LO = P - 1 - MAXREL
BANDW = P + 2 * MAXREL
L1_EARLY = ["Wq", "Wk0", "Wk1", "Wk2", "Wv0", "Wv1"]
HS = NH // 2
MS = MT1 // 2
NPAIR = NB // 2
TURNS = 17
TURNS_AHEAD = 16
NO_BANDS = 2


class Turns:

    def __init__(self):
        self.n, self.bank = 0, 0

    def begin(self, b, p):
        n = b * TURNS + TURNS_AHEAD - NO_BANDS
        if not isinstance(b, int) or b == NB - 2:
            self.n, self.bank = n, p
        else:
            assert b in (0, NB - 1) or (self.n == n and self.bank == p), (b, self.n, n)

    def next(self):
        n, k = self.n, self.bank
        self.n, self.bank = n + 1, 1 - k
        return n, k


def attention1(nc, t, shared):
    with ExitStack() as ctx:
        def sb(name, shape, dt=F32):
            return ctx.enter_context(nc.sbuf_tensor(name, shape, dt))

        def ps(name, shape, dt=F32):
            return ctx.enter_context(nc.psum_tensor(name, shape, dt))

        def sem(name):
            shared["semaphores"].append(nc.alloc_semaphore(name=name))
            return shared["semaphores"][-1]

        const = shared["const"]

        def cst(name):
            a, z = CONST_AT[name]
            return const[:, a:z]

        ident = cst("ident")
        weights = dict(shared["layer1"])
        weights["Wv2"] = sb("c_wv2", [P, KD, INNER])[:, :, :]
        weights["Wo"] = sb("c_wo", [P, MT1, D])[:, :, :]
        wq, wo = weights["Wq"], weights["Wo"]
        wk, wv = ([weights[f"W{n}{s}"] for s in range(NS)] for n in "kv")
        relk = sb("c_relk", [P, 2 * NREL])
        relv = sb("c_relv", [2 * NREL, 2 * DH1])
        bo = sb("c_bo", [P, D])
        alphas = sb("c_alphas", [P, 2])
        tanhs = sb("c_tanhs", [P, 2])
        coef = sb("c_coef", [P, NS, NH])
        zeros = sb("c_zeros", [P, BANDW])

        two = range(2)
        x_in = [sb(f"c_x{p}", [P, D]) for p in two]
        c_in = [sb(f"c_c{p}", [P, D]) for p in two]
        pick = [sb(f"c_pick{p}", [P, TOPK], I32) for p in two]
        picked = [[sb(f"c_y{p}{k}", [P, D]) for k in range(TOPK)] for p in two]
        x2 = [sb(f"c_x2{p}", [P, D]) for p in two]
        x2b = [sb(f"c_x2b{p}", [P, D]) for p in two]
        x3 = [sb(f"c_x3{p}", [P, D]) for p in two]
        stat = [sb(f"c_stat{p}", [P, 6]) for p in two]
        agg = [sb(f"c_agg{p}", [P, 2]) for p in two]
        rstd = [sb(f"c_rstd{p}", [P, 2]) for p in two]
        xn = [sb(f"c_xn{p}", [P, D]) for p in two]
        xT = sb("c_xT", [P, KD, 2, P])
        cT = sb("c_cT", [P, KD, 2, P])
        qT = sb("c_qT", [P, MT1, 2, P])
        kT = sb("c_kT", [P, MT1, 2, P])
        vT = sb("c_vT", [P, MT1, 2, P])
        v = [sb(f"c_v{p}", [P, INNER]) for p in two]
        relw = [sb(f"c_relw{p}", [P, NH, RELW]) for p in two]
        bias = [sb(f"c_bias{p}", [P, NH, TEXT]) for p in two]
        soft = [sb(f"c_soft{p}", [P, NH, P]) for p in two]
        top = sb("c_top", [P, NS, NH])
        total = sb("c_total", [P, NS, NH])
        share = sb("c_share", [P, NS, NH])
        pT = [sb(f"c_pT{k}", [P, 4, P]) for k in two]
        near = sb("c_near", [P, NH, TEXT])
        far = sb("c_far", [P, NH, TEXT])
        band = [sb(f"c_band{p}", [P, NH, NREL]) for p in two]
        bandT = sb("c_bandT", [2 * NREL, MT1, P])
        attT = sb("c_attT", [P, MT1, P])

        S = ps("c_S", [P, NH, P])
        T = [ps(f"c_T{k}", [P, 512]) for k in two]
        O = [ps(f"c_O{h}", [P, MS, P]) for h in two]

        rel_d = [nc.dram_tensor(f"rel_windows{p}", (P, NH, RELW), F32, kind="Internal").ap() for p in two]
        prob_d = [nc.dram_tensor(f"prob_rows{p}", (P, NH, BANDW), F32, kind="Internal").ap() for p in two]

        s_w = sem("c_weights")
        s_late = sem("c_late_weights")
        s_zero = sem("c_zero")
        s_setup = sem("c_setup")
        s_alpha = sem("c_alpha")
        s_clear = sem("c_clear")
        s_in = [sem(f"c_in{p}") for p in two]
        s_pick = [sem(f"c_picked{p}") for p in two]
        s_relout = [sem(f"c_relout{p}") for p in two]
        s_relin = [sem(f"c_relin{p}") for p in two]
        s_pout = [sem(f"c_pout{p}") for p in two]
        s_pin = [sem(f"c_pin{p}") for p in two]
        s_x3 = [sem(f"c_x3out{p}") for p in two]
        names = "filled emptied pick x2 var rstd xn x2b s_mm s_sub s_exp share soft tails bandv pv_mm o_mm o_sb y_mm x3"
        g = {n: sem("c_" + n) for n in names.split()}
        l_front, l_sum, l_pool = (sem("cl_" + n) for n in "front sum pool".split())
        l_softs = [sem(f"cl_soft{h}") for h in range(2)]

        W = [(relk[:, :], t["L1_relk"]), (relv[:, :], t["L1_relv"]), (bo[:, :], t["L1_bo"].partition_broadcast(P)),
             (alphas[:, :], t["L1_alphas"].partition_broadcast(P))]
        W_READY = 16 * len(W)

        def sheared(d, at, step, parts, width):
            part, head, _ = d.ap
            return bass.AP(d.tensor, d.offset + at, [[part[0] + step, parts], [head[0], NH], [1, width]])

        def by_batch(steps):
            def run(eng):
                for b in range(2):
                    steps(b, 0, b, b == 0, False)
                with eng.Fori(1, NPAIR - 1) as i:
                    for p in range(2):
                        steps(i * 2 + p, i, p, False, False)
                for p in range(2):
                    steps(NB - 2 + p, NPAIR - 1, p, False, p == 1)
            return run

        def last_pair(i):
            return isinstance(i, int) and i == NPAIR - 1

        def rows_of(d, b):
            return d[bass.ds(b, 1)].rearrange("o p d -> (o p) d")

        block = ctx.enter_context(nc.Block())

        @block.sync
        def _(sp):
            def load(b, p):
                sp.dma_start(c_in[p][:, :], rows_of(t["ctx"], b)).then_inc(s_in[p], 16)
                sp.dma_start(x_in[p][:, :], rows_of(t["x1"], b)).then_inc(s_in[p], 16)

            def rel_in(b, i, p):
                sp.wait_ge(s_relout[p], 16 * (i + 1))
                since(sp, g["s_sub"], 2 * (b - 1))
                sp.dma_start(bias[p][:, :, :], sheared(rel_d[p], P - 1, -1, P, TEXT)).then_inc(s_relin[p], 16)

            def prob_out(b, i, p):
                apart(sp, g["soft"], 2 * b + 2)
                since(sp, s_pin[p], 16 * i)
                sp.dma_start(prob_d[p][:, :, MAXREL:MAXREL + TEXT], soft[p][:, :, 0:TEXT]).then_inc(s_pout[p], 16)

            def band_in(b, i, p):
                sp.wait_ge(s_pout[p], 16 * (i + 1))
                sp.dma_start(band[p][:, :, 1:NREL - 1], sheared(prob_d[p], 1, 1, P, NREL - 2)).then_inc(s_pin[p], 16)

            def store(b, p):
                sp.wait_ge(g["x3"], b + 1)
                sp.dma_start(rows_of(t["x3"], b), x3[p][:, :]).then_inc(s_x3[p], 16)

            for p in two:
                load(p, p)
            for dst, src in W:
                sp.dma_start(dst, src).then_inc(s_w, 16)
            for p in two:
                sp.wait_ge(s_zero, 1)
                for h in range(NH):
                    sp.dma_start(prob_d[p][:, h, :], zeros[:, :]).then_inc(s_clear, 16)
            sp.wait_ge(s_clear, 16 * 2 * NH)
            rel_in(0, 0, 0)

            def steps(b, i, p, first, last):
                if p == 0 and not last_pair(i):
                    if first:
                        sp.wait_ge(g["xn"], 2)
                        sp.wait_ge(g["filled"], 1)
                    for q in two:
                        load(b + 2 + q, q)
                if not first:
                    store(b - 1, 1 - p)
                prob_out(b, i, p)
                if not last:
                    rel_in(b + 1, i + p, 1 - p)
                band_in(b, i, p)

            by_batch(steps)(sp)
            store(NB - 1, 1)
            for p in two:
                sp.wait_ge(s_x3[p], 16 * (NB // 2))

        @block.gpsimd
        def _(pool):
            nc.gpsimd.memset(zeros[:, :], 0.0).then_inc(s_zero, 1)
            pool.wait_ge(s_w, W_READY)
            lk = Link(pool, l_pool, 1)

            def gather(b, p):
                apart(pool, g["x2"], b - 1)
                apart(pool, g["pick"], b + 1)
                for k in range(TOPK):
                    nc.gpsimd.indirect_dma_start(picked[p][k][:, :], None, t["expert_out"],
                                                 bass.IndirectOffsetOnAxis(pick[p][:, k:k + 1], 0)).then_inc(s_pick[p], 16)

            def inverse_std(b, p):
                apart(pool, g["var"], b + 1)
                lk.begin(b)
                lk(nc.gpsimd.tensor_scalar(rstd[p][:, 0:1], agg[p][:, 1:2], EPS, None, ALU.add))
                nc.gpsimd.tensor_tensor(rstd[p][:, 1:2], rstd[p][:, 0:1], shared["mhalf"][:, :], ALU.pow).then_inc(g["rstd"], 1)

            def residual(b, p):
                pool.wait_ge(g["x2"], b + 1)
                since(pool, g["x3"], b - 1)
                nc.gpsimd.tensor_tensor(x2b[p][:, :], x2[p][:, :], bo[:, :], ALU.add).then_inc(g["x2b"], 1)

            def normalise(b, p, h):
                hs = slice(h * HS, (h + 1) * HS)
                pool.wait_ge(g["share"], 2 * b + h + 1)
                for s, (a, z) in enumerate(STREAMS):
                    ins = nc.gpsimd.tensor_tensor(soft[p][:, hs, a:z], soft[p][:, hs, a:z],
                                                  share[:, s, hs].unsqueeze(2).to_broadcast([P, HS, z - a]), ALU.mult)
                ins.then_inc(g["soft"], 1)

            def tails(b, p):
                pool.wait_ge(g["soft"], 2 * b + 2)
                since(pool, g["bandv"], b)
                for dst, m in ((near, "before_band"), (far, "behind_band")):
                    ins = nc.gpsimd.tensor_tensor(dst[:, :, :], soft[p][:, :, 0:TEXT],
                                                  cst(m).unsqueeze(1).to_broadcast([P, NH, TEXT]), ALU.mult)
                ins.then_inc(g["tails"], 1)

            for p in two:
                gather(p, p)
            for p in two:
                inverse_std(p, p)
            residual(0, 0)

            def steps(b, i, p, first, last):
                ahead = p == 0 and not last_pair(i)
                if ahead:
                    for q in two:
                        gather(b + 2 + q, q)
                for h in range(2):
                    normalise(b, p, h)
                if not last:
                    residual(b + 1, 1 - p)
                if ahead:
                    for q in two:
                        inverse_std(b + 2 + q, q)
                tails(b, p)

            by_batch(steps)(pool)

        @block.scalar
        def _(act):
            for name in ("Wv2", "Wo"):
                act.dma_start(weights[name], t["L1_" + name].rearrange("(k p) n -> p k n", p=P)).then_inc(s_late, 16)
            act.wait_ge(s_w, W_READY)
            nc.scalar.activation(tanhs[:, :], alphas[:, :], ACT.Tanh).then_inc(s_setup, 1)
            turns = Turns()

            def empty(dst, view, **kw):
                n, k = turns.next()
                act.wait_ge(g["filled"], n + 1)
                nc.scalar.activation(dst, view(T[k]), ACT.Copy, **kw).then_inc(g["emptied"], 1)

            def parts(m):
                return lambda bank: bank[:, :].rearrange("p (m n) -> p m n", m=m)

            def projected(dst, scale=1.0):
                for u in range(4):
                    empty(dst[:, 2 * u:2 * u + 2, :, :].rearrange("p m q n -> p (m q) n"), parts(4), scale=scale)

            def transposed(dst):
                empty(dst[:, :, :, :].rearrange("p c q n -> p (c q) n"), parts(4))

            def values():
                for q in two:
                    for w in two:
                        empty(v[q][:, w * 512:(w + 1) * 512], lambda bank: bank[:, :])

            def windows(b, i, p):
                since(act, s_relout[p], 16 * i)
                hi = REL_LO + NREL
                for u in two:
                    n, k = turns.next()
                    act.wait_ge(g["filled"], n + 1)
                    r = T[k][:, 0:HS * NREL].rearrange("p (h r) -> p h r", h=HS)
                    w = relw[p][:, u * HS:(u + 1) * HS, :]
                    nc.scalar.activation(w[:, :, 0:REL_LO], r[:, :, 0:1].to_broadcast([P, HS, REL_LO]), ACT.Copy)
                    nc.scalar.activation(w[:, :, REL_LO:hi], r, ACT.Copy)
                    nc.scalar.activation(w[:, :, hi:RELW], r[:, :, NREL - 1:NREL].to_broadcast([P, HS, RELW - hi]), ACT.Copy)\
                        .then_inc(g["emptied"], 1)
                act.wait_ge(g["emptied"], n + 1)
                since(act, s_relin[p], 16 * i)
                act.dma_start(rel_d[p], relw[p][:, :, :]).then_inc(s_relout[p], 16)

            def exps(b, p, h):
                act.wait_ge(g["s_sub"], 2 * b + h + 1)
                hs = slice(h * HS, (h + 1) * HS)
                nc.scalar.activation(soft[p][:, hs, :], soft[p][:, hs, :], ACT.Exp).then_inc(g["s_exp"], 1)

            def bands():
                for h in two:
                    empty(bandT[:, h * MS:(h + 1) * MS, :], lambda bank: bank[0:2 * NREL, :].rearrange("p (m n) -> p m n", m=MS))

            def attended(b):
                for h in two:
                    act.wait_ge(g["o_mm"], 2 * b + h + 1)
                    nc.scalar.activation(attT[:, h * MS:(h + 1) * MS, :], O[h][:, :, :], ACT.Copy).then_inc(g["o_sb"], 1)

            def probs():
                for k in range(4):
                    empty(pT[k % 2][:, :, :], parts(4))

            transposed(cT)
            transposed(xT)
            projected(qT, SCALE1)
            windows(0, 0, 0)
            projected(kT)
            projected(vT)

            def steps(b, i, p, first, last):
                turns.begin(b, p)
                if not first:
                    bands()
                if p == 0:
                    if not last_pair(i):
                        transposed(cT)
                    values()
                    if not first:
                        attended(b - 1)
                    exps(b, p, 0)
                    windows(b + 1, i, 1)
                    exps(b, p, 1)
                    if not last_pair(i):
                        projected(vT)
                else:
                    if not last_pair(i):
                        transposed(xT)
                    attended(b - 1)
                    exps(b, p, 0)
                    if not last_pair(i):
                        projected(qT, SCALE1)
                    exps(b, p, 1)
                    if not last_pair(i):
                        windows(b + 1, i + 1, 0)
                        projected(kT)
                probs()

            by_batch(steps)(act)
            bands()
            attended(NB - 1)

        @block.tensor
        def _(pe):
            pe.wait_ge(shared["s_layer1"], 16 * len(L1_EARLY))
            pe.wait_ge(s_w, W_READY)
            turns = Turns()

            def turn():
                n, k = turns.next()
                since(pe, g["emptied"], n - 1)
                return n, T[k]

            def taken(n):
                pe.wait_ge(g["emptied"], n + 1)

            def transposes(parts):
                n, bank = turn()
                for j, part in enumerate(parts):
                    ins = nc.tensor.transpose(bank[0:part.shape[1], j * P:(j + 1) * P], part, ident)
                ins.then_inc(g["filled"], 1)
                return n

            def context(i):
                for q in two:
                    pe.wait_ge(s_in[q], 32 * (i + 1))
                return transposes([c_in[q][:, c * P:(c + 1) * P] for c in range(KD) for q in two])

            def rows(i):
                pe.wait_ge(g["xn"], 2 * i + 2)
                return transposes([xn[q][:, c * P:(c + 1) * P] for c in range(KD) for q in two])

            def projected(streams, src):
                for u in range(4):
                    n, bank = turn()
                    dst = bank[:, :].rearrange("p (m q n) -> p m q n", m=2, q=2)
                    for mm in two:
                        m = 2 * u + mm
                        for w, (a, z) in streams:
                            for c in range(KD):
                                ins = nc.tensor.matmul(dst[:, mm, :, a:z], w[:, c, m * P:(m + 1) * P], src[:, c, :, a:z],
                                                       start=(c == 0), stop=(c == KD - 1))
                    ins.then_inc(g["filled"], 1)
                return n

            def queries(n_rows):
                taken(n_rows)
                return projected([(wq, (0, P))], xT)

            def keys():
                return projected(list(zip(wk, STREAMS)), cT)

            def transposed_values():
                return projected(list(zip(wv, STREAMS)), cT)

            def values():
                for q in two:
                    for w in two:
                        n = transposes([vT[:, 4 * w + j, q, :] for j in range(4)])
                return n

            def distances(p):
                for u in two:
                    n, bank = turn()
                    for j in range(MS):
                        ins = nc.tensor.matmul(bank[:, j * 2 * NREL:(j + 1) * 2 * NREL], qT[:, u * MS + j, p, :], relk[:, :],
                                               start=True, stop=True)
                    ins.then_inc(g["filled"], 1)

            def scores(b, p):
                for h in two:
                    since(pe, g["s_sub"], 2 * (b - 1) + h + 1)
                    for j in range(MS):
                        for a in two:
                            r = slice(a * DH1, (a + 1) * DH1)
                            m = h * MS + j
                            ins = nc.tensor.matmul(S[:, h * HS + a * MS + j, :], qT[r, m, p, :], kT[r, m, p, :], start=True, stop=True)
                    ins.then_inc(g["s_mm"], 1)

            def attend(b, p):
                def probabilities(k):
                    pe.wait_ge(g["soft"], 2 * b + k // 2 + 1)
                    return transposes([soft[p][:, 4 * k + j, :] for j in range(4)])

                def weighted(k, n):
                    taken(n)
                    if k == 0:
                        since(pe, g["x3"], b)
                    for j in range(4):
                        head = 4 * k + j
                        m, a = head // 2, head % 2
                        ins = nc.tensor.matmul(O[m // MS][a * DH1:(a + 1) * DH1, m % MS, :],
                                               v[p][:, head * DH1:(head + 1) * DH1], pT[k % 2][:, j, :],
                                               start=(m % MS == 0), stop=False, skip_group_check=True)
                    ins.then_inc(g["pv_mm"], 1)

                n = [probabilities(0), probabilities(1)]
                for k in range(4):
                    weighted(k, n[k])
                    if k < 2:
                        n.append(probabilities(k + 2))

            def bands(b, i, p):
                pe.wait_ge(g["bandv"], b + 1)
                pe.wait_ge(s_pin[p], 16 * (i + 1))
                for h in two:
                    n = transposes([band[p][:, 2 * m:2 * m + 2, :].rearrange("p h r -> p (h r)") for m in range(h * MS, (h + 1) * MS)])
                return n

            def distance_values(n_bands):
                taken(n_bands)
                for m in range(MT1):
                    ins = nc.tensor.matmul(O[m // MS][:, m % MS, :], relv[:, :], bandT[:, m, :], start=False,
                                           stop=(m % MS == MS - 1), skip_group_check=True)
                    if m % MS == MS - 1:
                        ins.then_inc(g["o_mm"], 1)

            def output(b):
                pe.wait_ge(g["o_sb"], 2 * b + 2)
                y = O[0][:, 0:KD, :].rearrange("p k n -> p (k n)")
                for m in range(MT1):
                    ins = nc.tensor.matmul(y, attT[:, m, :], wo[:, m, :], start=(m == 0), stop=(m == MT1 - 1))
                ins.then_inc(g["y_mm"], 1)

            context(0)
            taken(queries(rows(0)))
            distances(0)
            keys()
            pe.wait_ge(s_late, 32)
            transposed_values()

            def steps(b, i, p, first, last):
                turns.begin(b, p)
                scores(b, p)
                if not first:
                    n_bands = bands(b - 1, i - 1 + p, 1 - p)
                if p == 0:
                    if not last_pair(i):
                        context(i + 1)
                    values()
                    if not first:
                        distance_values(n_bands)
                    distances(1)
                    if not first:
                        output(b - 1)
                    if not last_pair(i):
                        transposed_values()
                else:
                    if not last_pair(i):
                        n_rows = rows(i + 1)
                    distance_values(n_bands)
                    if not last_pair(i):
                        n_queries = queries(n_rows)
                    output(b - 1)
                    if not last_pair(i):
                        taken(n_queries)
                        distances(0)
                        keys()
                attend(b, p)

            by_batch(steps)(pe)
            distance_values(bands(NB - 1, NPAIR - 1, 1))
            output(NB - 1)

        @block.vector
        def _(dve):
            dve.wait_ge(s_setup, 1)
            nc.vector.memset(coef[:, 0, :], 1.0).then_inc(s_alpha, 1)
            for s in range(1, NS):
                nc.vector.tensor_scalar(coef[:, s, :], tanhs[:, s - 1:s].to_broadcast([P, NH]), 1.0, None, ALU.add).then_inc(s_alpha, 1)
            dve.wait_ge(s_alpha, NS)
            front = Link(dve, l_front, 2)
            soft_l = [Link(dve, l, 2) for l in l_softs]
            sum_l = Link(dve, l_sum, 2)

            def pick_rows(b, i, p):
                since(dve, s_pick[p], 32 * i)
                nc.vector.tensor_copy(pick[p][:, :], shared["tile_rows"][:, bass.ds(b, 1), :].rearrange("p o k -> p (o k)"))\
                    .then_inc(g["pick"], 1)

            def rows(b, i, p):
                front.begin(b)
                dve.wait_ge(s_in[p], 32 * (i + 1))
                dve.wait_ge(s_pick[p], 32 * (i + 1))
                w = [shared["weights"][:, bass.ds(b, 1), k:k + 1].rearrange("p o k -> p (o k)") for k in range(TOPK)]
                front(nc.vector.scalar_tensor_tensor(x_in[p][:, :], picked[p][0][:, :], w[0], x_in[p][:, :], ALU.mult, ALU.add))
                since(dve, g["x2b"], b - 1)
                nc.vector.scalar_tensor_tensor(x2[p][:, :], picked[p][1][:, :], w[1], x_in[p][:, :], ALU.mult, ALU.add)\
                    .then_inc(g["x2"], 1)
                dve.wait_ge(g["x2"], b + 1)
                front(nc.vector.bn_stats(stat[p][:, :], x2[p][:, :]))
                front.end()
                nc.vector.bn_aggr(agg[p][:, :], stat[p][:, :]).then_inc(g["var"], 1)

            def rows_normal(b, p):
                dve.wait_ge(g["rstd"], b + 1)
                nc.vector.tensor_scalar(xn[p][:, :], x2[p][:, :], agg[p][:, 0:1], rstd[p][:, 1:2], ALU.subtract, ALU.mult)\
                    .then_inc(g["xn"], 1)

            def by_head(a):
                return a.rearrange("p (u m) n -> p m u n", u=2)

            def paired(a):
                return a.rearrange("p (m u) n -> p m u n", u=2)

            def less_max(b, i, p, h):
                lk = soft_l[h]
                lk.begin(b)
                hs = slice(h * HS, (h + 1) * HS)
                dve.wait_ge(s_relin[p], 16 * (i + 1))
                since(dve, s_pout[p], 16 * i)
                since(dve, g["tails"], b - 1)
                dve.wait_ge(g["s_mm"], 2 * b + h + 1)
                for s, (a, z) in enumerate(STREAMS):
                    m = top[:, s, hs].rearrange("p (m u) -> p m u", u=2)
                    if s == 0:
                        lk(nc.vector.tensor_tensor(paired(soft[p][:, hs, a:z]), by_head(S[:, hs, a:z]), paired(bias[p][:, hs, :]), ALU.add))
                        nc.vector.tensor_reduce(m, paired(soft[p][:, hs, a:z]), X, ALU.max)
                    else:
                        ins = nc.vector.tensor_reduce(m, by_head(S[:, hs, a:z]), X, ALU.max)
                lk(ins)
                for s, (a, z) in enumerate(STREAMS):
                    src = by_head(S[:, hs, a:z]) if s else paired(soft[p][:, hs, a:z])
                    m = top[:, s, hs].rearrange("p (m u) -> p m u", u=2).unsqueeze(3).to_broadcast([P, MS, 2, z - a])
                    ins = nc.vector.tensor_tensor(paired(soft[p][:, hs, a:z]), src, m, ALU.subtract)
                lk.end()
                ins.then_inc(g["s_sub"], 1)

            def shares(b, p, h):
                hs = slice(h * HS, (h + 1) * HS)
                sum_l.begin(2 * b + h)
                dve.wait_ge(g["s_exp"], 2 * b + h + 1)
                for s, (a, z) in enumerate(STREAMS):
                    ins = nc.vector.tensor_reduce(total[:, s, hs], soft[p][:, hs, a:z], X, ALU.add)
                sum_l(ins)
                since(dve, g["soft"], 2 * b + h - 1)
                sum_l(nc.vector.reciprocal(share[:, :, hs], total[:, :, hs]))
                nc.vector.tensor_tensor(share[:, :, hs], share[:, :, hs], coef[:, :, hs], ALU.mult).then_inc(g["share"], 1)
                sum_l.end()

            def ends(b, p):
                dve.wait_ge(g["tails"], b + 1)
                nc.vector.tensor_reduce(band[p][:, :, 0], near[:, :, :], X, ALU.add)
                nc.vector.tensor_reduce(band[p][:, :, NREL - 1], far[:, :, :], X, ALU.add).then_inc(g["bandv"], 1)

            def output(b, i, p):
                dve.wait_ge(g["y_mm"], b + 1)
                dve.wait_ge(g["x2b"], b + 1)
                since(dve, s_x3[p], 16 * i)
                y = O[0][:, 0:KD, :].rearrange("p k n -> p (k n)")
                nc.vector.tensor_tensor(x3[p][:, :], y, x2b[p][:, :], ALU.add).then_inc(g["x3"], 1)

            for p in two:
                pick_rows(p, 0, p)
            for p in two:
                rows(p, 0, p)
            for p in two:
                rows_normal(p, p)

            def steps(b, i, p, first, last):
                ahead = p == 0 and not last_pair(i)
                if ahead:
                    for q in two:
                        pick_rows(b + 2 + q, i + 1, q)
                for h in range(2):
                    less_max(b, i, p, h)
                for h in range(2):
                    shares(b, p, h)
                if not first:
                    output(b - 1, i - 1 + p, 1 - p)
                if ahead:
                    for q in two:
                        rows(b + 2 + q, i + 1, q)
                    for q in two:
                        rows_normal(b + 2 + q, q)
                ends(b, p)

            by_batch(steps)(dve)
            output(NB - 1, NPAIR - 1, 1)


HID = 1024
MH = HID // P
W_N = D * HID
LEVELS = 127.0
FLOOR = 1e-5
ROUND = 1.5 * 2.0 ** 23


def feed_forward(nc, t, shared, out):
    with ExitStack() as ctx:
        def sb(name, shape, dt=F32):
            return ctx.enter_context(nc.sbuf_tensor(name, shape, dt))

        def ps(name, shape, dt=F32):
            return ctx.enter_context(nc.psum_tensor(name, shape, dt))

        def sem(name):
            shared["semaphores"].append(nc.alloc_semaphore(name=name))
            return shared["semaphores"][-1]

        const = shared["const"]

        def cst(name):
            a, z = CONST_AT[name]
            return const[:, a:z]

        ident, ones = cst("ident"), cst("ones")
        two = range(2)
        wf = [sb(f"d_wf{k}", [P, W_N // P]) for k in two]
        wi = [sb(f"d_wi{k}", [P, W_N // P], BF16) for k in two]
        w1, w2 = wi[0][:, :].rearrange("p (k n) -> p k n", k=KD), wi[1][:, :].rearrange("p (k n) -> p k n", k=MH)
        ident_b = sb("d_ident", [P, P], BF16)
        taps = sb("d_taps", [P, MH, 3])
        cbias = sb("d_cbias", [P, MH])
        wsum = sb("d_wsum", [P, 2])
        wunit = sb("d_wunit", [P, 2])
        wscale = sb("d_wscale", [P, 2])
        x_in = [sb(f"d_x{p}", [P, D]) for p in two]
        stat = sb("d_stat", [P, 6])
        agg = sb("d_agg", [P, 2])
        rstd = sb("d_rstd", [P, 2])
        xn = sb("d_xn", [P, D])
        peak = sb("d_peak", [P, 4])
        unit = sb("d_unit", [P, 2])
        rnd = sb("d_rnd", [P, D])
        xi = [sb(f"d_xi{p}", [P, D], BF16) for p in two]
        diag = [sb(f"d_diag{k}", [P, P]) for k in two]
        xiT = sb("d_xiT", [P, KD, P], BF16)
        row = [sb(f"d_row{k}", [P, P]) for k in two]
        hp = [sb(f"d_hp{p}", [P, MH, P + 2]) for p in two]
        conv = [sb(f"d_conv{p}", [P, MH, P]) for p in two]
        gi = sb("d_gi", [P, MH, P], BF16)
        step = sb("d_step", [P, 1])
        res = [sb(f"d_res{p}", [P, D]) for p in two]
        XT = ps("d_XT", [P, KD, P], BF16)
        H = ps("d_H", [P, MH, P])
        B = ps("d_B", [P, 2 * P])
        GT = ps("d_GT", [P, HID])
        Y = ps("d_Y", [P, D])

        s_w = sem("d_weights")
        s_pad = sem("d_pad")
        s_id = sem("d_id")
        s_tot = sem("d_tot")
        s_wi = sem("d_wi")
        l_w, l_front, l_conv, l_q = (sem("dl_" + n) for n in "weights front conv quant".split())
        l_pool = sem("dl_pool")
        s_in = [sem(f"d_in{p}") for p in two]
        s_out = [sem(f"d_out{p}") for p in two]
        names = "var rstd xn xi xt_mm xt_sb row_mm row_sb h_mm h tap conv silu gt_mm peak2 diag2 row2_mm row2_sb gi y_mm y"
        g = {n: sem("d_" + n) for n in names.split()}

        W = [(wf[0][:, :].rearrange("p (k n) -> p k n", k=KD), t["L1_w1T"].rearrange("(k p) n -> p k n", p=P)),
             (wf[1][:, :].rearrange("p (k n) -> p k n", k=MH), t["L1_w2T"].rearrange("(k p) n -> p k n", p=P)),
             (taps[:, :, :], t["L1_conv_w"].rearrange("(m p) k -> p m k", p=P)),
             (cbias[:, :], t["L1_conv_b"])]
        W_READY = 16 * len(W)

        def by_batch(steps):
            def run(eng):
                for b in range(2):
                    steps(b, 0, b, b == 0, False)
                with eng.Fori(1, NB // 2 - 1) as i:
                    for p in range(2):
                        steps(i * 2 + p, i, p, False, False)
                for p in range(2):
                    steps(NB - 2 + p, NB // 2 - 1, p, False, p == 1)
            return run

        def rows_of(d, b):
            return d[bass.ds(b, 1)].rearrange("o p d -> (o p) d")

        block = ctx.enter_context(nc.Block())

        @block.sync
        def _(sp):
            def load(b, i, p):
                since(sp, g["y"], b - 1)
                sp.dma_start(x_in[p][:, :], rows_of(t["x3"], b)).then_inc(s_in[p], 16)

            def store(b, p):
                sp.wait_ge(g["y"], b + 1)
                sp.dma_start(rows_of(out, b), res[p][:, :]).then_inc(s_out[p], 16)

            load(0, 0, 0)
            load(1, 0, 1)

            def steps(b, i, p, first, last):
                store(b, p)
                if not (isinstance(b, int) and b + 2 >= NB):
                    load(b + 2, i + 1, p)

            by_batch(steps)(sp)
            for p in two:
                sp.wait_ge(s_out[p], 16 * (NB // 2))

        @block.gpsimd
        def _(pool):
            for p in two:
                nc.gpsimd.memset(hp[p][:, :, 0:1], 0.0).then_inc(s_pad, 1)
                nc.gpsimd.memset(hp[p][:, :, P + 1:P + 2], 0.0).then_inc(s_pad, 1)
            nc.gpsimd.tensor_copy(ident_b[:, :], ident).then_inc(s_id, 1)
            lk = Link(pool, l_pool, 1)

            def inverse_std(b):
                apart(pool, g["var"], b + 1)
                lk.begin(b)
                lk(nc.gpsimd.tensor_scalar(rstd[:, 0:1], agg[:, 1:2], EPS, None, ALU.add))
                nc.gpsimd.tensor_tensor(rstd[:, 1:2], rstd[:, 0:1], shared["mhalf"][:, :], ALU.pow).then_inc(g["rstd"], 1)

            by_batch(lambda b, *_: inverse_std(b))(pool)

        @block.scalar
        def _(act):
            for dst, src in W:
                act.dma_start(dst, src).then_inc(s_w, 16)
            act.wait_ge(s_w, W_READY)

            def front(b):
                act.wait_ge(g["xt_mm"], b + 1)
                since(act, g["h_mm"], b)
                nc.scalar.activation(xiT[:, :, :], XT[:, :, :], ACT.Copy).then_inc(g["xt_sb"], 1)
                act.wait_ge(g["row_mm"], b + 1)
                since(act, g["h"], b)
                nc.scalar.activation(row[0][:, :], B[:, 0:P], ACT.Copy).then_inc(g["row_sb"], 1)

            def middle_tap(b, p):
                act.wait_ge(g["h"], b + 1)
                since(act, g["gt_mm"], b - 1)
                since(act, g["gi"], b - 1)
                for m in range(MH):
                    ins = nc.scalar.activation(conv[p][:, m, :], hp[p][:, m, 1:P + 1], ACT.Identity,
                                               bias=cbias[:, m:m + 1], scale=taps[:, m, 1:2])
                ins.then_inc(g["tap"], 1)

            def activate(b, p):
                act.wait_ge(g["conv"], b + 1)
                nc.scalar.activation(conv[p][:, :, :], conv[p][:, :, :], ACT.Silu).then_inc(g["silu"], 1)

            def second(b):
                act.wait_ge(g["row2_mm"], b + 1)
                since(act, g["gi"], b)
                nc.scalar.activation(row[1][:, :], B[:, P:2 * P], ACT.Copy).then_inc(g["row2_sb"], 1)

            front(0)
            middle_tap(0, 0)

            def steps(b, i, p, first, last):
                activate(b, p)
                if not last:
                    front(b + 1)
                second(b)
                if not last:
                    middle_tap(b + 1, 1 - p)

            by_batch(steps)(act)

        @block.tensor
        def _(pe):
            pe.wait_ge(s_id, 1)
            pe.wait_ge(l_w, 2)
            nc.tensor.matmul(Y[:, 0:2], ones, wsum[:, :], start=True, stop=True).then_inc(s_tot, 1)
            pe.wait_ge(s_wi, 2)

            def front(b, i, p):
                pe.wait_ge(g["xi"], b + 1)
                since(pe, g["xt_sb"], b)
                for c in range(KD):
                    ins = nc.tensor.transpose(XT[:, c, :], xi[p][:, c * P:(c + 1) * P], ident_b[:, :])
                ins.then_inc(g["xt_mm"], 1)
                since(pe, g["row2_sb"], b - 1)
                nc.tensor.matmul(B[:, 0:P], ones, diag[0][:, :], start=True, stop=True).then_inc(g["row_mm"], 1)
                pe.wait_ge(g["xt_sb"], b + 1)
                since(pe, g["h"], b)
                for m in range(MH):
                    for c in range(KD):
                        ins = nc.tensor.matmul(H[:, m, :], w1[:, c, m * P:(m + 1) * P], xiT[:, c, :], start=(c == 0), stop=(c == KD - 1))
                ins.then_inc(g["h_mm"], 1)

            front(0, 0, 0)

            def steps(b, i, p, first, last):
                pe.wait_ge(g["silu"], b + 1)
                since(pe, g["peak2"], b)
                for m in range(MH):
                    ins = nc.tensor.transpose(GT[:, m * P:(m + 1) * P], conv[p][:, m, :], ident)
                ins.then_inc(g["gt_mm"], 1)
                if not last:
                    front(b + 1, i + p, 1 - p)
                pe.wait_ge(g["diag2"], b + 1)
                if not last:
                    pe.wait_ge(g["row_sb"], b + 2)
                nc.tensor.matmul(B[:, P:2 * P], ones, diag[1][:, :], start=True, stop=True).then_inc(g["row2_mm"], 1)
                pe.wait_ge(g["gi"], b + 1)
                since(pe, g["y"], b)
                for m in range(MH):
                    ins = nc.tensor.matmul(Y[:, :], gi[:, m, :], w2[:, m, :], start=(m == 0), stop=(m == MH - 1))
                ins.then_inc(g["y_mm"], 1)

            by_batch(steps)(pe)

        @block.vector
        def _(dve):
            dve.wait_ge(s_w, W_READY)
            wl = Link(dve, l_w, 8)
            for k in two:
                wl(nc.vector.tensor_reduce(wsum[:, k:k + 1], wf[k][:, :], X, ALU.add, apply_absolute_value=True))
            dve.wait_ge(s_tot, 1)
            wl(nc.vector.tensor_scalar(wunit[:, :], Y[:, 0:2], 1.0 / W_N, FLOOR, ALU.mult, ALU.max))
            wl(nc.vector.reciprocal(wscale[:, :], wunit[:, :]))
            for k in two:
                wl(nc.vector.tensor_scalar(wf[k][:, :], wf[k][:, :], wscale[:, k:k + 1], ROUND, ALU.mult, ALU.add))
                wl(nc.vector.tensor_scalar(wf[k][:, :], wf[k][:, :], -ROUND, -1.0, ALU.add, ALU.max))
                nc.vector.tensor_scalar(wi[k][:, :], wf[k][:, :], 1.0, None, ALU.min).then_inc(s_wi, 1)
            dve.wait_ge(s_wi, 2)
            front_l, conv_l, quant_l = Link(dve, l_front, 7), Link(dve, l_conv, 1), Link(dve, l_q, 5)

            def front(b, i, p):
                front_l.begin(b)
                dve.wait_ge(s_in[p], 16 * (i + 1))
                front_l(nc.vector.bn_stats(stat[:, :], x_in[p][:, :]))
                nc.vector.bn_aggr(agg[:, :], stat[:, :]).then_inc(g["var"], 1)
                dve.wait_ge(g["rstd"], b + 1)
                front_l(nc.vector.tensor_scalar(xn[:, :], x_in[p][:, :], agg[:, 0:1], rstd[:, 1:2], ALU.subtract, ALU.mult))
                front_l(nc.vector.tensor_reduce(peak[:, 0:1], xn[:, :], X, ALU.max, apply_absolute_value=True))
                front_l(nc.vector.tensor_scalar(unit[:, 0:1], peak[:, 0:1], FLOOR, 1.0 / LEVELS, ALU.max, ALU.mult))
                front_l(nc.vector.reciprocal(peak[:, 1:2], unit[:, 0:1]))
                front_l(nc.vector.tensor_scalar(rnd[:, :], xn[:, :], peak[:, 1:2], LEVELS, ALU.mult, ALU.min))
                front_l(nc.vector.tensor_scalar(rnd[:, :], rnd[:, :], -LEVELS - 1.0, ROUND, ALU.max, ALU.add))
                front_l.end()
                since(dve, g["xt_mm"], b - 1)
                nc.vector.tensor_scalar(xi[p][:, :], rnd[:, :], -ROUND, None, ALU.add)
                since(dve, g["row_mm"], b)
                nc.vector.tensor_scalar(diag[0][:, :], ident, unit[:, 0:1], wunit[:, 0:1], ALU.mult, ALU.mult).then_inc(g["xi"], 1)

            def hidden(b, i, p):
                dve.wait_ge(g["h_mm"], b + 1)
                dve.wait_ge(g["row_sb"], b + 1)
                if isinstance(b, int) and b < 2:
                    dve.wait_ge(s_pad, 4)
                nc.vector.tensor_tensor(hp[p][:, :, 1:P + 1], H[:, :, :], row[0][:, :].unsqueeze(1).to_broadcast([P, MH, P]), ALU.mult)\
                    .then_inc(g["h"], 1)

            def convolve(b, i, p):
                conv_l.begin(b)
                dve.wait_ge(g["tap"], b + 1)
                dve.wait_ge(g["h"], b + 1)
                for k in (0, 2):
                    for m in range(MH):
                        ins = nc.vector.scalar_tensor_tensor(conv[p][:, m, :], hp[p][:, m, k:k + P], taps[:, m, k:k + 1],
                                                             conv[p][:, m, :], ALU.mult, ALU.add)
                    if k == 0:
                        conv_l(ins)
                ins.then_inc(g["conv"], 1)

            def quantise(b, i, p):
                quant_l.begin(b)
                dve.wait_ge(g["gt_mm"], b + 1)
                nc.vector.tensor_reduce(peak[:, 2:3], GT[:, :], X, ALU.max, apply_absolute_value=True).then_inc(g["peak2"], 1)
                dve.wait_ge(g["peak2"], b + 1)
                quant_l(nc.vector.tensor_scalar(unit[:, 1:2], peak[:, 2:3], FLOOR, 1.0 / LEVELS, ALU.max, ALU.mult))
                quant_l(nc.vector.reciprocal(peak[:, 3:4], unit[:, 1:2]))
                since(dve, g["row2_mm"], b)
                nc.vector.tensor_scalar(diag[1][:, :], ident, peak[:, 3:4], None, ALU.mult).then_inc(g["diag2"], 1)
                quant_l(nc.vector.tensor_scalar(step[:, :], unit[:, 1:2], wunit[:, 1:2], None, ALU.mult))
                dve.wait_ge(g["row2_sb"], b + 1)
                quant_l(nc.vector.tensor_tensor(conv[p][:, :, :], conv[p][:, :, :], row[1][:, :].unsqueeze(1).to_broadcast([P, MH, P]), ALU.mult))
                quant_l(nc.vector.tensor_scalar(conv[p][:, :, :], conv[p][:, :, :], LEVELS, -LEVELS - 1.0, ALU.min, ALU.max))
                quant_l.end()
                since(dve, g["y_mm"], b)
                nc.vector.tensor_scalar(gi[:, :, :], conv[p][:, :, :], ROUND, -ROUND, ALU.add, ALU.add).then_inc(g["gi"], 1)

            def output(b, i, p):
                dve.wait_ge(g["y_mm"], b + 1)
                since(dve, s_out[p], 16 * i)
                nc.vector.scalar_tensor_tensor(res[p][:, :], Y[:, :], step[:, 0:1], x_in[p][:, :], ALU.mult, ALU.add)\
                    .then_inc(g["y"], 1)

            front(0, 0, 0)
            hidden(0, 0, 0)
            convolve(0, 0, 0)
            front(1, 0, 1)

            def steps(b, i, p, first, last):
                quantise(b, i, p)
                if not last:
                    hidden(b + 1, i + p, 1 - p)
                    convolve(b + 1, i + p, 1 - p)
                output(b, i, p)
                if not (isinstance(b, int) and b + 2 >= NB):
                    front(b + 2, i + 1, p)

            by_batch(steps)(dve)


def layer1(nc, t, shared, out):
    attention1(nc, t, shared)
    feed_forward(nc, t, shared, out)


def release_semaphores(nc, shared):
    nc.clear_and_free_semaphores(shared["semaphores"])
    nc.all_engine_barrier()
    shared["semaphores"] = []


def build(nc, t, out, phases="ABC"):
    with ExitStack() as ctx:
        def sb(name, shape, dt=F32):
            return ctx.enter_context(nc.sbuf_tensor(name, shape, dt))

        shared = {
            "const": sb("const", [P, CONST_W]),
            "mhalf": sb("mhalf", [P, 1]),
            "onehot": sb("onehot", [P, NB, TOPK, NE]),
            "slots": sb("slots", [P, NB, TOPK]),
            "weights": sb("weights", [P, NB, TOPK]),
            "tile_rows": sb("tile_rows", [P, NB, TOPK], I32),
            "tile_expert": sb("tile_expert", [P, N_TILES], I32),
            "tile_row": sb("tile_row", [P, N_TILES], I32),
            "semaphores": [],
            "s_experts": ctx.enter_context(nc.semaphore("s_experts")),
            "s_layer1": ctx.enter_context(nc.semaphore("s_layer1")),
            "early": sb("early", [P, len(L1_EARLY) * KD * INNER]),
        }
        size = KD * INNER
        shared["layer1"] = weights = {}
        for n, name in enumerate(L1_EARLY):
            weights[name] = shared["early"][:, n * size:(n + 1) * size].rearrange("p (k n) -> p k n", n=INNER)

        def load_layer1(eng):
            for name, dst in weights.items():
                eng.dma_start(dst, t["L1_" + name].rearrange("(k p) n -> p k n", p=P)).then_inc(shared["s_layer1"], 16)

        shared["load_layer1"] = load_layer1
        t["lists"] = nc.dram_tensor("expert_lists", (NE * ROWS_E, D), F32, kind="Internal").ap()
        t["expert_out"] = nc.dram_tensor("expert_out", (N_TILES * P, D), F32, kind="Internal").ap()
        t["x1"] = nc.dram_tensor("rows_after_attention", (NB, P, D), F32, kind="Internal").ap()
        t["x3"] = nc.dram_tensor("rows_after_attention_1", (NB, P, D), F32, kind="Internal").ap()
        with ExitStack() as moe:
            for name, shape in (("w1", [P, NE, KD, 2 * HE]), ("w2", [P, NE, KH, D]), ("b1", [P, NE, 2 * HE]), ("b2", [P, NE, D])):
                shared[name] = moe.enter_context(nc.sbuf_tensor("moe_" + name, shape, F32))

            def load_experts(eng):
                s = shared["s_experts"]
                eng.dma_start(shared["b1"][:, :, :], t["L0_bl1"].partition_broadcast(P)).then_inc(s, 16)
                eng.dma_start(shared["b2"][:, :, :], t["L0_bl2"].partition_broadcast(P)).then_inc(s, 16)
                eng.dma_start(shared["w1"][:, :, :, :], t["L0_Wl1"].rearrange("e (k p) n -> p e k n", p=P)).then_inc(s, 16)
                eng.dma_start(shared["w2"][:, :, :, :], t["L0_Wl2"].rearrange("e (k p) n -> p e k n", p=P)).then_inc(s, 16)

            shared["load_experts"] = load_experts
            layer0(nc, t, shared)
            release_semaphores(nc, shared)
            experts(nc, t, shared)
        layer1(nc, t, shared, out)


def strip_columns(w):
    a = np.zeros((w.shape[1], NH, STRIP), w.dtype)
    a[:, :, :DH0] = w.T.reshape(w.shape[1], NH, DH0)
    return a.reshape(w.shape[1], NH * STRIP)


def strip_bias(b, mask_row):
    a = np.zeros((NH, STRIP), b.dtype)
    a[:, :DH0] = b.reshape(NH, DH0)
    a[:, DH0] = mask_row
    return np.ascontiguousarray(a.reshape(MT0, P).T)


def pair_blocks(a):
    r, c = a.shape
    z = np.zeros((2 * r, 2 * c), a.dtype)
    z[:r, :c] = a
    z[r:, c:] = a
    return z


def layout1(L1_xattn_Wq, L1_xattn_Wk, L1_xattn_Wv, L1_xattn_Wk_ip, L1_xattn_Wv_ip, L1_xattn_Wk_ap, L1_xattn_Wv_ap, L1_xattn_Wo,
            L1_xattn_bo, L1_xattn_rel_k, L1_xattn_rel_v, L1_xattn_alpha, L1_xattn_beta, L1_ffn_w1, L1_ffn_conv_w, L1_ffn_conv_b,
            L1_ffn_w2):
    return {
        "L1_Wq": L1_xattn_Wq, "L1_Wk0": L1_xattn_Wk, "L1_Wk1": L1_xattn_Wk_ip, "L1_Wk2": L1_xattn_Wk_ap,
        "L1_Wv0": L1_xattn_Wv, "L1_Wv1": L1_xattn_Wv_ip, "L1_Wv2": L1_xattn_Wv_ap, "L1_Wo": L1_xattn_Wo, "L1_bo": L1_xattn_bo,
        "L1_relk": pair_blocks(L1_xattn_rel_k.T), "L1_relv": pair_blocks(L1_xattn_rel_v),
        "L1_alphas": np.stack([L1_xattn_alpha, L1_xattn_beta]),
        "L1_w1T": L1_ffn_w1.T, "L1_w2T": L1_ffn_w2.T, "L1_conv_w": L1_ffn_conv_w.reshape(HID, 3),
        "L1_conv_b": L1_ffn_conv_b.reshape(MH, P).T,
    }


def layout(x, ctx_1024, mask_Bx1x1xS2_ik0, L0_xattn_Wq, L0_xattn_bq, L0_xattn_Wk, L0_xattn_bk, L0_xattn_Wv, L0_xattn_bv,
           L0_xattn_gamma, L0_xattn_beta, L0_ffn_Wr, L0_ffn_br, L0_ffn_Wl1, L0_ffn_bl1, L0_ffn_Wl2, L0_ffn_bl2,
           L0_ffn_biases_N, **layer1_inputs):
    c = np.ascontiguousarray
    arrays = {
        "x": x, "ctx": ctx_1024, "mask": mask_Bx1x1xS2_ik0.reshape(NB, P),
        "L0_wqT": strip_columns(L0_xattn_Wq), "L0_wkT": strip_columns(L0_xattn_Wk), "L0_wvT": c(L0_xattn_Wv.T),
        "L0_wrT": c(L0_ffn_Wr.T),
        "L0_bq": strip_bias(L0_xattn_bq, 1.0 / SCALE0), "L0_bk": strip_bias(L0_xattn_bk, MASKED), "L0_bv": L0_xattn_bv,
        "L0_gamma": L0_xattn_gamma, "L0_beta": L0_xattn_beta, "L0_br": L0_ffn_br, "L0_pick_bias": L0_ffn_biases_N,
        "L0_Wl1": L0_ffn_Wl1, "L0_bl1": L0_ffn_bl1, "L0_Wl2": L0_ffn_Wl2, "L0_bl2": L0_ffn_bl2,
        "const": np.concatenate(list(CONST.values()), axis=1),
    }
    arrays.update(layout1(**layer1_inputs))
    return {n: c(a) for n, a in arrays.items()}


def kernel(**inputs):
    import concourse.bacc as bacc
    from concourse.bass_utils import run_bass_kernel_spmd

    nc = bacc.Bacc("TRN2", target_bir_lowering=False, num_devices=1)
    arrays = layout(**{n: np.asarray(a) for n, a in inputs.items()})
    t = {n: nc.dram_tensor("in_" + n, a.shape, mybir.dt.from_np(a.dtype), kind="ExternalInput").ap() for n, a in arrays.items()}
    out = nc.dram_tensor("out", (NB, P, D), F32, kind="ExternalOutput").ap()
    build(nc, t, out)
    result = run_bass_kernel_spmd(nc, [{"in_" + n: a for n, a in arrays.items()}], core_ids=[0])
    return result.results[0]["out"]
```

```python
from contextlib import ExitStack

import numpy as np

import concourse.bass as bass
from concourse import mybir

F32 = mybir.dt.float32
BF16 = mybir.dt.bfloat16
I32 = mybir.dt.int32
U32 = mybir.dt.uint32
ALU = mybir.AluOpType
ACT = mybir.ActivationFunctionType
X = mybir.AxisListType.X

P = 128
NB = 16
D = 256
KD = D // P
NH = 16

DH0 = D // NH
STRIP = 32
HPT = P // STRIP
MT0 = NH // HPT
SCALE0 = 1.0 / DH0 ** 0.5
MASKED = -1.0e9
EPS0 = 1e-6
EPS = 1e-5

TEXT, IMG = 77, 16
MAXREL = 16
BANDW = P + 2 * MAXREL

NE = 8
TOPK = 2
HE = 512
KH = HE // P
ROWS_E = NB * P + P
N_TILES = (NB * P * TOPK + NE * (P - 1)) // P


class Link:

    def __init__(self, eng, sem, per):
        self.eng, self.sem, self.per, self.n, self.base = eng, sem, per, 0, 0

    def begin(self, b):
        self.base, self.n = b * self.per, 0

    def add(self, ins):
        ins.then_inc(self.sem, 1)
        self.n += 1
        assert self.n <= self.per, self.n
        return self.base + self.n

    def wait(self, count):
        apart(self.eng, self.sem, count)

    def __call__(self, ins):
        self.wait(self.add(ins))

    def end(self):
        assert self.n == self.per, (self.n, self.per)


def since(eng, sem, count):
    if isinstance(count, int) and count <= 0:
        return
    eng.wait_ge(sem, count)


def apart(eng, sem, count):
    if not isinstance(count, int):
        count = eng.to_reg(count)
        eng.wait_ge(sem, 1)
    since(eng, sem, count)


def constants():
    c = {}
    c["ident"] = np.eye(P, dtype=np.float32)
    c["before"] = np.triu(np.ones((P, P), np.float32), 1)
    c["ones"] = np.ones((P, P), np.float32)
    aug = np.zeros((P, 1), np.float32)
    aug[DH0::STRIP] = 1.0
    c["aug"] = aug
    e = np.arange(NE, dtype=np.float32)
    c["expert"] = np.tile(e, (P, 1))
    c["list"] = np.tile(e * ROWS_E, (P, 1))
    c["sizes"] = np.tile(np.arange(NB, dtype=np.float32) * P, (P, 1))
    c["upto"] = np.tile((e[None, :] <= e[:, None]).astype(np.float32).reshape(1, -1), (P, 1))
    c["tiles"] = np.tile(np.arange(N_TILES, dtype=np.float32), (P, 1))
    i, j = np.arange(P)[:, None], np.arange(TEXT)[None, :]
    c["before_band"] = (j - i <= -MAXREL).astype(np.float32)
    c["behind_band"] = (j - i >= MAXREL).astype(np.float32)
    return c


CONST = constants()
CONST_AT = {}
_at = 0
for _name, _a in CONST.items():
    CONST_AT[_name] = (_at, _at + _a.shape[1])
    _at += _a.shape[1]
CONST_W = _at


def layer0(nc, t, shared):
    with ExitStack() as ctx:
        early, used = shared["early"], [0]

        def sb(name, shape, dt=F32):
            n = int(np.prod(shape[1:]))
            if dt != F32 or used[0] + n > early.shape[1]:
                return ctx.enter_context(nc.sbuf_tensor(name, shape, dt))
            a = early[:, used[0]:used[0] + n]
            used[0] += n
            if len(shape) == 3:
                a = a.rearrange("p (a b) -> p a b", a=shape[1])
            if len(shape) == 4:
                a = a.rearrange("p (a b c) -> p a b c", a=shape[1], b=shape[2])
            return a

        def ps(name, shape, dt=F32):
            return ctx.enter_context(nc.psum_tensor(name, shape, dt))

        def sem(name):
            shared["semaphores"].append(nc.alloc_semaphore(name=name))
            return shared["semaphores"][-1]

        const = shared["const"]

        def cst(name):
            a, z = CONST_AT[name]
            return const[:, a:z]

        ident, before, ones = cst("ident"), cst("before"), cst("ones")
        wq = sb("a_wq", [P, KD, MT0 * P])
        wk = sb("a_wk", [P, KD, MT0 * P])
        wv = sb("a_wv", [P, KD, D])
        wr = sb("a_wr", [P, KD, NE])
        bq = sb("a_bq", [P, MT0])
        bqs = sb("a_bqs", [P, MT0])
        bk = sb("a_bk", [P, MT0])
        bv = sb("a_bv", [P, D])
        gamma = sb("a_gamma", [P, D])
        beta = sb("a_beta", [P, D])
        br = sb("a_br", [P, NE])
        pick_bias = sb("a_pick_bias", [P, NE])
        zeros = sb("a_zeros", [P, D])

        x_in = [sb(f"a_x{p}", [P, D]) for p in range(2)]
        cT = [sb(f"a_cT{p}", [P, KD, P]) for p in range(2)]
        mask_in = [sb(f"a_mask{p}", [P, P], I32) for p in range(2)]
        x_res = [sb(f"a_xr{p}", [P, D]) for p in range(2)]
        c_res = [sb(f"a_cr{p}", [P, D]) for p in range(2)]
        keep = [sb(f"a_keep{p}", [P, P]) for p in range(2)]
        stat = sb("a_stat", [P, 3, 6])
        agg = sb("a_agg", [P, 3, 2])
        rstd = sb("a_rstd", [P, 3, 2])
        xn = [sb(f"a_xn{p}", [P, D]) for p in range(2)]
        xT = [sb(f"a_xT{p}", [P, KD, P]) for p in range(2)]
        qT = sb("a_qT", [P, MT0, P])
        kT = sb("a_kT", [P, MT0, P])
        va = [sb(f"a_va{p}", [P, NH, STRIP]) for p in range(2)]
        soft = [[sb(f"a_soft{p}{h}", [P, HPT // 2, MT0, P]) for h in range(2)] for p in range(2)]
        top = sb("a_top", [P, HPT, MT0])
        pT = [sb(f"a_pT{k}", [P, MT0, P]) for k in range(HPT)]
        oT = sb("a_oT", [P, MT0, P])
        den = sb("a_den", [P, NH])
        att = sb("a_att", [P, NH, DH0])
        attf = att[:, :, :].rearrange("p h d -> p (h d)")
        x1 = [sb(f"a_x1{p}", [P, D]) for p in range(2)]
        xn1 = [sb(f"a_xn1{p}", [P, D]) for p in range(2)]
        xn1T = sb("a_xn1T", [P, KD, P])
        score = sb("a_score", [P, NE])
        biased = sb("a_biased", [P, NE])
        best = sb("a_best", [P, 8])
        best_at = sb("a_best_at", [P, 8], U32)
        chosen = sb("a_chosen", [P, NE])
        negmax = sb("a_negmax", [P, 1])
        escore = shared["escore"]
        picked_row = sb("a_picked_row", [P, TOPK, NE])

        at_row = sb("a_at_row", [P, NE])
        slot_i = [sb(f"a_slot{p}", [P, TOPK], I32) for p in range(2)]
        base = sb("a_base", [P, NE])
        count = sb("a_count", [P, NE])
        count_i = sb("a_count_i", [P, NE], I32)
        cmp16 = sb("a_cmp16", [P, NE, NB])
        ntile = sb("a_ntile", [P, NE])
        cmp8 = sb("a_cmp8", [P, NE, NE])
        tile_end = sb("a_tile_end", [P, NE])
        tile_start = sb("a_tile_start", [P, NE])
        shift = shared["shift"]
        last = sb("a_last", [P, 1])
        tt = sb("a_tt", [P, N_TILES])
        cmpt = sb("a_cmpt", [P, N_TILES, NE])
        te = sb("a_te", [P, N_TILES])
        tr = sb("a_tr", [P, N_TILES])


        S = [ps(f"a_S{j}", [P, MT0, P]) for j in range(HPT)]
        M = [ps(f"a_M{j}", [P, 512]) for j in range(2)]
        T = [ps(f"a_T{j}", [P, 512]) for j in range(2)]

        s_w = sem("a_weights")
        s_const = sem("a_const")
        s_later = sem("a_later_weights")
        s_setup = sem("a_setup")
        s_bqs = sem("a_bqs")
        s_in = [sem(f"a_in{p}") for p in range(2)]
        s_ctx = [sem(f"a_ctx{p}") for p in range(2)]
        s_res = [sem(f"a_res{p}") for p in range(2)]
        s_x1out = [sem(f"a_x1out{p}") for p in range(2)]
        names = ("keep var rstd xn t_mm t_sb q_mm q_sb k_mm k_sb v_mm v_sb s_mm s_sub s_exp p_mm p_sb pv_mm ot_sb ot_mm att var1 rstd1 "
                 "x1 var2 rstd2 xn1 t1_mm t1_sb r_mm score esc pos_mm chosen prefix slot res")
        g = {n: sem("a_" + n) for n in names.split()}
        s_sc = [sem(f"a_scatter{p}") for p in range(2)]
        s_pad = [sem(f"a_pad{k}") for k in range(2)]
        s_count = sem("a_count")
        l_norm, l_max, l_out, l_choose, l_list, l_fin = (sem("al_" + n) for n in "norm max out choose list final".split())
        l_norm2 = sem("al_norm2")
        l_pool = [sem(f"al_pool{k}") for k in range(3)]

        W = [(const[:, :], t["const"]),
             (wq[:, :, :], t["L0_wqT"].rearrange("(k p) n -> p k n", p=P)),
             (bq[:, :], t["L0_bq"]), (bk[:, :], t["L0_bk"]),
             (wk[:, :, :], t["L0_wkT"].rearrange("(k p) n -> p k n", p=P)),
             (wv[:, :, :], t["L0_wvT"].rearrange("(k p) n -> p k n", p=P))]
        W_READY = 16 * (len(W) - 1)
        W_LATER = [(wr[:, :, :], t["L0_wrT"].rearrange("(k p) n -> p k n", p=P)),
                   (bv[:, :], t["L0_bv"].partition_broadcast(P)),
                   (gamma[:, :], t["L0_gamma"].partition_broadcast(P)),
                   (beta[:, :], t["L0_beta"].partition_broadcast(P)),
                   (br[:, :], t["L0_br"].partition_broadcast(P)),
                   (pick_bias[:, :], t["L0_pick_bias"].partition_broadcast(P))]
        LATER_READY = 16 * len(W_LATER)

        def by_batch(steps):
            def run(eng):
                for b in range(4):
                    steps(b, b // 2, b % 2)
                with eng.Fori(2, NB // 2 - 2) as i:
                    for p in range(2):
                        steps(i * 2 + p, i, p)
                for b in range(NB - 4, NB + 2):
                    steps(b, b // 2, b % 2)
            return run

        def there(b):
            return not isinstance(b, int) or 0 <= b < NB

        def rows_of(d, b):
            return d[bass.ds(b, 1)].rearrange("o p d -> (o p) d")

        block = ctx.enter_context(nc.Block())

        def pad(eng, first):
            eng.wait_ge(s_count, 1)
            for e in range(first, NE, 2):
                n = eng.value_load(count_i[0:1, e:e + 1], min_val=0, max_val=NB * P)
                eng.dma_start(t["lists"][bass.ds(n + e * ROWS_E, P)], zeros[:, :]).then_inc(s_pad[first], 16)
            eng.wait_ge(s_pad[first], 16 * NE // 2)

        @block.sync
        def _(sp):
            def store(b, p):
                sp.wait_ge(g["x1"], b + 1)
                sp.dma_start(rows_of(t["x1"], b), x1[p][:, :]).then_inc(s_x1out[p], 16)

            def load(b, p):
                since(sp, g["xn"], b - 1)
                since(sp, g["keep"], b - 1)
                sp.dma_start(x_in[p][:, :], rows_of(t["x"], b)).then_inc(s_in[p], 16)
                sp.dma_start(mask_in[p][:, :], t["mask"][bass.ds(b, 1)].rearrange("o s -> (o s)").partition_broadcast(P))\
                    .then_inc(s_in[p], 16)

            def load_context(b, p):
                since(sp, g["v_mm"], b - 1)
                sp.dma_start(cT[p][:, :, :].rearrange("p c n -> p (c n)"), rows_of(t["ctxT"], b)).then_inc(s_ctx[p], 16)

            def load_residual(b, p):
                since(sp, g["x1"], b - 1)
                sp.dma_start(x_res[p][:, :], rows_of(t["x"], b)).then_inc(s_res[p], 16)
                sp.dma_start(c_res[p][:, :], rows_of(t["ctx"], b)).then_inc(s_res[p], 16)

            load(0, 0)
            load_context(0, 0)
            load(1, 1)
            load_context(1, 1)
            load_residual(0, 0)
            for dst, src in W_LATER:
                sp.dma_start(dst, src).then_inc(s_later, 16)
            load(2, 0)
            load(3, 1)

            def steps(b, i, p):
                if there(b + 2):
                    load_context(b + 2, p)
                if there(b + 4):
                    load(b + 4, p)
                if there(b - 1):
                    store(b - 1, 1 - p)
                if there(b + 1):
                    load_residual(b + 1, 1 - p)
                if there(b):
                    shared["load_experts"](sp, i, p)

            by_batch(steps)(sp)
            pad(sp, 0)
            for p in range(2):
                sp.wait_ge(s_x1out[p], 16 * (NB // 2))

        @block.gpsimd
        def _(pool):
            nc.gpsimd.memset(zeros[:, :], 0.0).then_inc(s_setup, 1)
            nc.gpsimd.memset(shared["mhalf"][:, :], -0.5).then_inc(s_setup, 1)
            for p in range(2):
                nc.gpsimd.memset(va[p][:, :, :], 1.0).then_inc(s_setup, 1)
            pool.wait_ge(s_setup, 4)
            def inverse_std(link, eps, ready, done, b, k):
                apart(pool, ready, b + 1)
                link.begin(b)
                link(nc.gpsimd.tensor_scalar(rstd[:, k, 0:1], agg[:, k, 1:2], eps, None, ALU.add))
                nc.gpsimd.tensor_tensor(rstd[:, k, 1:2], rstd[:, k, 0:1], shared["mhalf"][:, :], ALU.pow).then_inc(done, 1)

            links = [Link(pool, l, 1) for l in l_pool]

            def std(n, b):
                eps, var, done = ((EPS, "var", "rstd"), (EPS0, "var1", "rstd1"), (EPS, "var2", "rstd2"))[n]
                inverse_std(links[n], eps, g[var], g[done], b, n)

            def residual(b, i, p):
                pool.wait_ge(s_res[p], 32 * (i + 1))
                nc.gpsimd.tensor_tensor(c_res[p][:, :], c_res[p][:, :], bv[:, :], ALU.add)
                nc.gpsimd.tensor_tensor(x_res[p][:, :], x_res[p][:, :], beta[:, :], ALU.add).then_inc(g["res"], 1)

            def scatter(b, p):
                apart(pool, g["slot"], b + 1)
                for k in range(TOPK):
                    nc.gpsimd.indirect_dma_start(t["lists"], bass.IndirectOffsetOnAxis(slot_i[p][:, k:k + 1], 0),
                                                 xn1[p][:, :], None).then_inc(s_sc[p], 16)

            for b in range(3):
                std(0, b)
            pool.wait_ge(s_later, LATER_READY)
            residual(0, 0, 0)

            def steps(b, i, p):
                if there(b + 3):
                    std(0, b + 3)
                if there(b - 1):
                    std(1, b - 1)
                if there(b - 1):
                    std(2, b - 1)
                if there(b + 1):
                    residual(b + 1, i + p, 1 - p)
                if there(b - 2):
                    scatter(b - 2, p)

            by_batch(steps)(pool)
            for p in range(2):
                pool.wait_ge(s_sc[p], 32 * (NB // 2))

        @block.scalar
        def _(act):
            act.dma_start(*W[0]).then_inc(s_const, 16)
            for dst, src in W[1:]:
                act.dma_start(dst, src).then_inc(s_w, 16)
            act.wait_ge(s_w, W_READY)
            nc.scalar.activation(bqs[:, :], bq[:, :], ACT.Copy, scale=SCALE0).then_inc(s_bqs, 1)
            act.wait_ge(s_bqs, 1)
            act.wait_ge(s_setup, 4)

            def project(b, p):
                act.wait_ge(g["t_mm"], b + 1)
                since(act, g["q_mm"], b - 1)
                nc.scalar.activation(xT[p][:, :, :], M[1][:, 0:D].rearrange("p (c n) -> p c n", c=KD), ACT.Copy).then_inc(g["t_sb"], 1)

            def queries(b, p):
                act.wait_ge(g["q_mm"], b + 1)
                since(act, g["s_mm"], b)
                for m in range(MT0):
                    ins = nc.scalar.activation(qT[:, m, :], M[0][:, m * P:(m + 1) * P], ACT.Identity,
                                               bias=bqs[:, m:m + 1], scale=SCALE0)
                ins.then_inc(g["q_sb"], 1)

            def values(b, p):
                act.wait_ge(g["v_mm"], b + 1)
                since(act, g["pv_mm"], 4 * (b - 1))
                nc.scalar.activation(va[p][:, :, 0:DH0], M[0][:, 0:D].rearrange("p (h d) -> p h d", h=NH), ACT.Copy)\
                    .then_inc(g["v_sb"], 1)

            def exps(b, p, h):
                act.wait_ge(g["s_sub"], 2 * b + h + 1)
                nc.scalar.activation(soft[p][h][:, :, :, :], soft[p][h][:, :, :, :], ACT.Exp).then_inc(g["s_exp"], 1)

            def probs(b, k):
                act.wait_ge(g["p_mm"], 4 * b + k + 1)
                since(act, g["pv_mm"], 4 * (b - 1) + k + 1)
                nc.scalar.activation(pT[k][:, :, :], S[k][:, :, :], ACT.Copy).then_inc(g["p_sb"], 1)

            def attended(b):
                act.wait_ge(g["pv_mm"], 4 * b + 4)
                since(act, g["ot_mm"], b)
                nc.scalar.activation(oT[:, :, :], M[0][:, :].rearrange("p (m n) -> p m n", m=MT0), ACT.Copy).then_inc(g["ot_sb"], 1)

            def next_rows(b):
                act.wait_ge(g["t1_mm"], b + 1)
                since(act, g["r_mm"], b)
                nc.scalar.activation(xn1T[:, :, :], T[1][:, 0:D].rearrange("p (c n) -> p c n", c=KD), ACT.Copy).then_inc(g["t1_sb"], 1)

            def exp_scores(b):
                act.wait_ge(g["score"], b + 1)
                nc.scalar.activation(escore[:, bass.ds(b, 1), :].rearrange("p o e -> p (o e)"), score[:, :], ACT.Exp,
                                     bias=negmax[:, 0:1]).then_inc(g["esc"], 1)

            project(0, 0)
            queries(0, 0)
            values(0, 0)
            project(1, 1)

            def steps(b, i, p):
                if there(b + 1):
                    queries(b + 1, 1 - p)
                if there(b):
                    for h in range(2):
                        exps(b, p, h)
                    for k in range(HPT // 2):
                        probs(b, k)
                if there(b + 1):
                    values(b + 1, 1 - p)
                if there(b - 2):
                    next_rows(b - 2)
                if there(b):
                    for k in range(HPT // 2, HPT):
                        probs(b, k)
                    attended(b)
                if there(b + 2):
                    project(b + 2, p)
                if there(b - 2):
                    exp_scores(b - 2)

            by_batch(steps)(act)
            pad(act, 1)

        @block.tensor
        def _(pe):
            pe.wait_ge(s_const, 16)

            def transposes(b, p):
                pe.wait_ge(g["xn"], b + 1)
                since(pe, g["k_sb"], b)
                for c in range(KD):
                    ins = nc.tensor.transpose(M[1][:, c * P:(c + 1) * P], xn[p][:, c * P:(c + 1) * P], ident)
                ins.then_inc(g["t_mm"], 1)

            def strips(out, w, src, tiles, done):
                for m in tiles:
                    for c in range(KD):
                        ins = nc.tensor.matmul(out[:, m * P:(m + 1) * P], w[:, c, m * P:(m + 1) * P], src[c],
                                               start=(c == 0), stop=(c == KD - 1))
                if done:
                    ins.then_inc(done, 1)

            def queries(b, p, tiles=range(MT0)):
                if tiles[0] == 0:
                    pe.wait_ge(g["t_sb"], b + 1)
                    since(pe, g["v_sb"], b)
                    since(pe, g["ot_sb"], b - 1)
                strips(M[0], wq, [xT[p][:, c, :] for c in range(KD)], tiles, g["q_mm"] if tiles[-1] == MT0 - 1 else None)

            def keys(b, i, p):
                pe.wait_ge(s_ctx[p], 16 * (i + 1))
                pe.wait_ge(g["t_sb"], b + 1)
                strips(M[1], wk, [cT[p][:, c, :] for c in range(KD)], range(MT0), g["k_mm"])

            def values(b, p):
                pe.wait_ge(g["q_sb"], b + 1)
                for c in range(KD):
                    ins = nc.tensor.matmul(M[0][:, 0:D], cT[p][:, c, :], wv[:, c, :], start=(c == 0), stop=(c == KD - 1))
                ins.then_inc(g["v_mm"], 1)

            def scores(b, p):
                pe.wait_ge(g["q_sb"], b + 1)
                pe.wait_ge(g["k_sb"], b + 1)
                since(pe, g["p_sb"], 4 * b)
                for m in range(MT0):
                    for j in range(HPT):
                        r = slice(j * STRIP, (j + 1) * STRIP)
                        ins = nc.tensor.matmul(S[j][:, m, :], qT[r, m, :], kT[r, m, :], start=True, stop=True)
                    if m == MT0 - 1:
                        ins.then_inc(g["s_mm"], 1)
                    if m > 0 and there(b + 1):
                        queries(b + 1, 1 - p, range(m - 1, m if m < MT0 - 1 else MT0))

            def probabilities(b, p, k):
                pe.wait_ge(g["s_exp"], 2 * b + k // 2 + 1)
                for m in range(MT0):
                    ins = nc.tensor.transpose(S[k][:, m, :], soft[p][k // 2][:, k % 2, m, :], ident)
                ins.then_inc(g["p_mm"], 1)

            def attend(b, p, k):
                pe.wait_ge(g["p_sb"], 4 * b + k + 1)
                if k == 0:
                    pe.wait_ge(g["v_sb"], b + 2 if there(b + 1) else b + 1)
                for m in range(MT0):
                    head = m * HPT + k
                    ins = nc.tensor.matmul(M[0][k * STRIP:(k + 1) * STRIP, m * P:(m + 1) * P], va[p][:, head, :],
                                           pT[k][:, m, :], start=True, stop=True, tile_position=(0, k * STRIP))
                ins.then_inc(g["pv_mm"], 1)

            def attention(b):
                pe.wait_ge(g["ot_sb"], b + 1)
                since(pe, g["att"], b)
                for m in range(MT0):
                    ins = nc.tensor.transpose(T[0][:, m * P:(m + 1) * P], oT[:, m, :], ident)
                ins.then_inc(g["ot_mm"], 1)

            def next_rows(b, p):
                pe.wait_ge(g["xn1"], b + 1)
                since(pe, g["prefix"], b)
                for c in range(KD):
                    ins = nc.tensor.transpose(T[1][:, c * P:(c + 1) * P], xn1[p][:, c * P:(c + 1) * P], ident)
                ins.then_inc(g["t1_mm"], 1)

            def router(b):
                if isinstance(b, int) and b == 0:
                    pe.wait_ge(s_later, LATER_READY)
                pe.wait_ge(g["t1_sb"], b + 1)
                for c in range(KD):
                    ins = nc.tensor.matmul(T[1][:, D:D + NE], xn1T[:, c, :], wr[:, c, :], start=(c == 0), stop=(c == KD - 1))
                ins.then_inc(g["r_mm"], 1)

            def places(b):
                pe.wait_ge(g["chosen"], b + 1)
                nc.tensor.matmul(T[1][:, D + NE:D + 2 * NE], before, chosen[:, :], start=True, stop=True)
                nc.tensor.matmul(T[1][:, D + 2 * NE:D + 3 * NE], ones, chosen[:, :], start=True, stop=True)\
                    .then_inc(g["pos_mm"], 1)

            transposes(0, 0)
            pe.wait_ge(s_w, W_READY)
            queries(0, 0)
            keys(0, 0, 0)
            values(0, 0)
            transposes(1, 1)
            scores(0, 0)

            def steps(b, i, p):
                if there(b - 1):
                    attention(b - 1)
                if there(b + 1):
                    keys(b + 1, i + p, 1 - p)
                if there(b):
                    for k in range(HPT // 2):
                        probabilities(b, p, k)
                if there(b + 1):
                    values(b + 1, 1 - p)
                if there(b - 2):
                    next_rows(b - 2, p)
                if there(b):
                    for k in range(HPT // 2, HPT):
                        probabilities(b, p, k)
                    for k in range(HPT // 2):
                        attend(b, p, k)
                if there(b - 2):
                    router(b - 2)
                if there(b):
                    for k in range(HPT // 2, HPT):
                        attend(b, p, k)
                if there(b + 2):
                    transposes(b + 2, p)
                if there(b + 1):
                    scores(b + 1, 1 - p)
                if there(b - 2):
                    places(b - 2)

            by_batch(steps)(pe)

        @block.vector
        def _(dve):
            dve.wait_ge(s_const, 16)
            norm, most, out, pick, place = (Link(dve, s, n) for s, n in
                                            ((l_norm, 1), (l_max, 2), (l_out, 4), (l_choose, 5), (l_list, 3)))
            fin = Link(dve, l_fin, 16)
            fin.begin(0)
            onehot, slots, weights = shared["onehot"], shared["slots"], shared["weights"]

            def hot(b):
                return onehot[:, bass.ds(b, 1)].rearrange("p o k e -> p (o k) e")

            def norm_stats(b, i, p):
                dve.wait_ge(s_in[p], 32 * (i + 1))
                norm.begin(b)
                return norm.add(nc.vector.bn_stats(stat[:, 0, :], x_in[p][:, :]))

            def keep_mask(b, p):
                since(dve, g["k_sb"], b - 1)
                nc.vector.tensor_scalar(keep[p][:, :], mask_in[p][:, :], 0.0, cst("aug"), ALU.not_equal, ALU.not_equal)\
                    .then_inc(g["keep"], 1)

            def norm_var(done):
                norm.wait(done)
                nc.vector.bn_aggr(agg[:, 0, :], stat[:, 0, :]).then_inc(g["var"], 1)

            def norm_rows(b, p):
                dve.wait_ge(g["rstd"], b + 1)
                since(dve, g["t_mm"], b - 1)
                nc.vector.tensor_scalar(xn[p][:, :], x_in[p][:, :], agg[:, 0, 0:1], rstd[:, 0, 1:2], ALU.subtract, ALU.mult)\
                    .then_inc(g["xn"], 1)

            def norm_in(b, i, p):
                norm_var(norm_stats(b, i, p))
                keep_mask(b, p)
                norm_rows(b, p)

            def keys(b, p):
                dve.wait_ge(g["k_mm"], b + 1)
                since(dve, g["s_mm"], b)
                dve.wait_ge(g["keep"], b + 1)
                for m in range(MT0):
                    ins = nc.vector.scalar_tensor_tensor(kT[:, m, :], M[1][:, m * P:(m + 1) * P], bk[:, m:m + 1],
                                                         keep[p][:, :], ALU.add, ALU.mult)
                ins.then_inc(g["k_sb"], 1)

            def maxima(b, h):
                if h == 0:
                    most.begin(b)
                    dve.wait_ge(g["s_mm"], b + 1)
                for u in range(HPT // 2):
                    j = h * (HPT // 2) + u
                    ins = nc.vector.tensor_reduce(top[:, j, :], S[j][:, :, :], X, ALU.max)
                return most.add(ins)

            def less_max(b, p, h, done):
                most.wait(done)
                since(dve, g["p_mm"], 4 * (b - 1))
                for u in range(HPT // 2):
                    j = h * (HPT // 2) + u
                    ins = nc.vector.tensor_tensor(soft[p][h][:, u, :, :], S[j][:, :, :],
                                                  top[:, j, :].unsqueeze(2).to_broadcast([P, MT0, P]), ALU.subtract)
                ins.then_inc(g["s_sub"], 1)

            o = T[0][:, :].rearrange("p (h d) -> p h d", h=NH)

            def denominators(b):
                out.begin(b)
                dve.wait_ge(g["ot_mm"], b + 1)
                return out.add(nc.vector.reciprocal(den[:, :], o[:, :, DH0]))

            def attention_out(done):
                out.wait(done)
                nc.vector.tensor_tensor(att[:, :, :], o[:, :, 0:DH0], den[:, :].unsqueeze(2).to_broadcast([P, NH, DH0]), ALU.mult)\
                    .then_inc(g["att"], 1)

            def out_rows(b, p):
                if isinstance(b, int) and b == 0:
                    dve.wait_ge(s_later, LATER_READY)
                dve.wait_ge(g["res"], b + 1)
                dve.wait_ge(g["att"], b + 1)
                return out.add(nc.vector.tensor_tensor(attf, attf, c_res[p][:, :], ALU.add))

            def out_stats(done):
                out.wait(done)
                return out.add(nc.vector.bn_stats(stat[:, 1, :], attf))

            def out_var(done):
                apart(dve, l_out, done)
                nc.vector.bn_aggr(agg[:, 1, :], stat[:, 1, :]).then_inc(g["var1"], 1)

            def rows_scaled(b):
                dve.wait_ge(g["rstd1"], b + 1)
                return out.add(nc.vector.scalar_tensor_tensor(attf, attf, agg[:, 1, 0:1], gamma[:, :], ALU.subtract, ALU.mult))

            def rows_out(b, i, p, done):
                since(dve, s_x1out[p], 16 * i)
                out.wait(done)
                nc.vector.scalar_tensor_tensor(x1[p][:, :], attf, rstd[:, 1, 1:2], x_res[p][:, :], ALU.mult, ALU.add)\
                    .then_inc(g["x1"], 1)

            def rows_stats(b, p):
                dve.wait_ge(g["x1"], b + 1)
                norm_2.begin(b)
                norm_2(nc.vector.bn_stats(stat[:, 2, :], x1[p][:, :]))
                nc.vector.bn_aggr(agg[:, 2, :], stat[:, 2, :]).then_inc(g["var2"], 1)

            def rows_normal(b, i, p):
                dve.wait_ge(g["rstd2"], b + 1)
                since(dve, s_sc[p], 32 * i)
                nc.vector.tensor_scalar(xn1[p][:, :], x1[p][:, :], agg[:, 2, 0:1], rstd[:, 2, 1:2], ALU.subtract, ALU.mult)\
                    .then_inc(g["xn1"], 1)

            def choose_score(b):
                pick.begin(b)
                dve.wait_ge(g["r_mm"], b + 1)
                since(dve, g["esc"], b)
                return pick.add(nc.vector.tensor_tensor(score[:, :], T[1][:, D:D + NE], br[:, :], ALU.add))

            def choose_biased(done):
                pick.wait(done)
                nc.vector.tensor_reduce(negmax[:, :], score[:, :], X, ALU.max, negate=True).then_inc(g["score"], 1)
                return pick.add(nc.vector.tensor_tensor(biased[:, :], score[:, :], pick_bias[:, :], ALU.add))

            def choose_best(done):
                pick.wait(done)
                return pick.add(nc.vector.max(best[:, :], biased[:, :]))

            def choose_index(done):
                pick.wait(done)
                return pick.add(nc.vector.max_index(best_at[:, :], best[:, :], biased[:, :]))

            def choose_hot(b, done):
                pick.wait(done)
                return pick.add(nc.vector.tensor_tensor(hot(b), cst("expert").unsqueeze(1).to_broadcast([P, TOPK, NE]),
                                                        best_at[:, 0:TOPK].unsqueeze(2).to_broadcast([P, TOPK, NE]), ALU.is_equal))

            def choose(b, done):
                since(dve, g["pos_mm"], b)
                pick.wait(done)
                oh = hot(b)
                nc.vector.tensor_tensor(chosen[:, :], oh[:, 0, :], oh[:, 1, :], ALU.add).then_inc(g["chosen"], 1)

            def list_counts(b):
                place.begin(b)
                dve.wait_ge(g["pos_mm"], b + 1)
                done = place.add(nc.vector.tensor_tensor(at_row[:, :], T[1][:, D + NE:D + 2 * NE], base[:, :], ALU.add))
                nc.vector.tensor_tensor(base[:, :], T[1][:, D + 2 * NE:D + 3 * NE], base[:, :], ALU.add).then_inc(g["prefix"], 1)
                return done

            def list_rows(b, done):
                place.wait(done)
                return place.add(nc.vector.tensor_tensor(picked_row[:, :, :], hot(b),
                                                         at_row[:, :].unsqueeze(1).to_broadcast([P, TOPK, NE]), ALU.mult))

            def list_sums(b, done):
                place.wait(done)
                row = slots[:, bass.ds(b, 1), :].rearrange("p o k -> p (o k)")
                return place.add(nc.vector.tensor_reduce(row, picked_row[:, :, :], X, ALU.add))

            def list_slots(b, i, p, done):
                since(dve, s_sc[p], 32 * i)
                place.wait(done)
                row = slots[:, bass.ds(b, 1), :].rearrange("p o k -> p (o k)")
                nc.vector.tensor_copy(slot_i[p][:, :], row).then_inc(g["slot"], 1)

            norm_2 = Link(dve, l_norm2, 1)
            norm_in(0, 0, 0)
            norm_in(1, 0, 1)
            dve.wait_ge(s_w, W_READY)
            fin(nc.vector.tensor_copy(base[:, :], cst("list")))
            keys(0, 0)
            for h in range(2):
                less_max(0, 0, h, maxima(0, h))
            norm_in(2, 1, 0)


            def steps(b, i, p):
                front, ahead, behind, lists = there(b + 3), there(b + 1), there(b - 1), there(b - 2)
                if behind:
                    den = denominators(b - 1)
                if ahead:
                    keys(b + 1, 1 - p)
                if behind:
                    attention_out(den)
                if front:
                    stats = norm_stats(b + 3, i + 1 + p, 1 - p)
                if behind:
                    rows = out_rows(b - 1, 1 - p)
                if front:
                    norm_var(stats)
                if behind:
                    rows = out_stats(rows)
                if lists:
                    best = choose_score(b - 2)
                if behind:
                    out_var(rows)
                if lists:
                    best = choose_biased(best)
                if behind:
                    rows = rows_scaled(b - 1)
                if front:
                    norm_rows(b + 3, 1 - p)
                if lists:
                    best = choose_best(best)
                if behind:
                    rows_out(b - 1, i - 1 + p, 1 - p, rows)
                if lists:
                    best = choose_index(best)
                if behind:
                    rows_stats(b - 1, 1 - p)
                if lists:
                    choose(b - 2, choose_hot(b - 2, best))
                if front:
                    keep_mask(b + 3, 1 - p)
                if behind:
                    rows_normal(b - 1, i - 1 + p, 1 - p)
                if ahead:
                    less_max(b + 1, 1 - p, 0, maxima(b + 1, 0))
                if lists:
                    row = list_counts(b - 2)
                if ahead:
                    top_done = maxima(b + 1, 1)
                if lists:
                    row = list_rows(b - 2, row)
                if ahead:
                    less_max(b + 1, 1 - p, 1, top_done)
                if lists:
                    list_slots(b - 2, i - 1, p, list_sums(b - 2, row))

            by_batch(steps)(dve)

            dve.wait_ge(g["slot"], NB)
            dve.wait_ge(g["prefix"], NB)
            fin(nc.vector.tensor_tensor(count[:, :], base[:, :], cst("list"), ALU.subtract))
            nc.vector.tensor_copy(count_i[:, :], count[:, :]).then_inc(s_count, 1)
            fin(nc.vector.tensor_tensor(cmp16[:, :, :], count[:, :].unsqueeze(2).to_broadcast([P, NE, NB]),
                                        cst("sizes").unsqueeze(1).to_broadcast([P, NE, NB]), ALU.is_gt))
            fin(nc.vector.tensor_reduce(ntile[:, :], cmp16[:, :, :], X, ALU.add))
            fin(nc.vector.tensor_tensor(cmp8[:, :, :], cst("upto").rearrange("p (a b) -> p a b", a=NE),
                                        ntile[:, :].unsqueeze(1).to_broadcast([P, NE, NE]), ALU.mult))
            fin(nc.vector.tensor_reduce(tile_end[:, :], cmp8[:, :, :], X, ALU.add))
            fin(nc.vector.tensor_tensor(tile_start[:, :], tile_end[:, :], ntile[:, :], ALU.subtract))
            fin(nc.vector.scalar_tensor_tensor(shift[:, :], tile_start[:, :], -float(P), cst("list"), ALU.mult, ALU.add))
            fin(nc.vector.tensor_scalar(last[:, :], tile_end[:, NE - 1:NE], -1.0, None, ALU.add))
            fin(nc.vector.tensor_scalar(tt[:, :], cst("tiles"), last[:, 0:1], None, ALU.min))
            fin(nc.vector.tensor_tensor(cmpt[:, :, :], tile_end[:, :].unsqueeze(1).to_broadcast([P, N_TILES, NE]),
                                        tt[:, :].unsqueeze(2).to_broadcast([P, N_TILES, NE]), ALU.is_le))
            fin(nc.vector.tensor_reduce(te[:, :], cmpt[:, :, :], X, ALU.add))
            nc.vector.tensor_copy(shared["tile_expert"][:, :], te[:, :])
            fin(nc.vector.tensor_tensor(cmpt[:, :, :], cst("expert").unsqueeze(1).to_broadcast([P, N_TILES, NE]),
                                        te[:, :].unsqueeze(2).to_broadcast([P, N_TILES, NE]), ALU.is_equal))
            fin(nc.vector.tensor_tensor(cmpt[:, :, :], cmpt[:, :, :], shift[:, :].unsqueeze(1).to_broadcast([P, N_TILES, NE]), ALU.mult))
            fin(nc.vector.tensor_reduce(tr[:, :], cmpt[:, :, :], X, ALU.add))
            fin(nc.vector.scalar_tensor_tensor(tr[:, :], tt[:, :], float(P), tr[:, :], ALU.mult, ALU.add))
            nc.vector.tensor_copy(shared["tile_row"][:, :], tr[:, :])
            fin.end()


def experts(nc, t, shared):
    with ExitStack() as ctx:
        def sb(name, shape, dt=F32):
            return ctx.enter_context(nc.sbuf_tensor(name, shape, dt))

        def ps(name, shape, dt=F32):
            return ctx.enter_context(nc.psum_tensor(name, shape, dt))

        def sem(name):
            shared["semaphores"].append(nc.alloc_semaphore(name=name))
            return shared["semaphores"][-1]

        a, z = CONST_AT["ident"]
        ident = shared["const"][:, a:z]
        w1, w2, b1, b2 = (shared[n] for n in ("w1", "w2", "b1", "b2"))
        tile_expert, tile_row = shared["tile_expert"], shared["tile_row"]
        rows = [sb(f"b_rows{p}", [P, D]) for p in range(2)]
        rowsT = [sb(f"b_rowsT{p}", [P, KD, P]) for p in range(2)]
        gate = [sb(f"b_gate{p}", [P, HE]) for p in range(2)]
        up = [sb(f"b_up{p}", [P, HE]) for p in range(2)]
        hidT = [sb(f"b_hidT{p}", [P, KH, P]) for p in range(2)]
        out = [sb(f"b_out{p}", [P, D]) for p in range(2)]
        zeros = sb("b_zeros", [P, BANDW])
        n = NB * TOPK
        chances, shifts = (gate[1][:, k * n * NE:(k + 1) * n * NE].rearrange("p (n e) -> p n e", e=NE) for k in range(2))
        val, moved = (up[1][:, k * n:(k + 1) * n].rearrange("p (b k) -> p b k", k=TOPK) for k in range(2))
        tot = up[1][:, 2 * n:2 * n + NB]
        G = [ps(f"b_G{p}", [P, HE]) for p in range(2)]
        U = [ps(f"b_U{p}", [P, HE]) for p in range(2)]
        RT = ps("b_RT", [P, KD, P])
        HT = ps("b_HT", [P, KH, P])
        Y = ps("b_Y", [P, D])

        s_b2 = sem("b_bias")
        s_zero = sem("b_zero")
        l_combine = sem("bl_combine")
        s_clear = sem("b_clear")
        s_in = [sem(f"b_in{p}") for p in range(2)]
        s_out = [sem(f"b_out_{p}") for p in range(2)]
        names = "rt_mm rt_sb g_mm u_mm gate silu up hid ht_mm ht_sb y_mm y_sb"
        g = {n: sem("b_" + n) for n in names.split()}

        def by_tile(steps):
            def run(eng):
                for n in range(4):
                    steps(n, n // 2, n % 2)
                with eng.Fori(2, (N_TILES - 3) // 2) as i:
                    for p in range(2):
                        steps(i * 2 + p, i, p)
                for n in range(2 * ((N_TILES - 3) // 2), N_TILES):
                    steps(n, n // 2, n % 2)
            return run

        def there(n):
            return not isinstance(n, int) or 0 <= n < N_TILES

        block = ctx.enter_context(nc.Block())

        @block.sync
        def _(sp):
            def load(n, p):
                at = tile_row[0:1, n:n + 1] if isinstance(n, int) else tile_row[0:1, bass.ds(n, 1)]
                row = sp.value_load(at, min_val=0, max_val=NE * ROWS_E - P)
                since(sp, g["rt_mm"], n - 1)
                sp.dma_start(rows[p][:, :], t["lists"][bass.ds(row, P)]).then_inc(s_in[p], 16)

            def store(n, p):
                sp.wait_ge(g["y_sb"], n + 1)
                sp.dma_start(t["expert_out"][bass.ds(n * P, P)], out[p][:, :]).then_inc(s_out[p], 16)

            def steps(n, i, p):
                load(n, p)
                if there(n - 3):
                    store(n - 3, 1 - p)

            by_tile(steps)(sp)
            for n in range(N_TILES - 3, N_TILES):
                store(n, n % 2)
            sp.wait_ge(s_out[0], 16 * ((N_TILES + 1) // 2))
            sp.wait_ge(s_out[1], 16 * (N_TILES // 2))

        @block.gpsimd
        def _(pool):
            nc.gpsimd.memset(zeros[:, :], 0.0).then_inc(s_zero, 1)

            def steps(n, i, p):
                pool.wait_ge(g["silu"], n + 1)
                pool.wait_ge(g["up"], n + 1)
                nc.gpsimd.tensor_tensor(up[p][:, :], up[p][:, :], gate[p][:, :], ALU.mult).then_inc(g["hid"], 1)

            by_tile(steps)(pool)

        @block.scalar
        def _(act):
            def rows_sb(n, i, p):
                act.wait_ge(g["rt_mm"], n + 1)
                since(act, g["u_mm"], n - 1)
                nc.scalar.activation(rowsT[p][:, :, :], RT[:, :, :], ACT.Copy).then_inc(g["rt_sb"], 1)

            def activate(n, p):
                act.wait_ge(g["gate"], n + 1)
                nc.scalar.activation(gate[p][:, :], gate[p][:, :], ACT.Silu).then_inc(g["silu"], 1)

            rows_sb(0, 0, 0)
            act.dma_start(b2, t["L0_bl2"].partition_broadcast(P)).then_inc(s_b2, 16)
            activate(0, 0)
            rows_sb(1, 0, 1)

            def steps(n, i, p):
                if there(n + 2):
                    rows_sb(n + 2, i + 1, p)
                act.wait_ge(g["ht_mm"], n + 1)
                since(act, g["y_mm"], n - 1)
                nc.scalar.activation(hidT[p][:, :, :], HT[:, :, :], ACT.Copy).then_inc(g["ht_sb"], 1)
                if there(n + 1):
                    activate(n + 1, 1 - p)
                if isinstance(n, int) and n < 4:
                    shared["load_layer1"](act, slice(2 * n, 2 * n + 2))
                if isinstance(n, int) and n == 3:
                    act.wait_ge(s_zero, 1)
                    for d in t["prob_rows"]:
                        act.dma_start(d, zeros[:, :].unsqueeze(1).to_broadcast([P, NH, BANDW])).then_inc(s_clear, 16)

            by_tile(steps)(act)
            act.wait_ge(s_clear, 16 * len(t["prob_rows"]))

        def expert_of(eng, n):
            at = tile_expert[0:1, n:n + 1] if isinstance(n, int) else tile_expert[0:1, bass.ds(n, 1)]
            return eng.value_load(at, min_val=0, max_val=NE - 1)

        @block.tensor
        def _(pe):
            pe.wait_ge(shared["s_experts"], shared["experts_ready"])

            def transposes(n, i, p):
                pe.wait_ge(s_in[p], 16 * (i + 1))
                since(pe, g["rt_sb"], n)
                for c in range(KD):
                    ins = nc.tensor.transpose(RT[:, c, :], rows[p][:, c * P:(c + 1) * P], ident)
                ins.then_inc(g["rt_mm"], 1)

            def first_products(n, p, dst, at, free, done):
                e = expert_of(pe, n)
                pe.wait_ge(g["rt_sb"], n + 1)
                since(pe, free, n - 1)
                for c in range(KD):
                    w = w1[:, bass.ds(e, 1), c, at:at + HE].rearrange("p o n -> p (o n)")
                    ins = nc.tensor.matmul(dst[p][:, :], rowsT[p][:, c, :], w, start=(c == 0), stop=(c == KD - 1))
                ins.then_inc(done, 1)

            def gates(n, p):
                first_products(n, p, G, 0, g["gate"], g["g_mm"])

            def ups(n, p):
                first_products(n, p, U, HE, g["up"], g["u_mm"])

            transposes(0, 0, 0)
            gates(0, 0)
            ups(0, 0)
            transposes(1, 0, 1)

            def steps(n, i, p):
                if there(n + 2):
                    transposes(n + 2, i + 1, p)
                if there(n + 1):
                    gates(n + 1, 1 - p)
                pe.wait_ge(g["hid"], n + 1)
                since(pe, g["ht_sb"], n)
                for k in range(KH):
                    ins = nc.tensor.transpose(HT[:, k, :], up[p][:, k * P:(k + 1) * P], ident)
                ins.then_inc(g["ht_mm"], 1)
                if there(n + 1):
                    ups(n + 1, 1 - p)
                e = expert_of(pe, n)
                pe.wait_ge(g["ht_sb"], n + 1)
                since(pe, g["y_sb"], n)
                for k in range(KH):
                    w = w2[:, bass.ds(e, 1), k, :].rearrange("p o n -> p (o n)")
                    ins = nc.tensor.matmul(Y[:, :], hidT[p][:, k, :], w, start=(k == 0), stop=(k == KH - 1))
                ins.then_inc(g["y_mm"], 1)

            by_tile(steps)(pe)

        @block.vector
        def _(dve):
            dve.wait_ge(shared["s_experts"], shared["experts_ready"])

            def combine():
                lk = Link(dve, l_combine, 8)
                lk.begin(0)
                onehot, weights = shared["onehot"], shared["weights"]
                flat = onehot[:, :, :, :].rearrange("p b k e -> p (b k) e")
                lk.add(nc.vector.tensor_tensor(chances.rearrange("p (b k) e -> p b k e", b=NB), onehot[:, :, :, :],
                                               shared["escore"][:, :, :].unsqueeze(2).to_broadcast([P, NB, TOPK, NE]), ALU.mult))
                lk(nc.vector.tensor_tensor(shifts, flat, shared["shift"][:, :].unsqueeze(1).to_broadcast([P, NB * TOPK, NE]), ALU.mult))
                nc.vector.tensor_reduce(val.rearrange("p b k -> p (b k)"), chances, X, ALU.add)
                lk(nc.vector.tensor_reduce(moved.rearrange("p b k -> p (b k)"), shifts, X, ALU.add))
                lk.add(nc.vector.tensor_tensor(tot, val[:, :, 0], val[:, :, 1], ALU.add))
                lk(nc.vector.tensor_tensor(moved, shared["slots"][:, :, :], moved, ALU.subtract))
                lk.add(nc.vector.tensor_copy(shared["tile_rows"][:, :, :], moved))
                lk(nc.vector.reciprocal(tot, tot))
                lk(nc.vector.tensor_tensor(weights[:, :, :], val, tot.unsqueeze(2).to_broadcast([P, NB, TOPK]), ALU.mult))
                lk.end()

            def hidden(n, i, p):
                e = expert_of(dve, n)
                dve.wait_ge(g["g_mm"], n + 1)
                since(dve, g["hid"], n - 1)
                bias = b1[:, bass.ds(e, 1), :].rearrange("p o n -> p (o n)")
                nc.vector.tensor_tensor(gate[p][:, :], G[p][:, :], bias[:, 0:HE], ALU.add).then_inc(g["gate"], 1)
                dve.wait_ge(g["u_mm"], n + 1)
                since(dve, g["ht_mm"], n - 1)
                nc.vector.tensor_tensor(up[p][:, :], U[p][:, :], bias[:, HE:2 * HE], ALU.add).then_inc(g["up"], 1)

            hidden(0, 0, 0)
            combine()
            dve.wait_ge(s_b2, 16)

            def steps(n, i, p):
                if there(n + 1):
                    hidden(n + 1, i + p, 1 - p)
                e = expert_of(dve, n)
                dve.wait_ge(g["y_mm"], n + 1)
                since(dve, s_out[p], 16 * i)
                nc.vector.tensor_tensor(out[p][:, :], Y[:, :], b2[:, bass.ds(e, 1), :].rearrange("p o n -> p (o n)"), ALU.add)\
                    .then_inc(g["y_sb"], 1)

            by_tile(steps)(dve)


HID = 1024
MH = HID // P
W_N = D * HID
LEVELS = 127.0
FLOOR = 1e-5
ROUND = 1.5 * 2.0 ** 23

DH1 = 64
INNER = NH * DH1
MT1 = INNER // P
NREL = 2 * MAXREL + 1
STREAMS = [(0, TEXT), (TEXT, TEXT + IMG), (TEXT + IMG, P)]
NS = len(STREAMS)
SCALE1 = 1.0 / DH1 ** 0.5
RELW = P - 1 + TEXT
REL_LO = P - 1 - MAXREL
L1_EARLY = ["Wq", "Wk0", "Wk1", "Wk2", "Wv0", "Wv1"]
HS = NH // 2
MS = MT1 // 2
NPAIR = NB // 2
SHORT = [(s, z - a) for s, (a, z) in enumerate(STREAMS) if s]
NSHORT = P - TEXT
NGROUP = 2
BG = NB // NGROUP
VALUE_TILES = [(s, at, min(at + P, NB * n)) for s, n in SHORT for at in range(0, NB * n, P)]
PAIR_TILES = [(m, m + 2) for m in range(0, MT1, 2)]
LOOP_END = NPAIR - 2
NO_BANDS = 2
AHEAD_TURNS = 1 + 2 + 2
EVEN_TURNS = NO_BANDS + 4 + 4 + 4 + AHEAD_TURNS
ODD_TURNS = NO_BANDS + 4 + 4 + AHEAD_TURNS
TO_KEYS = NO_BANDS + 4
PAIR_TURNS = EVEN_TURNS + ODD_TURNS
VALUES_AT = 2 * MT1 + 2 * AHEAD_TURNS
TURNS_AHEAD = VALUES_AT + 2 * len(VALUE_TILES) + 4 + 4
assert PAIR_TURNS % 2 == 0


class Turns:

    def __init__(self):
        self.n, self.bank = 0, 0

    @staticmethod
    def at(i, p):
        return i * PAIR_TURNS + p * EVEN_TURNS + TURNS_AHEAD - NO_BANDS

    def begin(self, b, i, p):
        if not isinstance(b, int) or b == 2 * LOOP_END:
            self.n, self.bank = self.at(i, p), self.at(0, p) % 2
        else:
            assert b in (0, NB - 1) or (self.n == self.at(i, p) and self.bank == self.n % 2), (b, self.n)

    def next(self):
        n, k = self.n, self.bank
        self.n, self.bank = n + 1, 1 - k
        return n, k


def attention1(nc, t, shared):
    with ExitStack() as ctx:
        def sb(name, shape, dt=F32):
            return ctx.enter_context(nc.sbuf_tensor(name, shape, dt))

        def ps(name, shape, dt=F32):
            return ctx.enter_context(nc.psum_tensor(name, shape, dt))

        def sem(name):
            shared["semaphores"].append(nc.alloc_semaphore(name=name))
            return shared["semaphores"][-1]

        const = shared["const"]

        def cst(name):
            a, z = CONST_AT[name]
            return const[:, a:z]

        ident = cst("ident")
        weights = dict(shared["layer1"])
        weights["Wv2"] = sb("c_wv2", [P, KD, INNER])[:, :, :]
        weights["Wo"] = shared["b2"]
        assert NE == MT1
        wq, wo = weights["Wq"], weights["Wo"]
        wk, wv = ([weights[f"W{n}{s}"] for s in range(NS)] for n in "kv")
        relk = sb("c_relk", [P, 2 * NREL])
        relv = sb("c_relv", [2 * NREL, 2 * DH1])
        bo = sb("c_bo", [P, D])
        alphas = sb("c_alphas", [P, 2])
        taps = sb("c_taps", [P, MH, 3])
        tanhs = sb("c_tanhs", [P, 2])
        coef = sb("c_coef", [P, NS, NH])
        wsum = sb("c_wsum", [P, 2])
        wscale = sb("c_wscale", [P, 2])

        two = range(2)
        wf, wunit = [weights[f"Wk{s}"].rearrange("p k n -> p (k n)") for s, _ in SHORT], shared["ffn_unit"]
        x_in = [sb(f"c_x{p}", [P, D]) for p in two]
        pick = [sb(f"c_pick{p}", [P, TOPK], I32) for p in two]
        picked = [[sb(f"c_y{p}{k}", [P, D]) for k in range(TOPK)] for p in two]
        x2 = [sb(f"c_x2{p}", [P, D]) for p in two]
        x2b = [sb(f"c_x2b{p}", [P, D]) for p in two]
        x3 = [sb(f"c_x3{p}", [P, D]) for p in two]
        stat = [sb(f"c_stat{p}", [P, 6]) for p in two]
        agg = [sb(f"c_agg{p}", [P, 2]) for p in two]
        rstd = [sb(f"c_rstd{p}", [P, 2]) for p in two]
        xn = [sb(f"c_xn{p}", [P, D]) for p in two]
        xT = sb("c_xT", [P, KD, P])
        qT = [sb(f"c_qT{p}", [P, MT1, P]) for p in two]
        cT = sb("c_cT", [P, KD, 2, TEXT])
        kT = sb("c_kT", [P, MT1, 2, P])
        vT = sb("c_vT", [P, MT1, 2, TEXT])
        v = [sb(f"c_v{p}", [P, INNER]) for p in two]
        relw = [sb(f"c_relw{h}", [P, HS, RELW]) for h in two]
        bias = [sb(f"c_bias{p}", [P, NH, TEXT]) for p in two]
        soft = [sb(f"c_soft{p}", [P, NH, P]) for p in two]
        spare = soft[0][:, :, :].rearrange("p h n -> p (h n)")
        short_c, at = {}, 0
        for s, n in SHORT:
            short_c[s] = spare[:, at:at + KD * NB * n].rearrange("p (c n) -> p c n", c=KD)
            at += KD * NB * n
        short_k = [[v[h][:, k * BG * NSHORT:(k + 1) * BG * NSHORT] for k in two] for h in range(NGROUP)]
        short_v = [soft[1][:, k * HS:(k + 1) * HS, :].rearrange("p h n -> p (h n)") for k in two]
        top = sb("c_top", [P, NS, NH])
        total = sb("c_total", [P, NS, NH])
        share = sb("c_share", [P, NS, NH])
        pT = [sb(f"c_pT{k}", [P, 4, P]) for k in two]
        near = sb("c_near", [P, NH, TEXT])
        far = sb("c_far", [P, NH, TEXT])
        band = [sb(f"c_band{p}", [P, NH, NREL]) for p in two]
        bandT = sb("c_bandT", [2 * NREL, MT1, P])
        attT = sb("c_attT", [P, MT1, P])

        S = ps("c_S", [P, NH, P])
        T = [ps(f"c_T{k}", [P, 512]) for k in two]
        O = [ps(f"c_O{h}", [P, MS, P]) for h in two]

        rel_d = [nc.dram_tensor(f"rel_windows{p}", (P, NH, RELW), F32, kind="Internal").ap() for p in two]
        prob_d = t["prob_rows"]

        short_kd = nc.dram_tensor("short_keys", (P, MT1, NB * NSHORT), F32, kind="Internal").ap()
        short_vd = {s: nc.dram_tensor(f"short_values{s}", (NB * n, INNER), F32, kind="Internal").ap() for s, n in SHORT}

        s_w = sem("c_weights")
        s_short = sem("c_short_context")
        s_kout = [[sem(f"c_short_keys_out{h}{k}") for k in two] for h in range(NGROUP)]
        s_vout = [sem(f"c_short_values_out{k}") for k in two]
        s_kin = sem("c_short_keys_in")
        s_vin = sem("c_short_values_in")
        s_ctx = sem("c_context")
        s_late = sem("c_late_weights")
        s_setup = sem("c_setup")
        s_alpha = sem("c_alpha")
        s_ffn = sem("c_ffn_weights")
        s_sums = sem("c_ffn_sums")
        s_total = sem("c_ffn_total")
        l_ffn = sem("cl_ffn")
        s_in = [sem(f"c_in{p}") for p in two]
        s_pick = [sem(f"c_picked{p}") for p in two]
        s_relout = [sem(f"c_relout{h}") for h in two]
        s_relin = [sem(f"c_relin{p}") for p in two]
        s_pout = [sem(f"c_pout{p}") for p in two]
        s_pin = [sem(f"c_pin{p}") for p in two]
        s_x3 = [sem(f"c_x3out{p}") for p in two]
        names = "filled emptied pick x2 var rstd xn x2b s_mm s_sub s_exp share soft tails bandv pv_mm o_mm o_sb y_mm x3"
        g = {n: sem("c_" + n) for n in names.split()}
        l_front, l_sum, l_pool = (sem("cl_" + n) for n in "front sum pool".split())
        l_softs = [sem(f"cl_soft{h}") for h in range(2)]

        W = [(relk[:, :], t["L1_relk"]), (relv[:, :], t["L1_relv"]), (bo[:, :], t["L1_bo"].partition_broadcast(P)),
             (alphas[:, :], t["L1_alphas"].partition_broadcast(P)),
             (taps[:, :, :], t["L1_conv_w"].rearrange("(m p) k -> p m k", p=P))]
        W_READY = 16 * len(W)

        def sheared(d, at, step, parts, width):
            part, head, _ = d.ap
            return bass.AP(d.tensor, d.offset + at, [[part[0] + step, parts], [head[0], NH], [1, width]])

        def by_batch(steps):
            def run(eng):
                for b in range(2):
                    steps(b, 0, b, b == 0, False)
                with eng.Fori(1, LOOP_END) as i:
                    for p in range(2):
                        steps(i * 2 + p, i, p, False, False)
                for b in range(2 * LOOP_END, NB):
                    steps(b, b // 2, b % 2, False, b == NB - 1)
            return run

        def there(b):
            return not isinstance(b, int) or b < NB

        def rows_of(d, b):
            return d[bass.ds(b, 1)].rearrange("o p d -> (o p) d")

        block = ctx.enter_context(nc.Block())

        @block.sync
        def _(sp):
            def load(b, p):
                sp.dma_start(x_in[p][:, :], rows_of(t["x1"], b)).then_inc(s_in[p], 16)

            def load_context(b, p):
                sp.dma_start(cT[:, :, p, :], rows_of(t["ctxT"], b).rearrange("p (c n) -> p c n", c=KD)[:, :, 0:TEXT]).then_inc(s_ctx, 16)

            def load_keys(b, p):
                sp.dma_start(kT[:, :, p, TEXT:P], short_kd[:, :, bass.ds(b * NSHORT, NSHORT)]).then_inc(s_kin, 16)

            def load_values(b, p):
                for s, n in SHORT:
                    a, z = STREAMS[s]
                    sp.dma_start(v[p][a:z, :], short_vd[s][bass.ds(b * n, n)]).then_inc(s_vin, 16)

            def rel_in(b, i, p):
                for h in two:
                    apart(sp, s_relout[h], 16 * (b + 1))
                since(sp, g["s_sub"], 2 * (b - 1))
                sp.dma_start(bias[p][:, :, :], sheared(rel_d[p], P - 1, -1, P, TEXT)).then_inc(s_relin[p], 16)

            def prob_out(b, i, p):
                apart(sp, g["soft"], 2 * b + 2)
                since(sp, s_pin[p], 16 * i)
                sp.dma_start(prob_d[p][:, :, MAXREL:MAXREL + TEXT], soft[p][:, :, 0:TEXT]).then_inc(s_pout[p], 16)

            def band_in(b, i, p):
                sp.wait_ge(s_pout[p], 16 * (i + 1))
                sp.dma_start(band[p][:, :, 1:NREL - 1], sheared(prob_d[p], 1, 1, P, NREL - 2)).then_inc(s_pin[p], 16)

            def store(b, p):
                sp.wait_ge(g["x3"], b + 1)
                sp.dma_start(rows_of(t["x3"], b), x3[p][:, :]).then_inc(s_x3[p], 16)

            for s, n in SHORT:
                sp.dma_start(short_c[s], t[f"short_ctxT{s}"].rearrange("p (c n) -> p c n", c=KD)).then_inc(s_short, 16)
            for p in two:
                load(p, p)
            for q in two:
                load_context(q, q)
            for dst, src in W:
                sp.dma_start(dst, src).then_inc(s_w, 16)
            sp.wait_ge(g["x2"], 1)
            load(2, 0)
            sp.wait_ge(g["emptied"], 2 * MT1)
            for name in ("Wv2", "Wo"):
                sp.dma_start(weights[name], t["L1_" + name].rearrange("(k p) n -> p k n", p=P)).then_inc(s_late, 16)
            sp.dma_start(wf[0].rearrange("p (k n) -> p k n", k=KD), t["L1_w1T"].rearrange("(k p) n -> p k n", p=P)).then_inc(s_ffn, 16)
            sp.dma_start(wf[1].rearrange("p (k n) -> p k n", k=MH), t["L1_w2T"].rearrange("(k p) n -> p k n", p=P)).then_inc(s_ffn, 16)
            for q in two:
                rel_in(q, 0, q)
            for out in s_kout[0] + s_kout[1]:
                sp.wait_ge(out, 16 * (MT1 // 2))
            for q in two:
                load_keys(q, q)
            for k in two:
                sp.wait_ge(s_vout[k], 16 * len(VALUE_TILES[k::2]))
            for q in two:
                load_values(q, q)

            apart(sp, g["filled"], TURNS_AHEAD)
            for q in two:
                load_context(2 + q, q)

            def steps(b, i, p, first, last):
                if there(b + 3):
                    apart(sp, g["x2"], b + 2)
                    load(b + 3, 1 - p)
                if p == 0 and not first:
                    apart(sp, g["pv_mm"], 4 * b)
                    for q in two:
                        load_values(b + q, q)
                if p == 1 and there(b + 1):
                    apart(sp, g["s_mm"], 2 * b + 2)
                    for q in two:
                        load_keys(b + 1 + q, q)
                if p == 1 and there(b + 3):
                    apart(sp, g["filled"], Turns.at(i, 1) + TO_KEYS)
                    for q in two:
                        load_context(b + 3 + q, q)
                prob_out(b, i, p)
                if not first:
                    store(b - 1, 1 - p)
                band_in(b, i, p)
                if there(b + 2):
                    rel_in(b + 2, i + 1, p)

            by_batch(steps)(sp)
            store(NB - 1, 1)
            for p in two:
                sp.wait_ge(s_x3[p], 16 * (NB // 2))

        @block.gpsimd
        def _(pool):
            lk = Link(pool, l_pool, 1)

            def gather(b, p):
                apart(pool, g["x2"], b - 1)
                apart(pool, g["pick"], b + 1)
                for k in range(TOPK):
                    nc.gpsimd.indirect_dma_start(picked[p][k][:, :], None, t["expert_out"],
                                                 bass.IndirectOffsetOnAxis(pick[p][:, k:k + 1], 0)).then_inc(s_pick[p], 16)

            def inverse_std(b, p):
                apart(pool, g["var"], b + 1)
                lk.begin(b)
                lk(nc.gpsimd.tensor_scalar(rstd[p][:, 0:1], agg[p][:, 1:2], EPS, None, ALU.add))
                nc.gpsimd.tensor_tensor(rstd[p][:, 1:2], rstd[p][:, 0:1], shared["mhalf"][:, :], ALU.pow).then_inc(g["rstd"], 1)

            def residual(b, p):
                pool.wait_ge(g["x2"], b + 1)
                since(pool, g["x3"], b - 1)
                nc.gpsimd.tensor_tensor(x2b[p][:, :], x2[p][:, :], bo[:, :], ALU.add).then_inc(g["x2b"], 1)

            def normalise(b, p, h):
                hs = slice(h * HS, (h + 1) * HS)
                pool.wait_ge(g["share"], 2 * b + h + 1)
                for s, (a, z) in enumerate(STREAMS):
                    ins = nc.gpsimd.tensor_tensor(soft[p][:, hs, a:z], soft[p][:, hs, a:z],
                                                  share[:, s, hs].unsqueeze(2).to_broadcast([P, HS, z - a]), ALU.mult)
                ins.then_inc(g["soft"], 1)

            def tails(b, p):
                pool.wait_ge(g["soft"], 2 * b + 2)
                since(pool, g["bandv"], b)
                for dst, m in ((near, "before_band"), (far, "behind_band")):
                    ins = nc.gpsimd.tensor_tensor(dst[:, :, :], soft[p][:, :, 0:TEXT],
                                                  cst(m).unsqueeze(1).to_broadcast([P, NH, TEXT]), ALU.mult)
                ins.then_inc(g["tails"], 1)

            for p in two:
                gather(p, p)
            inverse_std(0, 0)
            gather(2, 0)
            inverse_std(1, 1)
            pool.wait_ge(s_w, W_READY)
            residual(0, 0)
            for m in range(MH):
                for k in range(3):
                    nc.gpsimd.tensor_scalar(shared["tap"][:, m, k, :], ident, taps[:, m, k:k + 1], None, ALU.mult)

            def steps(b, i, p, first, last):
                if there(b + 2):
                    inverse_std(b + 2, p)
                if there(b + 3):
                    gather(b + 3, 1 - p)
                for h in range(2):
                    normalise(b, p, h)
                tails(b, p)
                if there(b + 1):
                    residual(b + 1, 1 - p)

            by_batch(steps)(pool)

        @block.scalar
        def _(act):
            turns = Turns()

            def empty(dst, view, **kw):
                n, k = turns.next()
                act.wait_ge(g["filled"], n + 1)
                nc.scalar.activation(dst, view(T[k]), ACT.Copy, **kw).then_inc(g["emptied"], 1)

            def parts(m):
                return lambda bank: bank[:, :].rearrange("p (m n) -> p m n", m=m)

            def projected(dst, tiles):
                for a, z in tiles:
                    n = 2 * (z - a)
                    empty(dst[:, a:z, :, 0:TEXT].rearrange("p m q n -> p (m q) n"),
                          lambda bank: bank[:, 0:n * TEXT].rearrange("p (m n) -> p m n", m=n))

            def queries(p):
                for u in two:
                    empty(qT[p][:, u * MS:(u + 1) * MS, :], parts(MS), scale=SCALE1)

            def short_keys():
                def step(u, first):
                    for k in two:
                        m = u * 2 + k
                        for h in range(NGROUP):
                            turns.n = m * NGROUP + h
                            if not first:
                                act.wait_ge(s_kout[h][k], 16 * u)
                            empty(short_k[h][k], lambda bank: bank[:, 0:BG * NSHORT])
                        for h in range(NGROUP):
                            apart(act, g["emptied"], m * NGROUP + h + 1)
                            act.dma_start(short_kd[:, bass.ds(m, 1), h * BG * NSHORT:(h + 1) * BG * NSHORT].rearrange("p o n -> p (o n)"),
                                          short_k[h][k]).then_inc(s_kout[h][k], 16)
                step(0, True)
                with act.Fori(1, MT1 // 2) as u:
                    step(u, False)
                turns.n = NGROUP * MT1

            def short_values():
                for k, (s, a, z) in enumerate(VALUE_TILES):
                    since(act, s_vout[k % 2], 16 * (k // 2))
                    for w in two:
                        empty(short_v[k % 2][0:z - a, w * 512:(w + 1) * 512], lambda bank: bank[0:z - a, :])
                    act.wait_ge(g["emptied"], turns.n)
                    act.dma_start(short_vd[s][a:z, :], short_v[k % 2][0:z - a, :]).then_inc(s_vout[k % 2], 16)

            def rows():
                empty(xT[:, :, :], lambda bank: bank[:, 0:D].rearrange("p (c n) -> p c n", c=KD))

            def values():
                for q in two:
                    for w in two:
                        empty(v[q][0:TEXT, w * 512:(w + 1) * 512], lambda bank: bank[0:TEXT, :])

            def windows(b, i, p):
                hi = REL_LO + NREL
                for h in two:
                    n, k = turns.next()
                    act.wait_ge(g["filled"], n + 1)
                    since(act, s_relout[h], 16 * b)
                    r, w = T[k][:, 0:HS * NREL].rearrange("p (h r) -> p h r", h=HS), relw[h]
                    nc.scalar.activation(w[:, :, 0:REL_LO], r[:, :, 0:1].to_broadcast([P, HS, REL_LO]), ACT.Copy)
                    nc.scalar.activation(w[:, :, REL_LO:hi], r, ACT.Copy)
                    nc.scalar.activation(w[:, :, hi:RELW], r[:, :, NREL - 1:NREL].to_broadcast([P, HS, RELW - hi]), ACT.Copy)\
                        .then_inc(g["emptied"], 1)
                    act.wait_ge(g["emptied"], n + 1)
                    since(act, s_relin[p], 16 * i)
                    act.dma_start(rel_d[p][:, h * HS:(h + 1) * HS, :], w[:, :, :]).then_inc(s_relout[h], 16)

            def exps(b, p, h):
                act.wait_ge(g["s_sub"], 2 * b + h + 1)
                hs = slice(h * HS, (h + 1) * HS)
                nc.scalar.activation(soft[p][:, hs, :], soft[p][:, hs, :], ACT.Exp).then_inc(g["s_exp"], 1)

            def bands():
                for h in two:
                    empty(bandT[:, h * MS:(h + 1) * MS, :], lambda bank: bank[0:2 * NREL, :].rearrange("p (m n) -> p m n", m=MS))

            def attended(b):
                for h in two:
                    act.wait_ge(g["o_mm"], 2 * b + h + 1)
                    nc.scalar.activation(attT[:, h * MS:(h + 1) * MS, :], O[h][:, :, :], ACT.Copy).then_inc(g["o_sb"], 1)

            def probs(k):
                empty(pT[k % 2][:, :, :], parts(4))

            short_keys()
            act.wait_ge(s_w, W_READY)
            nc.scalar.activation(tanhs[:, :], alphas[:, :], ACT.Tanh).then_inc(s_setup, 1)
            for q in two:
                rows()
                queries(q)
                windows(q, 0, q)
            assert turns.n == VALUES_AT
            short_values()
            projected(kT, PAIR_TILES)
            projected(vT, PAIR_TILES)
            for out in s_kout[0] + s_kout[1]:
                act.wait_ge(out, 16 * (MT1 // 2))

            def steps(b, i, p, first, last):
                turns.begin(b, i, p)
                if not first:
                    bands()
                if p == 0:
                    values()
                    exps(b, p, 0)
                    if there(b + 2):
                        projected(vT, PAIR_TILES[:2])
                    exps(b, p, 1)
                    if there(b + 2):
                        projected(vT, PAIR_TILES[2:])
                else:
                    if there(b + 2):
                        projected(kT, PAIR_TILES[:1])
                    exps(b, p, 0)
                    if there(b + 2):
                        projected(kT, PAIR_TILES[1:])
                    exps(b, p, 1)
                if there(b + 2):
                    rows()
                if not first:
                    attended(b - 1)
                if there(b + 2):
                    queries(p)
                    windows(b + 2, i + 1, p)
                for k in range(4):
                    probs(k)

            by_batch(steps)(act)
            bands()
            attended(NB - 1)

        @block.tensor
        def _(pe):
            pe.wait_ge(shared["s_layer1"], 16 * len(L1_EARLY))
            turns = Turns()

            def turn():
                n, k = turns.next()
                since(pe, g["emptied"], n - 1)
                return n, T[k]

            def taken(n):
                pe.wait_ge(g["emptied"], n + 1)

            def transposes(parts):
                n, bank = turn()
                for j, part in enumerate(parts):
                    ins = nc.tensor.transpose(bank[0:part.shape[1], j * P:(j + 1) * P], part, ident)
                ins.then_inc(g["filled"], 1)
                return n

            def short_keys():
                for m in range(MT1):
                    for h in range(NGROUP):
                        _, bank = turn()
                        dst = bank[:, 0:BG * NSHORT].rearrange("p (b n) -> p b n", b=BG)
                        for s, n in SHORT:
                            a, z = (e - TEXT for e in STREAMS[s])
                            for c in range(KD):
                                ins = nc.tensor.matmul(dst[:, :, a:z], wk[s][:, c, m * P:(m + 1) * P],
                                                       short_c[s][:, c, h * BG * n:(h + 1) * BG * n].rearrange("p (b n) -> p b n", b=BG),
                                                       start=(c == 0), stop=(c == KD - 1))
                        ins.then_inc(g["filled"], 1)

            def short_values(tiles):
                for s, a, z in tiles:
                    for w in two:
                        n, bank = turn()
                        for c in range(KD):
                            ins = nc.tensor.matmul(bank[0:z - a, :], short_c[s][:, c, a:z], wv[s][:, c, w * 512:(w + 1) * 512],
                                                   start=(c == 0), stop=(c == KD - 1))
                        ins.then_inc(g["filled"], 1)

            def rows(b, p):
                pe.wait_ge(g["xn"], b + 1)
                return transposes([xn[p][:, c * P:(c + 1) * P] for c in range(KD)])

            def projected(weight):
                for first_tile, end in PAIR_TILES:
                    n, bank = turn()
                    dst = bank[:, 0:(end - first_tile) * 2 * TEXT].rearrange("p (m q n) -> p m q n", q=2, n=TEXT)
                    for m in range(first_tile, end):
                        for c in range(KD):
                            ins = nc.tensor.matmul(dst[:, m - first_tile, :, :], weight[:, c, m * P:(m + 1) * P], cT[:, c, :, :],
                                                   start=(c == 0), stop=(c == KD - 1))
                    ins.then_inc(g["filled"], 1)

            def queries(n_rows):
                taken(n_rows)
                for u in two:
                    n, bank = turn()
                    for j in range(MS):
                        m = u * MS + j
                        for c in range(KD):
                            ins = nc.tensor.matmul(bank[:, j * P:(j + 1) * P], wq[:, c, m * P:(m + 1) * P], xT[:, c, :],
                                                   start=(c == 0), stop=(c == KD - 1))
                    ins.then_inc(g["filled"], 1)

            def context(i):
                pe.wait_ge(s_ctx, 32 * (i + 1))

            def values():
                for q in two:
                    for w in two:
                        n = transposes([vT[:, 4 * w + j, q, :] for j in range(4)])
                return n

            def distances(p):
                for u in two:
                    n, bank = turn()
                    for j in range(MS):
                        ins = nc.tensor.matmul(bank[:, j * 2 * NREL:(j + 1) * 2 * NREL], qT[p][:, u * MS + j, :], relk[:, :],
                                               start=True, stop=True)
                    ins.then_inc(g["filled"], 1)

            def scores(b, i, p):
                pe.wait_ge(s_kin, 32 * (i + 1))
                for h in two:
                    since(pe, g["s_sub"], 2 * (b - 1) + h + 1)
                    for j in range(MS):
                        for a in two:
                            r = slice(a * DH1, (a + 1) * DH1)
                            m = h * MS + j
                            ins = nc.tensor.matmul(S[:, h * HS + a * MS + j, :], qT[p][r, m, :], kT[r, m, p, :], start=True, stop=True)
                    ins.then_inc(g["s_mm"], 1)

            def probabilities(b, p, k):
                pe.wait_ge(g["soft"], 2 * b + k // 2 + 1)
                return transposes([soft[p][:, 4 * k + j, :] for j in range(4)])

            def weighted(b, p, k, n):
                taken(n)
                if k == 0:
                    since(pe, g["x3"], b)
                for j in range(4):
                    head = 4 * k + j
                    m, a = head // 2, head % 2
                    ins = nc.tensor.matmul(O[m // MS][a * DH1:(a + 1) * DH1, m % MS, :],
                                           v[p][:, head * DH1:(head + 1) * DH1], pT[k % 2][:, j, :],
                                           start=(m % MS == 0), stop=False, skip_group_check=True)
                ins.then_inc(g["pv_mm"], 1)

            def bands(b, i, p):
                pe.wait_ge(g["bandv"], b + 1)
                pe.wait_ge(s_pin[p], 16 * (i + 1))
                for h in two:
                    n = transposes([band[p][:, 2 * m:2 * m + 2, :].rearrange("p h r -> p (h r)") for m in range(h * MS, (h + 1) * MS)])
                return n

            def distance_values(n_bands):
                taken(n_bands)
                for m in range(MT1):
                    ins = nc.tensor.matmul(O[m // MS][:, m % MS, :], relv[:, :], bandT[:, m, :], start=False,
                                           stop=(m % MS == MS - 1), skip_group_check=True)
                    if m % MS == MS - 1:
                        ins.then_inc(g["o_mm"], 1)

            def output(b):
                pe.wait_ge(g["o_sb"], 2 * b + 2)
                y = O[0][:, 0:KD, :].rearrange("p k n -> p (k n)")
                for m in range(MT1):
                    ins = nc.tensor.matmul(y, attT[:, m, :], wo[:, m, :], start=(m == 0), stop=(m == MT1 - 1))
                ins.then_inc(g["y_mm"], 1)

            pe.wait_ge(s_short, 16 * len(SHORT))
            short_keys()
            for q in two:
                queries(rows(q, q))
                pe.wait_ge(s_w, W_READY)
                distances(q)
            short_values(VALUE_TILES[:2])
            pe.wait_ge(s_late, 32)
            short_values(VALUE_TILES[2:4])
            pe.wait_ge(s_sums, 2)
            nc.tensor.matmul(O[0][:, 0, 0:2], cst("ones"), wsum[:, :], start=True, stop=True).then_inc(s_total, 1)
            short_values(VALUE_TILES[4:])
            context(0)
            projected(wk[0])
            projected(wv[0])
            pe.wait_ge(l_ffn, 1)

            def steps(b, i, p, first, last):
                turns.begin(b, i, p)
                scores(b, i, p)
                if not first:
                    n_bands = bands(b - 1, i - 1 + p, 1 - p)
                if p == 0:
                    values()
                    if there(b + 2):
                        context(i + 1)
                        projected(wv[0])
                elif there(b + 2):
                    projected(wk[0])
                if there(b + 2):
                    n_rows = rows(b + 2, p)
                if not first:
                    distance_values(n_bands)
                if there(b + 2):
                    queries(n_rows)
                    distances(p)
                if not first:
                    output(b - 1)
                n = [probabilities(b, p, 0), probabilities(b, p, 1)]
                pe.wait_ge(s_vin, 64 * (i + 1))
                for k in range(4):
                    weighted(b, p, k, n[k])
                    if k < 2:
                        n.append(probabilities(b, p, k + 2))

            by_batch(steps)(pe)
            distance_values(bands(NB - 1, NPAIR - 1, 1))
            output(NB - 1)

        @block.vector
        def _(dve):
            front = Link(dve, l_front, 2)
            soft_l = [Link(dve, l, 2) for l in l_softs]
            sum_l = Link(dve, l_sum, 2)

            def pick_rows(b, i, p):
                since(dve, s_pick[p], 32 * i)
                nc.vector.tensor_copy(pick[p][:, :], shared["tile_rows"][:, bass.ds(b, 1), :].rearrange("p o k -> p (o k)"))\
                    .then_inc(g["pick"], 1)

            def rows(b, i, p):
                front.begin(b)
                dve.wait_ge(s_in[p], 16 * (i + 1))
                dve.wait_ge(s_pick[p], 32 * (i + 1))
                w = [shared["weights"][:, bass.ds(b, 1), k:k + 1].rearrange("p o k -> p (o k)") for k in range(TOPK)]
                front(nc.vector.scalar_tensor_tensor(x_in[p][:, :], picked[p][0][:, :], w[0], x_in[p][:, :], ALU.mult, ALU.add))
                since(dve, g["x2b"], b - 1)
                nc.vector.scalar_tensor_tensor(x2[p][:, :], picked[p][1][:, :], w[1], x_in[p][:, :], ALU.mult, ALU.add)\
                    .then_inc(g["x2"], 1)
                dve.wait_ge(g["x2"], b + 1)
                front(nc.vector.bn_stats(stat[p][:, :], x2[p][:, :]))
                front.end()
                nc.vector.bn_aggr(agg[p][:, :], stat[p][:, :]).then_inc(g["var"], 1)

            def rows_normal(b, p):
                dve.wait_ge(g["rstd"], b + 1)
                nc.vector.tensor_scalar(xn[p][:, :], x2[p][:, :], agg[p][:, 0:1], rstd[p][:, 1:2], ALU.subtract, ALU.mult)\
                    .then_inc(g["xn"], 1)

            def by_head(a):
                return a.rearrange("p (u m) n -> p m u n", u=2)

            def paired(a):
                return a.rearrange("p (m u) n -> p m u n", u=2)

            def less_max(b, i, p, h):
                lk = soft_l[h]
                lk.begin(b)
                hs = slice(h * HS, (h + 1) * HS)
                dve.wait_ge(s_relin[p], 16 * (i + 1))
                since(dve, s_pout[p], 16 * i)
                since(dve, g["tails"], b - 1)
                dve.wait_ge(g["s_mm"], 2 * b + h + 1)
                for s, (a, z) in enumerate(STREAMS):
                    m = top[:, s, hs].rearrange("p (m u) -> p m u", u=2)
                    if s == 0:
                        lk(nc.vector.tensor_tensor(paired(soft[p][:, hs, a:z]), by_head(S[:, hs, a:z]), paired(bias[p][:, hs, :]), ALU.add))
                        nc.vector.tensor_reduce(m, paired(soft[p][:, hs, a:z]), X, ALU.max)
                    else:
                        ins = nc.vector.tensor_reduce(m, by_head(S[:, hs, a:z]), X, ALU.max)
                lk(ins)
                for s, (a, z) in enumerate(STREAMS):
                    src = by_head(S[:, hs, a:z]) if s else paired(soft[p][:, hs, a:z])
                    m = top[:, s, hs].rearrange("p (m u) -> p m u", u=2).unsqueeze(3).to_broadcast([P, MS, 2, z - a])
                    ins = nc.vector.tensor_tensor(paired(soft[p][:, hs, a:z]), src, m, ALU.subtract)
                lk.end()
                ins.then_inc(g["s_sub"], 1)

            def shares(b, p, h):
                hs = slice(h * HS, (h + 1) * HS)
                sum_l.begin(2 * b + h)
                dve.wait_ge(g["s_exp"], 2 * b + h + 1)
                for s, (a, z) in enumerate(STREAMS):
                    ins = nc.vector.tensor_reduce(total[:, s, hs], soft[p][:, hs, a:z], X, ALU.add)
                sum_l(ins)
                since(dve, g["soft"], 2 * b + h - 1)
                sum_l(nc.vector.reciprocal(share[:, :, hs], total[:, :, hs]))
                nc.vector.tensor_tensor(share[:, :, hs], share[:, :, hs], coef[:, :, hs], ALU.mult).then_inc(g["share"], 1)
                sum_l.end()

            def ends(b, p):
                dve.wait_ge(g["tails"], b + 1)
                nc.vector.tensor_reduce(band[p][:, :, 0], near[:, :, :], X, ALU.add)
                nc.vector.tensor_reduce(band[p][:, :, NREL - 1], far[:, :, :], X, ALU.add).then_inc(g["bandv"], 1)

            def output(b, i, p):
                dve.wait_ge(g["y_mm"], b + 1)
                dve.wait_ge(g["x2b"], b + 1)
                since(dve, s_x3[p], 16 * i)
                y = O[0][:, 0:KD, :].rearrange("p k n -> p (k n)")
                nc.vector.tensor_tensor(x3[p][:, :], y, x2b[p][:, :], ALU.add).then_inc(g["x3"], 1)

            for p in two:
                pick_rows(p, 0, p)
            rows(0, 0, 0)
            pick_rows(2, 1, 0)
            rows(1, 0, 1)
            for p in two:
                rows_normal(p, p)

            dve.wait_ge(s_ffn, 32)
            for k in two:
                nc.vector.tensor_reduce(wsum[:, k:k + 1], wf[k], X, ALU.add, apply_absolute_value=True).then_inc(s_sums, 1)
            dve.wait_ge(s_setup, 1)
            nc.vector.memset(coef[:, 0, :], 1.0).then_inc(s_alpha, 1)
            for s in range(1, NS):
                nc.vector.tensor_scalar(coef[:, s, :], tanhs[:, s - 1:s].to_broadcast([P, NH]), 1.0, None, ALU.add).then_inc(s_alpha, 1)
            dve.wait_ge(s_alpha, NS)
            link = Link(dve, l_ffn, 8)
            dve.wait_ge(s_total, 1)
            link(nc.vector.tensor_scalar(wunit[:, :], O[0][:, 0, 0:2], 1.0 / W_N, FLOOR, ALU.mult, ALU.max))
            link(nc.vector.reciprocal(wscale[:, :], wunit[:, :]))
            for k in two:
                link(nc.vector.tensor_scalar(wf[k], wf[k], wscale[:, k:k + 1], ROUND, ALU.mult, ALU.add))
                link(nc.vector.tensor_scalar(wf[k], wf[k], -ROUND, -1.0, ALU.add, ALU.max))
                link(nc.vector.tensor_scalar(shared["ffn"][k], wf[k], 1.0, None, ALU.min))

            def steps(b, i, p, first, last):
                if there(b + 3):
                    pick_rows(b + 3, i + 1 + p, 1 - p)
                if there(b + 2):
                    rows(b + 2, i + 1, p)
                less_max(b, i, p, 0)
                if there(b + 2):
                    rows_normal(b + 2, p)
                less_max(b, i, p, 1)
                for h in range(2):
                    shares(b, p, h)
                if not first:
                    output(b - 1, i - 1 + p, 1 - p)
                ends(b, p)

            by_batch(steps)(dve)
            output(NB - 1, NPAIR - 1, 1)


def feed_forward(nc, t, shared, out):
    with ExitStack() as ctx:
        def sb(name, shape, dt=F32):
            return ctx.enter_context(nc.sbuf_tensor(name, shape, dt))

        def ps(name, shape, dt=F32):
            return ctx.enter_context(nc.psum_tensor(name, shape, dt))

        def sem(name):
            shared["semaphores"].append(nc.alloc_semaphore(name=name))
            return shared["semaphores"][-1]

        const = shared["const"]

        def cst(name):
            a, z = CONST_AT[name]
            return const[:, a:z]

        ident, ones = cst("ident"), cst("ones")
        two = range(2)
        wunit, tap = shared["ffn_unit"], shared["tap"]
        w1, w2 = (w.rearrange("p (k n) -> p k n", k=k) for w, k in zip(shared["ffn"], (KD, MH)))
        ident_b = sb("d_ident", [P, P], BF16)
        cbias = sb("d_cbias", [P, MH])
        x_in = [sb(f"d_x{p}", [P, D]) for p in two]
        x_res = [sb(f"d_xr{p}", [P, D]) for p in two]
        stat = sb("d_stat", [P, 6])
        agg = sb("d_agg", [P, 2])
        rstd = sb("d_rstd", [P, 2])
        xn = sb("d_xn", [P, D])
        peak = sb("d_peak", [P, 4])
        unit = sb("d_unit", [P, 2])
        rnd = sb("d_rnd", [P, D])
        xi = [sb(f"d_xi{p}", [P, D], BF16) for p in two]
        diag1 = [sb(f"d_diag1{p}", [P, P]) for p in two]
        diag2 = sb("d_diag2", [P, P])
        xiT = sb("d_xiT", [P, KD, P], BF16)
        row1 = sb("d_row1", [P, P])
        row2 = sb("d_row2", [P, P])
        hp = [sb(f"d_hp{p}", [P, MH, P + 2]) for p in two]
        act_h = [sb(f"d_act{p}", [P, MH, P]) for p in two]
        gi = sb("d_gi", [P, MH, P], BF16)
        step = [sb(f"d_step{p}", [P, 1]) for p in two]
        res = [sb(f"d_res{p}", [P, D]) for p in two]
        XT = ps("d_XT", [P, 8 * P], BF16)
        H = ps("d_H", [P, MH, P])
        CV = ps("d_CV", [P, MH, P])
        GT = ps("d_GT", [P, HID])
        YR = ps("d_YR", [P, 512])
        Y, R2, R1 = YR[:, 0:D], YR[:, D:D + P], YR[:, D + P:D + 2 * P]

        s_w = sem("d_weights")
        s_pad = sem("d_pad")
        s_id = sem("d_id")
        l_front, l_q, l_pool = (sem("dl_" + n) for n in "front quant pool".split())
        s_in = [sem(f"d_in{p}") for p in two]
        s_res = [sem(f"d_res{p}") for p in two]
        s_out = [sem(f"d_out{p}") for p in two]
        names = ("var rstd xi xt_mm xt_sb row1_mm row1_sb h_mm h cv_mm silu gt_mm peak2 diag2 row2_mm row2_sb scaled gi y_mm y")
        g = {n: sem("d_" + n) for n in names.split()}


        def by_batch(steps):
            def run(eng):
                for b in range(-2, 4):
                    steps(b, b // 2, b % 2)
                with eng.Fori(2, NB // 2 - 2) as i:
                    for p in range(2):
                        steps(i * 2 + p, i, p)
                for b in range(NB - 4, NB + 1):
                    steps(b, b // 2, b % 2)
            return run

        def there(b):
            return not isinstance(b, int) or 0 <= b < NB

        def rows_of(d, b):
            return d[bass.ds(b, 1)].rearrange("o p d -> (o p) d")

        block = ctx.enter_context(nc.Block())

        @block.sync
        def _(sp):
            def load(b, p):
                since(sp, g["xi"], b - 1)
                sp.dma_start(x_in[p][:, :], rows_of(t["x3"], b)).then_inc(s_in[p], 16)

            def load_residual(b, p):
                since(sp, g["y"], b - 1)
                sp.dma_start(x_res[p][:, :], rows_of(t["x3"], b)).then_inc(s_res[p], 16)

            def store(b, p):
                sp.wait_ge(g["y"], b + 1)
                sp.dma_start(rows_of(out, b), res[p][:, :]).then_inc(s_out[p], 16)

            load(0, 0)
            load(1, 1)
            sp.dma_start(cbias[:, :], t["L1_conv_b"]).then_inc(s_w, 16)

            def steps(b, i, p):
                if there(b + 4):
                    load(b + 4, p)
                if there(b):
                    load_residual(b, p)
                if there(b - 1):
                    store(b - 1, 1 - p)

            by_batch(steps)(sp)
            for p in two:
                sp.wait_ge(s_out[p], 16 * (NB // 2))

        @block.gpsimd
        def _(pool):
            lk = Link(pool, l_pool, 1)

            def inverse_std(b):
                apart(pool, g["var"], b + 1)
                lk.begin(b)
                lk(nc.gpsimd.tensor_scalar(rstd[:, 0:1], agg[:, 1:2], EPS, None, ALU.add))
                nc.gpsimd.tensor_tensor(rstd[:, 1:2], rstd[:, 0:1], shared["mhalf"][:, :], ALU.pow).then_inc(g["rstd"], 1)

            def scale(b, p):
                pool.wait_ge(g["row2_sb"], b + 1)
                nc.gpsimd.tensor_tensor(act_h[p][:, :, :], act_h[p][:, :, :], row2[:, :].unsqueeze(1).to_broadcast([P, MH, P]), ALU.mult)\
                    .then_inc(g["scaled"], 1)

            nc.gpsimd.tensor_copy(ident_b[:, :], ident).then_inc(s_id, 1)
            inverse_std(0)
            for p in two:
                nc.gpsimd.memset(hp[p][:, :, 0:1], 0.0).then_inc(s_pad, 1)
                nc.gpsimd.memset(hp[p][:, :, P + 1:P + 2], 0.0).then_inc(s_pad, 1)
            def steps(b, i, p):
                if there(b + 3):
                    inverse_std(b + 3)
                if there(b):
                    scale(b, p)

            by_batch(steps)(pool)

        @block.scalar
        def _(act):
            act.wait_ge(s_w, 16)

            def rows_sb(b):
                act.wait_ge(g["xt_mm"], b + 1)
                since(act, g["h_mm"], b)
                nc.scalar.activation(xiT[:, :, :], XT[:, 0:D].rearrange("p (k n) -> p k n", k=KD), ACT.Copy).then_inc(g["xt_sb"], 1)

            def steps_sb(b):
                act.wait_ge(g["row1_mm"], b + 1)
                since(act, g["h"], b)
                nc.scalar.activation(row1[:, :], R1, ACT.Copy).then_inc(g["row1_sb"], 1)

            def activate(b, p, half):
                act.wait_ge(g["cv_mm"], 2 * b + half + 1)
                since(act, g["gi"], b - 1)
                for m in range(half * MH // 2, (half + 1) * MH // 2):
                    ins = nc.scalar.activation(act_h[p][:, m, :], CV[:, m, :], ACT.Silu, bias=cbias[:, m:m + 1])
                ins.then_inc(g["silu"], 1)

            def scales_sb(b):
                act.wait_ge(g["row2_mm"], b + 1)
                since(act, g["scaled"], b)
                nc.scalar.activation(row2[:, :], R2, ACT.Copy).then_inc(g["row2_sb"], 1)

            def steps(b, i, p):
                if there(b + 2):
                    rows_sb(b + 2)
                if there(b):
                    scales_sb(b)
                if there(b + 1):
                    for half in two:
                        activate(b + 1, 1 - p, half)
                if there(b + 2):
                    steps_sb(b + 2)

            by_batch(steps)(act)

        @block.tensor
        def _(pe):
            pe.wait_ge(s_id, 1)

            def transposes(b, p):
                pe.wait_ge(g["xi"], b + 1)
                since(pe, g["xt_sb"], b)
                for c in range(KD):
                    ins = nc.tensor.transpose(XT[:, c * P:(c + 1) * P], xi[p][:, c * P:(c + 1) * P], ident_b[:, :])
                ins.then_inc(g["xt_mm"], 1)

            def hidden(b, p):
                since(pe, g["y"], b - 2)
                since(pe, g["row2_sb"], b - 1)
                nc.tensor.matmul(R1, ones, diag1[p][:, :], start=True, stop=True).then_inc(g["row1_mm"], 1)
                pe.wait_ge(g["xt_sb"], b + 1)
                since(pe, g["h"], b)
                for m in range(MH):
                    for c in range(KD):
                        ins = nc.tensor.matmul(H[:, m, :], w1[:, c, m * P:(m + 1) * P], xiT[:, c, :], start=(c == 0), stop=(c == KD - 1))
                ins.then_inc(g["h_mm"], 1)

            def convolve(b, p, half):
                pe.wait_ge(g["h"], b + 1)
                since(pe, g["silu"], 2 * (b - 1) + half + 1)
                for m in range(half * MH // 2, (half + 1) * MH // 2):
                    for k in range(3):
                        ins = nc.tensor.matmul(CV[:, m, :], tap[:, m, k, :], hp[p][:, m, k:k + P], start=(k == 0), stop=(k == 2))
                ins.then_inc(g["cv_mm"], 1)

            def activated(b, p):
                pe.wait_ge(g["silu"], 2 * b + 2)
                since(pe, g["peak2"], b)
                for m in range(MH):
                    ins = nc.tensor.transpose(GT[:, m * P:(m + 1) * P], act_h[p][:, m, :], ident)
                ins.then_inc(g["gt_mm"], 1)

            def scales(b):
                pe.wait_ge(g["diag2"], b + 1)
                since(pe, g["y"], b)
                if there(b + 1):
                    pe.wait_ge(g["row1_sb"], b + 2)
                nc.tensor.matmul(R2, ones, diag2[:, :], start=True, stop=True).then_inc(g["row2_mm"], 1)

            def output(b):
                pe.wait_ge(g["gi"], b + 1)
                since(pe, g["y"], b)
                if there(b + 2):
                    pe.wait_ge(g["row1_sb"], b + 3)
                for m in range(MH):
                    ins = nc.tensor.matmul(Y, gi[:, m, :], w2[:, m, :], start=(m == 0), stop=(m == MH - 1))
                ins.then_inc(g["y_mm"], 1)

            def steps(b, i, p):
                if there(b):
                    activated(b, p)
                if there(b - 1):
                    output(b - 1)
                if there(b + 1):
                    convolve(b + 1, 1 - p, 0)
                if there(b + 2):
                    transposes(b + 2, p)
                if there(b):
                    scales(b)
                if there(b + 1):
                    convolve(b + 1, 1 - p, 1)
                if there(b + 2):
                    hidden(b + 2, p)

            by_batch(steps)(pe)

        @block.vector
        def _(dve):
            front_l, quant_l = Link(dve, l_front, 7), Link(dve, l_q, 4)

            def stats(b, i, p):
                front_l.begin(b)
                dve.wait_ge(s_in[p], 16 * (i + 1))
                return front_l.add(nc.vector.bn_stats(stat[:, :], x_in[p][:, :]))

            def variance(done):
                front_l.wait(done)
                nc.vector.bn_aggr(agg[:, :], stat[:, :]).then_inc(g["var"], 1)

            def whole_rows(b, p):
                dve.wait_ge(g["rstd"], b + 1)
                front_l(nc.vector.tensor_scalar(xn[:, :], x_in[p][:, :], agg[:, 0:1], rstd[:, 1:2], ALU.subtract, ALU.mult))
                front_l(nc.vector.tensor_reduce(peak[:, 0:1], xn[:, :], X, ALU.max, apply_absolute_value=True))
                front_l(nc.vector.tensor_scalar(unit[:, 0:1], peak[:, 0:1], FLOOR, 1.0 / LEVELS, ALU.max, ALU.mult))
                front_l(nc.vector.reciprocal(peak[:, 1:2], unit[:, 0:1]))
                front_l(nc.vector.tensor_scalar(rnd[:, :], xn[:, :], peak[:, 1:2], LEVELS, ALU.mult, ALU.min))
                front_l(nc.vector.tensor_scalar(rnd[:, :], rnd[:, :], -LEVELS - 1.0, ROUND, ALU.max, ALU.add))
                front_l.end()
                since(dve, g["xt_mm"], b - 1)
                nc.vector.tensor_scalar(xi[p][:, :], rnd[:, :], -ROUND, None, ALU.add)
                since(dve, g["row1_mm"], b - 1)
                nc.vector.tensor_scalar(diag1[p][:, :], ident, unit[:, 0:1], wunit[:, 0:1], ALU.mult, ALU.mult).then_inc(g["xi"], 1)

            def hidden(b, p):
                dve.wait_ge(g["h_mm"], b + 1)
                dve.wait_ge(g["row1_sb"], b + 1)
                since(dve, g["cv_mm"], 2 * (b - 1))
                nc.vector.tensor_tensor(hp[p][:, :, 1:P + 1], H[:, :, :], row1[:, :].unsqueeze(1).to_broadcast([P, MH, P]), ALU.mult)\
                    .then_inc(g["h"], 1)

            def peaks(b):
                dve.wait_ge(g["gt_mm"], b + 1)
                nc.vector.tensor_reduce(peak[:, 2:3], GT[:, :], X, ALU.max, apply_absolute_value=True).then_inc(g["peak2"], 1)

            def scales(b, p):
                quant_l.begin(b)
                dve.wait_ge(g["peak2"], b + 1)
                quant_l(nc.vector.tensor_scalar(unit[:, 1:2], peak[:, 2:3], FLOOR, 1.0 / LEVELS, ALU.max, ALU.mult))
                quant_l(nc.vector.reciprocal(peak[:, 3:4], unit[:, 1:2]))
                since(dve, g["row2_mm"], b)
                nc.vector.tensor_scalar(diag2[:, :], ident, peak[:, 3:4], None, ALU.mult).then_inc(g["diag2"], 1)
                quant_l.add(nc.vector.tensor_scalar(step[p][:, :], unit[:, 1:2], wunit[:, 1:2], None, ALU.mult))

            def whole_columns(b, p):
                dve.wait_ge(g["scaled"], b + 1)
                quant_l(nc.vector.tensor_scalar(act_h[p][:, :, :], act_h[p][:, :, :], LEVELS, -LEVELS - 1.0, ALU.min, ALU.max))
                quant_l.end()
                since(dve, g["y_mm"], b)
                nc.vector.tensor_scalar(gi[:, :, :], act_h[p][:, :, :], ROUND, -ROUND, ALU.add, ALU.add).then_inc(g["gi"], 1)

            def output(b, i, p):
                dve.wait_ge(g["y_mm"], b + 1)
                dve.wait_ge(s_res[p], 16 * (i + 1))
                since(dve, s_out[p], 16 * i)
                nc.vector.scalar_tensor_tensor(res[p][:, :], Y, step[p][:, 0:1], x_res[p][:, :], ALU.mult, ALU.add)\
                    .then_inc(g["y"], 1)

            variance(stats(0, 0, 0))
            whole_rows(0, 0)
            dve.wait_ge(s_pad, 4)

            def steps(b, i, p):
                if there(b + 3):
                    done = stats(b + 3, i + 1 + p, 1 - p)
                if there(b):
                    peaks(b)
                if there(b + 3):
                    variance(done)
                if there(b):
                    scales(b, p)
                if there(b - 1):
                    output(b - 1, i - 1 + p, 1 - p)
                if there(b + 3):
                    whole_rows(b + 3, 1 - p)
                if there(b):
                    whole_columns(b, p)
                if there(b + 2):
                    hidden(b + 2, p)

            by_batch(steps)(dve)


def layer1(nc, t, shared, out):
    attention1(nc, t, shared)
    feed_forward(nc, t, shared, out)


def release_semaphores(nc, shared):
    nc.clear_and_free_semaphores(shared["semaphores"])
    nc.all_engine_barrier()
    shared["semaphores"] = []


def build(nc, t, out, phases="ABC"):
    with ExitStack() as ctx:
        def sb(name, shape, dt=F32):
            return ctx.enter_context(nc.sbuf_tensor(name, shape, dt))

        shared = {
            "const": sb("const", [P, CONST_W]),
            "mhalf": sb("mhalf", [P, 1]),
            "onehot": sb("onehot", [P, NB, TOPK, NE]),
            "escore": sb("escore", [P, NB, NE]),
            "shift": sb("shift", [P, NE]),
            "slots": sb("slots", [P, NB, TOPK]),
            "weights": sb("weights", [P, NB, TOPK]),
            "tile_rows": sb("tile_rows", [P, NB, TOPK], I32),
            "tile_expert": sb("tile_expert", [P, N_TILES], I32),
            "tile_row": sb("tile_row", [P, N_TILES], I32),
            "semaphores": [],
            "s_experts": ctx.enter_context(nc.semaphore("s_experts")),
            "s_layer1": ctx.enter_context(nc.semaphore("s_layer1")),
            "early": sb("early", [P, len(L1_EARLY) * KD * INNER + NE * D]),
        }
        size = KD * INNER
        shared["layer1"] = weights = {}
        for n, name in enumerate(L1_EARLY):
            weights[name] = shared["early"][:, n * size:(n + 1) * size].rearrange("p (k n) -> p k n", n=INNER)

        def load_layer1(eng, part):
            for name, dst in list(weights.items())[part]:
                eng.dma_start(dst, t["L1_" + name].rearrange("(k p) n -> p k n", p=P)).then_inc(shared["s_layer1"], 16)

        shared["load_layer1"] = load_layer1
        shared["b2"] = shared["early"][:, len(L1_EARLY) * size:].rearrange("p (e d) -> p e d", e=NE)
        t["lists"] = nc.dram_tensor("expert_lists", (NE * ROWS_E, D), F32, kind="Internal").ap()
        t["expert_out"] = nc.dram_tensor("expert_out", (N_TILES * P, D), F32, kind="Internal").ap()
        t["x1"] = nc.dram_tensor("rows_after_attention", (NB, P, D), F32, kind="Internal").ap()
        t["x3"] = nc.dram_tensor("rows_after_attention_1", (NB, P, D), F32, kind="Internal").ap()
        t["prob_rows"] = [nc.dram_tensor(f"prob_rows{p}", (P, NH, BANDW), F32, kind="Internal").ap() for p in range(2)]
        with ExitStack() as moe:
            for name, shape in (("w1", [P, NE, KD, 2 * HE]), ("w2", [P, NE, KH, D]), ("b1", [P, NE, 2 * HE])):
                shared[name] = moe.enter_context(nc.sbuf_tensor("moe_" + name, shape, F32))

            def load_experts(eng, e, half):
                s = shared["s_experts"]

                def one(a):
                    return a[bass.ds(e, 1)]

                rows = slice(half * P, (half + 1) * P)
                eng.dma_start(shared["w1"][:, bass.ds(e, 1), half, :], one(t["L0_Wl1"])[:, rows].rearrange("e p n -> p e n")).then_inc(s, 16)
                ks = slice(half * KH // 2, (half + 1) * KH // 2)
                eng.dma_start(shared["w2"][:, bass.ds(e, 1), ks, :].rearrange("p o k n -> p (o k) n"),
                              one(t["L0_Wl2"])[:, half * HE // 2:(half + 1) * HE // 2].rearrange("e (k p) n -> p (e k) n", p=P)).then_inc(s, 16)
                if half == 0:
                    eng.dma_start(shared["b1"][:, bass.ds(e, 1), :], one(t["L0_bl1"]).partition_broadcast(P)).then_inc(s, 16)

            shared["experts_ready"] = 16 * 5 * NE
            shared["load_experts"] = load_experts
            layer0(nc, t, shared)
            release_semaphores(nc, shared)
            experts(nc, t, shared)
        shared["ffn"] = [sb(f"ffn_w{k}", [P, W_N // P], BF16)[:, :] for k in range(2)]
        shared["tap"] = sb("ffn_tap", [P, MH, 3, P])
        shared["ffn_unit"] = sb("ffn_unit", [P, 2])
        layer1(nc, t, shared, out)


def strip_columns(w):
    a = np.zeros((w.shape[1], NH, STRIP), w.dtype)
    a[:, :, :DH0] = w.T.reshape(w.shape[1], NH, DH0)
    return a.reshape(w.shape[1], NH * STRIP)


def strip_bias(b, mask_row):
    a = np.zeros((NH, STRIP), b.dtype)
    a[:, :DH0] = b.reshape(NH, DH0)
    a[:, DH0] = mask_row
    return np.ascontiguousarray(a.reshape(MT0, P).T)


def pair_blocks(a):
    r, c = a.shape
    z = np.zeros((2 * r, 2 * c), a.dtype)
    z[:r, :c] = a
    z[r:, c:] = a
    return z


def transposed_context(a):
    a = a.reshape(-1, KD, P).transpose(2, 1, 0)
    return a.reshape(P, -1)


def layout1(L1_xattn_Wq, L1_xattn_Wk, L1_xattn_Wv, L1_xattn_Wk_ip, L1_xattn_Wv_ip, L1_xattn_Wk_ap, L1_xattn_Wv_ap, L1_xattn_Wo,
            L1_xattn_bo, L1_xattn_rel_k, L1_xattn_rel_v, L1_xattn_alpha, L1_xattn_beta, L1_ffn_w1, L1_ffn_conv_w, L1_ffn_conv_b,
            L1_ffn_w2):
    return {
        "L1_Wq": L1_xattn_Wq, "L1_Wk0": L1_xattn_Wk, "L1_Wk1": L1_xattn_Wk_ip, "L1_Wk2": L1_xattn_Wk_ap,
        "L1_Wv0": L1_xattn_Wv, "L1_Wv1": L1_xattn_Wv_ip, "L1_Wv2": L1_xattn_Wv_ap, "L1_Wo": L1_xattn_Wo, "L1_bo": L1_xattn_bo,
        "L1_relk": pair_blocks(L1_xattn_rel_k.T), "L1_relv": pair_blocks(L1_xattn_rel_v),
        "L1_alphas": np.stack([L1_xattn_alpha, L1_xattn_beta]),
        "L1_w1T": L1_ffn_w1.T, "L1_w2T": L1_ffn_w2.T, "L1_conv_w": L1_ffn_conv_w.reshape(HID, 3),
        "L1_conv_b": L1_ffn_conv_b.reshape(MH, P).T,
    }


def layout(x, ctx_1024, mask_Bx1x1xS2_ik0, L0_xattn_Wq, L0_xattn_bq, L0_xattn_Wk, L0_xattn_bk, L0_xattn_Wv, L0_xattn_bv,
           L0_xattn_gamma, L0_xattn_beta, L0_ffn_Wr, L0_ffn_br, L0_ffn_Wl1, L0_ffn_bl1, L0_ffn_Wl2, L0_ffn_bl2,
           L0_ffn_biases_N, **layer1_inputs):
    c = np.ascontiguousarray
    arrays = {
        "x": x, "ctx": ctx_1024, "mask": mask_Bx1x1xS2_ik0.reshape(NB, P),
        "L0_wqT": strip_columns(L0_xattn_Wq), "L0_wkT": strip_columns(L0_xattn_Wk), "L0_wvT": c(L0_xattn_Wv.T),
        "L0_wrT": c(L0_ffn_Wr.T),
        "L0_bq": strip_bias(L0_xattn_bq, 1.0 / SCALE0), "L0_bk": strip_bias(L0_xattn_bk, MASKED), "L0_bv": L0_xattn_bv,
        "L0_gamma": L0_xattn_gamma, "L0_beta": L0_xattn_beta, "L0_br": L0_ffn_br, "L0_pick_bias": L0_ffn_biases_N,
        "L0_Wl1": L0_ffn_Wl1, "L0_bl1": L0_ffn_bl1, "L0_Wl2": L0_ffn_Wl2, "L0_bl2": L0_ffn_bl2,
        "ctxT": np.stack([transposed_context(a) for a in ctx_1024]),
        **{f"short_ctxT{s}": transposed_context(ctx_1024[:, a:z]) for s, (a, z) in enumerate(STREAMS) if s},
        "const": np.concatenate(list(CONST.values()), axis=1),
    }
    arrays.update(layout1(**layer1_inputs))
    return {n: c(a) for n, a in arrays.items()}


def kernel(**inputs):
    import concourse.bacc as bacc
    from concourse.bass_utils import run_bass_kernel_spmd

    nc = bacc.Bacc("TRN2", target_bir_lowering=False, num_devices=1)
    arrays = layout(**{n: np.asarray(a) for n, a in inputs.items()})
    t = {n: nc.dram_tensor("in_" + n, a.shape, mybir.dt.from_np(a.dtype), kind="ExternalInput").ap() for n, a in arrays.items()}
    out = nc.dram_tensor("out", (NB, P, D), F32, kind="ExternalOutput").ap()
    build(nc, t, out)
    result = run_bass_kernel_spmd(nc, [{"in_" + n: a for n, a in arrays.items()}], core_ids=[0])
    return result.results[0]["out"]
```
